# Optimizing a Trainium2 kernel written in Bass

```python
import numpy as np
import jax
import jax.numpy as jnp

def _softmax(x, axis=-1):
    return jax.nn.softmax(x, axis=axis)

def _gelu(x):
    return jax.nn.gelu(x, approximate=True)

def _silu(x):
    return jax.nn.silu(x)

def _sigmoid(x):
    return jax.nn.sigmoid(x)

def _layernorm(x, axis=-1, eps=1e-05):
    m = jnp.mean(x, axis=axis, keepdims=True)
    v = jnp.var(x, axis=axis, keepdims=True)
    return (x - m) / jnp.sqrt(v + eps)

def _scatter_add(tgt, idx, src, axis=0):
    return tgt.at[idx].add(src)

def _segment_sum(src, seg, n):
    return jax.ops.segment_sum(src, seg, n)
kernel_name = 'mk_adaln_d2_jaxref_r4_f5d11f'

def setup_inputs(seed: int=0):
    np.random.seed(seed)
    _w = jnp.asarray

    def _L0_attn_setup():
        import jax, jax.numpy as jnp
        import numpy as np
        import math
        D_MODEL = 256
        N_HEADS = 16
        HEAD_DIM = D_MODEL // N_HEADS
        FEAT = 16
        WINDOW = 64
        EPS_NORM = 1e-06
        EPS_LIN = 1e-06
        CHUNK = 128

        def rmsnorm(x, w):
            return x * jax.lax.rsqrt(jnp.mean(x * x, axis=-1, keepdims=True) + EPS_NORM) * w

        def taylor_feature_map(x):
            d = x.shape[-1]
            iu, ju = jnp.triu_indices(d)
            scale = jnp.where(iu == ju, 0.5, 1.0 / math.sqrt(2.0)).astype(x.dtype)
            quad = x[..., iu] * x[..., ju] * scale
            ones = jnp.ones(x.shape[:-1] + (1,), dtype=x.dtype)
            return jnp.concatenate([ones, x, quad], axis=-1)

        def linear_attention_causal(q_phi, k_phi, v):
            B, T, H, F = q_phi.shape
            D = v.shape[-1]
            Nc = T // CHUNK
            qc = q_phi.reshape(B, Nc, CHUNK, H, F).transpose(1, 0, 2, 3, 4)
            kc = k_phi.reshape(B, Nc, CHUNK, H, F).transpose(1, 0, 2, 3, 4)
            vc = v.reshape(B, Nc, CHUNK, H, D).transpose(1, 0, 2, 3, 4)
            causal = jnp.tril(jnp.ones((CHUNK, CHUNK), dtype=q_phi.dtype))

            def step(carry, inp):
                kv, ksum = carry
                qb, kb, vb = inp
                A = jnp.einsum('bchf,bshf->bhcs', qb, kb) * causal
                y = jnp.einsum('bhcs,bshd->bchd', A, vb) + jnp.einsum('bchf,bhfd->bchd', qb, kv)
                z = jnp.einsum('bhcs->bch', A) + jnp.einsum('bchf,bhf->bch', qb, ksum)
                kv = kv + jnp.einsum('bshf,bshd->bhfd', kb, vb)
                ksum = ksum + kb.sum(axis=1)
                return ((kv, ksum), y / (z[..., None] + EPS_LIN))
            kv0 = jnp.zeros((B, H, F, D), dtype=q_phi.dtype)
            ks0 = jnp.zeros((B, H, F), dtype=q_phi.dtype)
            _, ys = jax.lax.scan(step, (kv0, ks0), (qc, kc, vc))
            return ys.transpose(1, 0, 2, 3, 4).reshape(B, T, H, D)

        def sliding_window_attention(q, k, v):
            B, T, H, D = q.shape
            scale = 1.0 / math.sqrt(D)
            t = jnp.arange(T)
            allowed = (t[None, :] <= t[:, None]) & (t[None, :] >= t[:, None] - WINDOW)
            scores = jnp.einsum('bqhd,bkhd->bhqk', q, k) * scale
            scores = jnp.where(allowed[None, None], scores, -jnp.inf)
            attn = jax.nn.softmax(scores, axis=-1)
            out = jnp.einsum('bhqk,bkhd->bqhd', attn, v)
            return out.reshape(B, T, H * D)
        key = jax.random.key(seed)
        ks = jax.random.split(key, 7)
        B, T = (2, 512)
        s = 0.02
        return {'x': jax.random.normal(ks[0], (B, T, D_MODEL), jnp.float32), 'norm_w': jnp.ones((D_MODEL,), jnp.float32), 'Wq': jax.random.normal(ks[1], (D_MODEL, D_MODEL), jnp.float32) * s, 'Wk': jax.random.normal(ks[2], (D_MODEL, D_MODEL), jnp.float32) * s, 'Wv': jax.random.normal(ks[3], (D_MODEL, D_MODEL), jnp.float32) * s, 'Wqf': jax.random.normal(ks[4], (HEAD_DIM, FEAT), jnp.float32) * s, 'Wkf': jax.random.normal(ks[5], (HEAD_DIM, FEAT), jnp.float32) * s, 'Wout': jax.random.normal(ks[6], (2 * D_MODEL, D_MODEL), jnp.float32) * s}
    _L0_attn_in = _L0_attn_setup()

    def _L0_ffn_setup():
        import jax, jax.numpy as jnp
        import numpy as np
        DIM = 256

        def _reference_tuple_inner(x, W_r, W_k, W_v, mu_r, mu_k):
            B, T, C = x.shape
            x_prev = jnp.concatenate([jnp.zeros((B, 1, C), x.dtype), x[:, :-1, :]], axis=1)
            xr = mu_r * x + (1.0 - mu_r) * x_prev
            xk = mu_k * x + (1.0 - mu_k) * x_prev
            r = jax.nn.sigmoid(jnp.einsum('btc,dc->btd', xr, W_r))
            k = jnp.einsum('btc,dc->btd', xk, W_k)
            k_act = jnp.square(jax.nn.relu(k))
            out = r * jnp.einsum('btc,dc->btd', k_act, W_v)
            new_state = x[:, -1, :]
            return (out, new_state)
        key = jax.random.key(seed)
        ks = jax.random.split(key, 6)
        B, T, C = (8, 512, DIM)
        x = jax.random.normal(ks[0], (B, T, C), dtype=jnp.float32)
        s = 1.0 / np.sqrt(C)
        W_r = jax.random.uniform(ks[1], (C, C), jnp.float32, -s, s)
        W_k = jax.random.uniform(ks[2], (C, C), jnp.float32, -s, s)
        W_v = jax.random.uniform(ks[3], (C, C), jnp.float32, -s, s)
        mu_r = jax.random.uniform(ks[4], (C,), jnp.float32)
        mu_k = jax.random.uniform(ks[5], (C,), jnp.float32)
        return {'x': x, 'W_r': W_r, 'W_k': W_k, 'W_v': W_v, 'mu_r': mu_r, 'mu_k': mu_k}
    _L0_ffn_in = _L0_ffn_setup()
    _L0_c = _w((lambda *s: np.random.randn(*s).astype(np.float32) * 0.05)(8, 256))
    _L0_wmod = _w((lambda *s: np.random.randn(*s).astype(np.float32) * 0.05)(256, 6 * 256) * 256 ** (-0.5))

    def _L1_attn_setup():
        import jax, jax.numpy as jnp
        import numpy as np
        MAX_WAVELENGTH = 10000.0
        NEG_INF = -1000000000.0

        def apply_rope(x):
            S, D = (x.shape[1], x.shape[-1])
            inv_freq = 1.0 / MAX_WAVELENGTH ** (jnp.arange(0, D, 2, dtype=jnp.float32) / D)
            t = jnp.arange(S, dtype=jnp.float32)[:, None] * inv_freq[None, :]
            emb = jnp.concatenate([t, t], axis=-1)
            cos = jnp.cos(emb)[None, :, None, :].astype(x.dtype)
            sin = jnp.sin(emb)[None, :, None, :].astype(x.dtype)
            x1, x2 = jnp.split(x, 2, axis=-1)
            rotated = jnp.concatenate([-x2, x1], axis=-1)
            return x * cos + rotated * sin
        key = jax.random.key(seed)
        k1, k2, k3 = jax.random.split(key, 3)
        B, S, dim = (2, 512, 256)
        x = jax.random.normal(k1, (B, S, dim), dtype=jnp.float32)
        w_qkv = jax.random.normal(k2, (dim, 3 * dim), dtype=jnp.float32) * dim ** (-0.5)
        w_proj = jax.random.normal(k3, (dim, dim), dtype=jnp.float32) * dim ** (-0.5)
        b_proj = jnp.zeros((dim,), dtype=jnp.float32)
        return {'x': x, 'w_qkv': w_qkv, 'w_proj': w_proj, 'b_proj': b_proj}
    _L1_attn_in = _L1_attn_setup()

    def _L1_ffn_setup():
        import jax, jax.numpy as jnp
        import numpy as np
        D_IN, D_HID = (256, 1024)

        def _ternary(key, shape):
            return jax.random.randint(key, shape, -1, 2).astype(jnp.float32)

        def _tlin(x, w, s):
            return jnp.einsum('bsi,oi->bso', x, w) * s
        key = jax.random.key(seed)
        ks = jax.random.split(key, 12)
        inv = lambda fan: 1.0 / np.sqrt(fan).astype(np.float32)
        return {'x': jax.random.normal(ks[0], (4, 512, D_IN), dtype=jnp.float32), 'w1_w': _ternary(ks[1], (D_HID, D_IN)), 'w1_s': jax.random.uniform(ks[2], (D_HID,), dtype=jnp.float32) * inv(D_IN), 'w2_w': _ternary(ks[3], (D_HID, D_IN)), 'w2_s': jax.random.uniform(ks[4], (D_HID,), dtype=jnp.float32) * inv(D_IN), 'h1_w': _ternary(ks[5], (D_HID, D_HID)), 'h1_s': jax.random.uniform(ks[6], (D_HID,), dtype=jnp.float32) * inv(D_HID), 'h2_w': _ternary(ks[7], (D_HID, D_HID)), 'h2_s': jax.random.uniform(ks[8], (D_HID,), dtype=jnp.float32) * inv(D_HID), 'w3_w': _ternary(ks[9], (D_IN, D_HID)), 'w3_s': jax.random.uniform(ks[10], (D_IN,), dtype=jnp.float32) * inv(D_HID)}
    _L1_ffn_in = _L1_ffn_setup()
    _L1_c = _w((lambda *s: np.random.randn(*s).astype(np.float32) * 0.05)(8, 256))
    _L1_wmod = _w((lambda *s: np.random.randn(*s).astype(np.float32) * 0.05)(256, 6 * 256) * 256 ** (-0.5))
    _d = {'L0_attn_x': _L0_attn_in['x'], 'L0_attn_norm_w': _L0_attn_in['norm_w'], 'L0_attn_Wq': _L0_attn_in['Wq'], 'L0_attn_Wk': _L0_attn_in['Wk'], 'L0_attn_Wv': _L0_attn_in['Wv'], 'L0_attn_Wqf': _L0_attn_in['Wqf'], 'L0_attn_Wkf': _L0_attn_in['Wkf'], 'L0_attn_Wout': _L0_attn_in['Wout'], 'L0_ffn_W_r': _L0_ffn_in['W_r'], 'L0_ffn_W_k': _L0_ffn_in['W_k'], 'L0_ffn_W_v': _L0_ffn_in['W_v'], 'L0_ffn_mu_r': _L0_ffn_in['mu_r'], 'L0_ffn_mu_k': _L0_ffn_in['mu_k'], 'L0_c': _L0_c, 'L0_wmod': _L0_wmod, 'L1_attn_w_qkv': _L1_attn_in['w_qkv'], 'L1_attn_w_proj': _L1_attn_in['w_proj'], 'L1_attn_b_proj': _L1_attn_in['b_proj'], 'L1_ffn_w1_w': _L1_ffn_in['w1_w'], 'L1_ffn_w1_s': _L1_ffn_in['w1_s'], 'L1_ffn_w2_w': _L1_ffn_in['w2_w'], 'L1_ffn_w2_s': _L1_ffn_in['w2_s'], 'L1_ffn_h1_w': _L1_ffn_in['h1_w'], 'L1_ffn_h1_s': _L1_ffn_in['h1_s'], 'L1_ffn_h2_w': _L1_ffn_in['h2_w'], 'L1_ffn_h2_s': _L1_ffn_in['h2_s'], 'L1_ffn_w3_w': _L1_ffn_in['w3_w'], 'L1_ffn_w3_s': _L1_ffn_in['w3_s'], 'L1_c': _L1_c, 'L1_wmod': _L1_wmod}
    _x0 = _d['L0_attn_x']
    _d['L0_attn_x'] = jax.random.normal(jax.random.fold_in(jax.random.key(seed), 1), (8, 512, 256), dtype=_x0.dtype)
    del _x0
    return _d

def reference(L0_attn_x, L0_attn_norm_w, L0_attn_Wq, L0_attn_Wk, L0_attn_Wv, L0_attn_Wqf, L0_attn_Wkf, L0_attn_Wout, L0_ffn_W_r, L0_ffn_W_k, L0_ffn_W_v, L0_ffn_mu_r, L0_ffn_mu_k, L0_c, L0_wmod, L1_attn_w_qkv, L1_attn_w_proj, L1_attn_b_proj, L1_ffn_w1_w, L1_ffn_w1_s, L1_ffn_w2_w, L1_ffn_w2_s, L1_ffn_h1_w, L1_ffn_h1_s, L1_ffn_h2_w, L1_ffn_h2_s, L1_ffn_w3_w, L1_ffn_w3_s, L1_c, L1_wmod):

    def _L0_attn_ref(x, norm_w, Wq, Wk, Wv, Wqf, Wkf, Wout):
        import jax, jax.numpy as jnp
        import numpy as np
        import math
        D_MODEL = 256
        N_HEADS = 16
        HEAD_DIM = D_MODEL // N_HEADS
        FEAT = 16
        WINDOW = 64
        EPS_NORM = 1e-06
        EPS_LIN = 1e-06
        CHUNK = 128

        def rmsnorm(x, w):
            return x * jax.lax.rsqrt(jnp.mean(x * x, axis=-1, keepdims=True) + EPS_NORM) * w

        def taylor_feature_map(x):
            d = x.shape[-1]
            iu, ju = jnp.triu_indices(d)
            scale = jnp.where(iu == ju, 0.5, 1.0 / math.sqrt(2.0)).astype(x.dtype)
            quad = x[..., iu] * x[..., ju] * scale
            ones = jnp.ones(x.shape[:-1] + (1,), dtype=x.dtype)
            return jnp.concatenate([ones, x, quad], axis=-1)

        def linear_attention_causal(q_phi, k_phi, v):
            B, T, H, F = q_phi.shape
            D = v.shape[-1]
            Nc = T // CHUNK
            qc = q_phi.reshape(B, Nc, CHUNK, H, F).transpose(1, 0, 2, 3, 4)
            kc = k_phi.reshape(B, Nc, CHUNK, H, F).transpose(1, 0, 2, 3, 4)
            vc = v.reshape(B, Nc, CHUNK, H, D).transpose(1, 0, 2, 3, 4)
            causal = jnp.tril(jnp.ones((CHUNK, CHUNK), dtype=q_phi.dtype))

            def step(carry, inp):
                kv, ksum = carry
                qb, kb, vb = inp
                A = jnp.einsum('bchf,bshf->bhcs', qb, kb) * causal
                y = jnp.einsum('bhcs,bshd->bchd', A, vb) + jnp.einsum('bchf,bhfd->bchd', qb, kv)
                z = jnp.einsum('bhcs->bch', A) + jnp.einsum('bchf,bhf->bch', qb, ksum)
                kv = kv + jnp.einsum('bshf,bshd->bhfd', kb, vb)
                ksum = ksum + kb.sum(axis=1)
                return ((kv, ksum), y / (z[..., None] + EPS_LIN))
            kv0 = jnp.zeros((B, H, F, D), dtype=q_phi.dtype)
            ks0 = jnp.zeros((B, H, F), dtype=q_phi.dtype)
            _, ys = jax.lax.scan(step, (kv0, ks0), (qc, kc, vc))
            return ys.transpose(1, 0, 2, 3, 4).reshape(B, T, H, D)

        def sliding_window_attention(q, k, v):
            B, T, H, D = q.shape
            scale = 1.0 / math.sqrt(D)
            t = jnp.arange(T)
            allowed = (t[None, :] <= t[:, None]) & (t[None, :] >= t[:, None] - WINDOW)
            scores = jnp.einsum('bqhd,bkhd->bhqk', q, k) * scale
            scores = jnp.where(allowed[None, None], scores, -jnp.inf)
            attn = jax.nn.softmax(scores, axis=-1)
            out = jnp.einsum('bhqk,bkhd->bqhd', attn, v)
            return out.reshape(B, T, H * D)
        B, T, _ = x.shape
        h = rmsnorm(x, norm_w)
        q = (h @ Wq).reshape(B, T, N_HEADS, HEAD_DIM)
        k = (h @ Wk).reshape(B, T, N_HEADS, HEAD_DIM)
        v = (h @ Wv).reshape(B, T, N_HEADS, HEAD_DIM)
        q_phi = taylor_feature_map(q @ Wqf)
        k_phi = taylor_feature_map(k @ Wkf)
        lin = linear_attention_causal(q_phi, k_phi, v).reshape(B, T, D_MODEL)
        win = sliding_window_attention(q, k, v)
        out = jnp.concatenate([lin, win], axis=-1) @ Wout
        return x + out

    def _L0_ffn_ref(x, W_r, W_k, W_v, mu_r, mu_k):
        import jax, jax.numpy as jnp
        import numpy as np
        DIM = 256

        def _reference_tuple_inner(x, W_r, W_k, W_v, mu_r, mu_k):
            B, T, C = x.shape
            x_prev = jnp.concatenate([jnp.zeros((B, 1, C), x.dtype), x[:, :-1, :]], axis=1)
            xr = mu_r * x + (1.0 - mu_r) * x_prev
            xk = mu_k * x + (1.0 - mu_k) * x_prev
            r = jax.nn.sigmoid(jnp.einsum('btc,dc->btd', xr, W_r))
            k = jnp.einsum('btc,dc->btd', xk, W_k)
            k_act = jnp.square(jax.nn.relu(k))
            out = r * jnp.einsum('btc,dc->btd', k_act, W_v)
            new_state = x[:, -1, :]
            return (out, new_state)
        return _reference_tuple_inner(x, W_r, W_k, W_v, mu_r, mu_k)[0]

    def _L1_attn_ref(x, w_qkv, w_proj, b_proj):
        import jax, jax.numpy as jnp
        import numpy as np
        MAX_WAVELENGTH = 10000.0
        NEG_INF = -1000000000.0

        def apply_rope(x):
            S, D = (x.shape[1], x.shape[-1])
            inv_freq = 1.0 / MAX_WAVELENGTH ** (jnp.arange(0, D, 2, dtype=jnp.float32) / D)
            t = jnp.arange(S, dtype=jnp.float32)[:, None] * inv_freq[None, :]
            emb = jnp.concatenate([t, t], axis=-1)
            cos = jnp.cos(emb)[None, :, None, :].astype(x.dtype)
            sin = jnp.sin(emb)[None, :, None, :].astype(x.dtype)
            x1, x2 = jnp.split(x, 2, axis=-1)
            rotated = jnp.concatenate([-x2, x1], axis=-1)
            return x * cos + rotated * sin
        B, S, dim = x.shape
        heads = 16
        head_dim = dim // heads
        scale = head_dim ** (-0.5)
        qkv = x @ w_qkv
        qkv = qkv.reshape(B, S, 3, heads, head_dim)
        Q, K, V = (qkv[:, :, 0], qkv[:, :, 1], qkv[:, :, 2])
        Q = apply_rope(Q)
        K = apply_rope(K)
        attn = jnp.einsum('bqhd,bkhd->bhqk', Q, K) * scale
        causal = jnp.tril(jnp.ones((S, S), dtype=bool))[None, None]
        attn = jnp.where(causal, attn, jnp.asarray(NEG_INF, attn.dtype))
        attn = jax.nn.softmax(attn, axis=-1)
        out = jnp.einsum('bhqk,bkhd->bqhd', attn, V).reshape(B, S, dim)
        return out @ w_proj + b_proj

    def _L1_ffn_ref(x, w1_w, w1_s, w2_w, w2_s, h1_w, h1_s, h2_w, h2_s, w3_w, w3_s):
        import jax, jax.numpy as jnp
        import numpy as np
        D_IN, D_HID = (256, 1024)

        def _ternary(key, shape):
            return jax.random.randint(key, shape, -1, 2).astype(jnp.float32)

        def _tlin(x, w, s):
            return jnp.einsum('bsi,oi->bso', x, w) * s
        h = jax.nn.silu(_tlin(x, w1_w, w1_s)) * _tlin(x, w2_w, w2_s)
        h = jax.nn.gelu(_tlin(h, h1_w, h1_s), approximate=False)
        h = jax.nn.gelu(_tlin(h, h2_w, h2_s), approximate=False)
        return _tlin(h, w3_w, w3_s)
    x = L0_attn_x
    mod = (_silu(L0_c) @ L0_wmod).reshape(L0_c.shape[0], 6, 1, -1)
    sa, ca, ga, sb, cb, gb = (mod[:, 0], mod[:, 1], mod[:, 2], mod[:, 3], mod[:, 4], mod[:, 5])
    ga = (2 * (ga >= 0) - 1) * jnp.maximum(jnp.abs(ga), 0.25)
    gb = (2 * (gb >= 0) - 1) * jnp.maximum(jnp.abs(gb), 0.25)
    h = _layernorm(x, axis=-1) * (1 + ca) + sa
    x = x + ga * _L0_attn_ref(h, L0_attn_norm_w, L0_attn_Wq, L0_attn_Wk, L0_attn_Wv, L0_attn_Wqf, L0_attn_Wkf, L0_attn_Wout)
    h = _layernorm(x, axis=-1) * (1 + cb) + sb
    x = x + gb * _L0_ffn_ref(h, L0_ffn_W_r, L0_ffn_W_k, L0_ffn_W_v, L0_ffn_mu_r, L0_ffn_mu_k)
    mod = (_silu(L1_c) @ L1_wmod).reshape(L1_c.shape[0], 6, 1, -1)
    sa, ca, ga, sb, cb, gb = (mod[:, 0], mod[:, 1], mod[:, 2], mod[:, 3], mod[:, 4], mod[:, 5])
    ga = (2 * (ga >= 0) - 1) * jnp.maximum(jnp.abs(ga), 0.25)
    gb = (2 * (gb >= 0) - 1) * jnp.maximum(jnp.abs(gb), 0.25)
    h = _layernorm(x, axis=-1) * (1 + ca) + sa
    x = x + ga * _L1_attn_ref(h, L1_attn_w_qkv, L1_attn_w_proj, L1_attn_b_proj)
    h = _layernorm(x, axis=-1) * (1 + cb) + sb
    x = x + gb * _L1_ffn_ref(h, L1_ffn_w1_w, L1_ffn_w1_s, L1_ffn_w2_w, L1_ffn_w2_s, L1_ffn_h1_w, L1_ffn_h1_s, L1_ffn_h2_w, L1_ffn_h2_s, L1_ffn_w3_w, L1_ffn_w3_s)
    return x

_drawn_inputs = setup_inputs


def setup_inputs(seed=0):
    import zlib

    import numpy as np

    out = dict(_drawn_inputs(seed))
    spreads = {'L0_attn_norm_w': (1.0, 0.2), 'L1_attn_b_proj': (0.0, 0.1)}
    factors = {}
    for name, (base, spread) in spreads.items():
        noise = np.random.default_rng([zlib.crc32(name.encode()), seed]).standard_normal(out[name].shape)
        drawn = base * np.exp(spread * noise) if base else spread * noise
        out[name] = jnp.asarray(drawn.astype(out[name].dtype))
    for name, factor in factors.items():
        out[name] = (out[name] * factor).astype(out[name].dtype)
    return out
```

```python
from contextlib import ExitStack

import numpy as np

import concourse.bass as bass
from concourse import mybir

F32 = mybir.dt.float32
F32R = mybir.dt.float32r
ALU = mybir.AluOpType
ACT = mybir.ActivationFunctionType
AX = mybir.AxisListType

P = 128
B = 8
S = 512
D = 256
NT = S // P
ND = D // P
NH = 16
HD = D // NH
NP = NH // 2
G = 64
WIN = 64
HID = 1024
NHID = HID // P
NMOD = 6
LN_EPS = 1e-5
RMS_EPS = 1e-6
LIN_EPS = 1e-6
NEG = -1e30
VW = 32
SLOTS = 3


class Turn:

    def __init__(self, slot, nth, per_step):
        self.slot, self.nth, self.per_step = slot, nth, per_step

    def filled(self, b):
        return b * self.per_step + self.nth + 1


    def emptied(self, b):
        return b * self.per_step + self.nth + 1

    def freed(self, b):
        return b * self.per_step + self.nth + 2


DIAGONALS = ((0, 512, 2), (1024, 384, 4), (1536, 768, 2))


def weight_views(pair):
    first, rest = pair[:, 0:1024].rearrange("p (a q) -> p a q", a=2), pair[:, 1024:2560].rearrange("p (a q) -> p a q", a=2)
    return first, rest[:, :, 0:512], rest[:, :, 512:768]


def turns_of(order):
    per = [len(range(s, len(order), SLOTS)) for s in range(SLOTS)]
    assert len(set(order)) == len(order)
    return {key: Turn(i % SLOTS, i // SLOTS, per[i % SLOTS]) for i, key in enumerate(order)}


def end_wait(eng, waits):
    eng.sem_inc(waits, 1)


def groups(nat):
    return nat.rearrange("p h (g d) -> p h g d", d=HD)


def heads(x):
    return x.rearrange("p (h d) -> p h d", d=HD)


def twice(x):
    return x.unsqueeze(2).broadcast_to([P, NH, 2, HD])


def modulation_setup(nc, eng, link, modT, sgn, mag):
    for v in (1, 4):
        a = modT[:, v * ND:(v + 1) * ND, :]
        link(nc.vector.tensor_scalar(a, a, 1.0, None, ALU.add))
    for v in (2, 5):
        a = modT[:, v * ND:(v + 1) * ND, :]
        link(nc.vector.tensor_scalar(sgn[:], a, 0.0, 2.0, ALU.is_ge, ALU.mult))
        link(nc.vector.tensor_scalar(mag[:], a, -1.0, None, ALU.mult))
        link(nc.vector.tensor_tensor(mag[:], a, mag[:], ALU.max))
        link(nc.vector.tensor_scalar(mag[:], mag[:], 0.25, None, ALU.max))
        link(nc.vector.scalar_tensor_tensor(a, sgn[:], -1.0, mag[:], ALU.add, ALU.mult))



def order_layer0():
    o = ["gates", "hT"]
    for t in range(NT):
        o.append(("proj", t))
        if t:
            o += [("stack", t - 1, k) for k in range(4)]
    o.append("v")
    o += [("stack", NT - 1, k) for k in range(4)]
    o += [("winmax", 0, g) for g in range(2)] + [("winmax", t, g) for t in range(1, NT) for g in range(4)]
    o.append("maxT")
    for seq in range(2 * NP + 2):
        if seq < 2 * NP:
            o += [("lin", seq, u) for u in range(3)] if seq < NP else [("win", seq - NP, u) for u in range(2)]
        if seq >= 3 and seq % 2:
            o.append(("heads", (seq - 3) // 2))
    o += [("oT", 0), ("oT", 1), "out", "xT", "r", "k", "ffn"]
    return o


def layer0(nc, x, norm_w, Wq, Wk, Wv, Wqf, Wkf, Wout, W_r, W_k, W_v, mu_r, mu_k, c, wmod, x_mid):
    turns = turns_of(order_layer0())
    with ExitStack() as ctx:
        def sb(name, shape, dt=F32):
            return ctx.enter_context(nc.sbuf_tensor("a_" + name, shape, dt))

        def sem(name):
            return ctx.enter_context(nc.semaphore("a_" + name))

        ring = ctx.enter_context(nc.psum_tensor("a_ring", [P, SLOTS, 1024], F32))
        acc = ctx.enter_context(nc.psum_tensor("a_acc", [P, 2, 512], F32))

        ident = sb("ident", [P, P])
        identr = sb("identr", [P, P], F32R)
        band = sb("band", [P, 192])
        bandT = sb("bandT", [P, 192])
        bandr = sb("bandr", [P, 192], F32R)
        bandTr = sb("bandTr", [P, 192], F32R)
        minus_half = sb("minus_half", [P, 4])
        wqk = sb("wqk", [P, ND, 2 * D])
        wqkf = sb("wqkf", [P, ND, 2 * D])
        wv = sb("wv", [P, ND, D])
        wout = sb("wout", [P, 2 * ND, D])
        wrT = sb("wrT", [P, ND, D])
        wkT = sb("wkT", [P, ND, D])
        wvT = sb("wvT", [P, ND, D])
        turned = sb("turned", [P, ND, D])
        fold = sb("fold", [P, 2, P])
        normw = sb("normw", [P, ND])
        mu = sb("mu", [P, 2, ND])
        one_mu = sb("one_mu", [P, 2, ND])
        cT = sb("cT", [P, ND, B])
        cS = sb("cS", [P, ND, B])
        modT = sb("modT", [P, NMOD * ND, B])
        sgn = sb("sgn", [P, ND, B])
        mag = sb("mag", [P, ND, B])
        mod = sb("mod", [P, NMOD * ND])
        gates = sb("gates", [P, 4, D])
        xin = sb("xin", [P, NT, D])
        xn = sb("xn", [P, NT, D])
        h = sb("h", [P, NT, D])
        xg = sb("xg", [P, NT, D])
        tmp = sb("tmp", [P, NT, D])
        x1 = h
        x2 = sb("x2", [P, NT, D])
        sq = sb("sq", [P, D])
        stats = sb("stats", [P, NT, 6])
        meanvar = sb("meanvar", [P, NT, 2])
        vareps = sb("vareps", [P, NT])
        rstd = sb("rstd", [P, NT])
        sumsq = sb("sumsq", [P, NT])
        msq = sb("msq", [P, NT])
        rrms = sb("rrms", [P, NT])
        hT = tmp[:].rearrange("p t d -> p (t d)").rearrange("p (k s) -> p k s", k=ND)
        nat = [[sb(f"nat{k}_{i}", [P, NH, G], F32R) for i in range(2)] for k in range(4)]
        stack = [sb(f"stack{k}", [P, NP, S], F32R) for k in range(4)]
        va = sb("va", [P, NT, NH, VW])
        negmax = sb("negmax", [P, NT, NH])
        maxT = sb("maxT", [NH, S], F32R)
        work = sb("work", [P, 5120])
        probs = [work[:, 2560 * i:2560 * (i + 1)] for i in range(2)]
        wm = work[:, 0:ND * NMOD * D].rearrange("p (k n) -> p k n", k=ND)
        raw = work[:, 3072:3072 + 3 * ND * D].rearrange("p (i k n) -> p i k n", i=3, k=ND)
        mix = work[:, 0:2048].rearrange("p (i k s) -> p i k s", i=2, k=ND)
        kr = work[:, 2048:3072].rearrange("p (k s) -> p k s", k=ND)
        ka = work[:, 3072:4096].rearrange("p (k s) -> p k s", k=ND)
        rg = work[:, 4096:5120].rearrange("p (t d) -> p t d", t=NT)
        den = sb("den", [P, 2, NT, 4])
        rden = sb("rden", [P, 2, NT, 4])
        sums = [sb(f"sums{i}", [P, S]) for i in range(2)]
        onat = sb("onat", [P, NT, 2 * D])
        oT = sb("oT", [P, 2 * ND, S])
        xT = sb("xT", [P, ND, S + 2])

        s_w = sem("weights_loaded")
        s_small = sem("small_loaded")
        s_const = sem("constants_ready")
        s_pool = sem("pool_setup_step")
        s_diag = sem("fold_blocks_zeroed")
        s_silu = sem("silu_c_ready")
        s_modp = sem("modulation_product")
        s_modr = sem("modulation_read")
        s_wt = sem("weights_turned")
        s_wr = sem("turned_weights_read")
        s_setup = sem("dve_setup_step")
        s_ready = sem("weights_ready")
        x_in = sem("x_loaded")
        xin_free = sem("x_used")
        slot_full = [sem(f"slot{i}_full") for i in range(SLOTS)]
        slot_free = [sem(f"slot{i}_free") for i in range(SLOTS)]
        dve_step = sem("dve_own_result")
        dve_waits = sem("dve_waits_met")
        pool_waits = sem("pool_waits_met")
        act_step = sem("act_own_result")
        pool_step = sem("pool_own_result")
        mod_ready = sem("mod_ready")
        var_ready = sem("var_ready")
        rstd_ready = sem("rstd_ready")
        h_ready = sem("h_ready")
        sumsq_ready = sem("sumsq_ready")
        hn_ready = sem("hn_ready")
        xg_ready = sem("xg_ready")
        hi_ready = sem("hi_ready")
        lo_ready = sem("lo_ready")
        maxT_ready = sem("maxT_ready")
        maxrow_ready = sem("maxrow_in_stack")
        lin_ready = sem("lin_weights_masked")
        pv_done = sem("pair_products_done")
        sums_ready = sem("sums_copied")
        xn_ready = sem("xn_ready")
        xT_ready = sem("xT_ready")
        mix_ready = sem("mix_ready")
        kr_ready = sem("kr_ready")
        ka_ready = sem("ka_ready")
        x2_ready = sem("x2_ready")
        x2_sent = sem("x2_sent")
        block = ctx.enter_context(nc.Block())

        x_v = x.rearrange("b (t p) d -> b p t d", p=P)
        out_v = x_mid.rearrange("b (t p) d -> b p t d", p=P)
        rows = "(k p) n -> p k n"

        def heads_of(o, a):
            return o[:, :, a * 4 * HD:(a + 1) * 4 * HD].rearrange("p t (h d) -> p t h d", d=HD)

        def banks(slot, w):
            return ring[:, slot].rearrange("p (a q) -> p a q", a=2)[:, :, 0:w]

        lin_units = [[(e, 0, 512 * e, 512 * e) for e in range(2)],
                     [(e, kb, 512 * e + o, 1024 + 768 * e + o) for kb, o in ((1, 0), (3, 384)) for e in range(2)],
                     [(e, 2, 512 * e, 1536 + 768 * e) for e in range(2)]]
        win_units = [[(e, kb, 512 * e + o, 512 * e + o) for kb, o in ((0, 0), (1, 192), (3, 384)) for e in range(2)],
                     [(e, 2, 512 * e, 1024 + 192 * e) for e in range(2)]]

        @block.sync
        def _(sp):
            for dst, src in ((wqk[:, :, 0:D], Wq.rearrange(rows, p=P)), (wqk[:, :, D:2 * D], Wk.rearrange(rows, p=P)),
                             (wv[:], Wv.rearrange(rows, p=P)), (wout[:], Wout.rearrange(rows, p=P)),
                             (raw[:, 0], W_r.rearrange(rows, p=P)), (raw[:, 1], W_k.rearrange(rows, p=P)),
                             (raw[:, 2], W_v.rearrange(rows, p=P)), (wm, wmod.rearrange(rows, p=P))):
                sp.dma_start(dst, src).then_inc(s_w, 16)
            for dst, src in ((normw[:], norm_w), (mu[:, 0], mu_r), (mu[:, 1], mu_k)):
                sp.dma_start(dst, src.rearrange("(k p) -> p k", p=P), allow_slow_non_contiguous=True).then_inc(s_small, 16)
            for k in range(ND):
                sp.dma_start(cT[:, k, :], c[:, k * P:(k + 1) * P].rearrange("b p -> p b"), allow_slow_non_contiguous=True).then_inc(s_small, 16)
            sp.wait_ge(s_diag, 1)
            for i, w in enumerate((Wqf, Wkf)):
                for e in range(P // HD):
                    sp.dma_start(fold[e * HD:(e + 1) * HD, i, e * HD:(e + 1) * HD], w).then_inc(s_small, 16)
            with sp.Fori(0, B) as b:
                sp.wait_ge(xin_free, b + 1)
                sp.dma_start(xin[:], x_v[b]).then_inc(x_in, 16)
                sp.wait_ge(maxT_ready, b + 1)
                for e in range(2):
                    sp.dma_start(stack[0][e * G + 3 * HD:e * G + 3 * HD + 1, :, :].bitcast(F32),
                                 maxT[e:NH:2, :].bitcast(F32)).then_inc(maxrow_ready, 16)

        @block.gpsimd
        def _(pool):
            n = [0]

            def link(ins):
                n[0] += 1
                ins.then_inc(s_pool, 1)
                pool.wait_ge(s_pool, n[0])

            nc.gpsimd.memset(fold[:], 0.0).then_inc(s_diag, 1)
            link(nc.gpsimd.memset(ident[:], 1.0))
            link(nc.gpsimd.affine_select(out=ident[:], in_=ident[:], compare_op=ALU.is_equal, fill=0.0, base=0,
                                         pattern=[[-1, P]], channel_multiplier=1))
            for m, base in ((band, WIN), (bandT, WIN)):
                link(nc.gpsimd.memset(m[:], 0.0))
                link(nc.gpsimd.affine_select(out=m[:], in_=m[:], compare_op=ALU.is_ge, fill=NEG, base=base,
                                             pattern=[[-1, 192]], channel_multiplier=1))
                link(nc.gpsimd.affine_select(out=m[:], in_=m[:], compare_op=ALU.is_ge, fill=NEG, base=0,
                                             pattern=[[1, 192]], channel_multiplier=-1))
            nc.gpsimd.memset(minus_half[:], -0.5)
            nc.gpsimd.memset(xT[:, :, 0:1], 0.0)
            link(nc.gpsimd.memset(va[:], 0.0))
            nc.gpsimd.memset(va[:, :, :, HD:HD + 1], 1.0).then_inc(s_const, 1)
            pool.wait_ge(s_ready, 1)
            own = 2
            with pool.Fori(0, B) as b:
                pool.wait_ge(var_ready, b * 3 + 1)
                nc.gpsimd.tensor_tensor(rstd[:], vareps[:], minus_half[:], ALU.pow).then_inc(rstd_ready, 1)
                pool.wait_ge(var_ready, b * 3 + 2)
                nc.gpsimd.tensor_tensor(rrms[:], msq[:], minus_half[:], ALU.pow).then_inc(rstd_ready, 1)
                pool.wait_ge(h_ready, b + 1)
                nc.gpsimd.tensor_tensor(xg[:], h[:], gates[:, 2:3, :].broadcast_to([P, NT, D]), ALU.mult).then_inc(pool_step, 1)
                pool.wait_ge(pool_step, b * own + 1)
                pool.wait_ge(x_in, b * 16 + 16)
                nc.gpsimd.tensor_tensor(xg[:], xg[:], xin[:], ALU.add).then_inc(pool_step, 1)
                pool.wait_ge(pool_step, b * own + 2)
                pool.sem_inc(xg_ready, 1)
                pool.sem_inc(xin_free, 1)
                for p in range(NP):
                    for u, (o, step, blocks) in enumerate(DIAGONALS):
                        v = turns["lin", p, u]
                        pb = probs[p % 2]
                        d = bass.AP(tensor=pb.tensor, offset=pb.offset + o, ap=[pb.ap[0], [step, blocks], [1, P]])
                        pool.wait_ge(slot_free[v.slot], v.freed(b))
                        end_wait(pool, pool_waits)
                        nc.gpsimd.affine_select(out=d, in_=d, compare_op=ALU.is_ge, fill=0.0, base=0,
                                                pattern=[[0, blocks], [1, P]],
                                                channel_multiplier=-1).then_inc(lin_ready, 1)
                pool.wait_ge(var_ready, b * 3 + 3)
                nc.gpsimd.tensor_tensor(rstd[:], vareps[:], minus_half[:], ALU.pow).then_inc(rstd_ready, 1)

        @block.vector
        def _(dve):
            n = [0]

            def once(ins):
                n[0] += 1
                ins.then_inc(s_setup, 1)
                dve.wait_ge(s_setup, n[0])

            dve.wait_ge(s_const, 1)
            nc.vector.tensor_copy(identr[:], ident[:])
            nc.vector.tensor_copy(bandr[:], band[:])
            nc.vector.tensor_copy(bandTr[:], bandT[:])
            for k in range(4):
                for i in range(2):
                    once(nc.vector.memset(nat[k][i][:].bitcast(F32), 0.0))
            for i in range(2):
                once(nc.vector.memset(nat[1][i][:, :, 3 * HD:3 * HD + 1].bitcast(F32), 1.0))
            dve.wait_ge(s_small, 16 * (3 + ND + 2 * P // HD))
            once(nc.vector.tensor_scalar(one_mu[:], mu[:], -1.0, 1.0, ALU.mult, ALU.add))
            dve.wait_ge(s_modp, 1)
            once(nc.vector.tensor_copy(modT[:].rearrange("p v b -> p (v b)"), ring[:, 0, 0:NMOD * ND * B]))
            modulation_setup(nc, dve, once, modT, sgn, mag)
            dve.wait_ge(s_w, 16 * 8)
            for k in range(ND):
                once(nc.vector.tensor_scalar(wqk[:, k], wqk[:, k], normw[:, k:k + 1], None, ALU.mult))
                once(nc.vector.tensor_scalar(wv[:, k], wv[:, k], normw[:, k:k + 1], None, ALU.mult))
            dve.sem_inc(s_wr, 1)
            for i, w in enumerate((wrT, wkT, wvT)):
                dve.wait_ge(s_wt, i + 1)
                nc.vector.tensor_copy(w[:].rearrange("p k n -> p (k n)"), ring[:, 0, 0:512]).then_inc(s_wr, 1)
            for i in range(2):
                dve.wait_ge(s_wt, 4 + 2 * i)
                nc.vector.tensor_copy(turned[:].rearrange("p k n -> p (k n)"), ring[:, 0, 0:512]).then_inc(s_wr, 1)
                dve.wait_ge(s_wt, 5 + 2 * i)
                nc.vector.tensor_copy(wqkf[:, :, i * D:(i + 1) * D], ring[:, 0, 0:512].rearrange("p (k n) -> p k n", n=D)).then_inc(s_wr, 1)
            dve.wait_ge(s_wr, 8)
            dve.sem_inc(xin_free, 1)
            dve.sem_inc(maxrow_ready, 1)
            dve.sem_inc(s_ready, 1)

            n = [0]
            STEPS = 28
            with dve.Fori(0, B) as b:
                m = [0]

                def link(ins, before_aggregate=False):
                    m[0] += 1
                    ins.then_inc(dve_step, 1)
                    dve.wait_ge(dve_step, b * STEPS + m[0])
                    if before_aggregate:
                        end_wait(dve, dve_waits)

                def norm_stats(src, k, first):
                    for t in range(NT):
                        ins = nc.vector.bn_stats(stats[:, t], src[:, t])
                    link(ins, before_aggregate=True)
                    for t in range(NT):
                        ins = nc.vector.bn_aggr(meanvar[:, t], stats[:, t])
                    link(ins)
                    nc.vector.tensor_scalar(vareps[:], meanvar[:, :, 1], LN_EPS, None, ALU.add).then_inc(var_ready, 1)

                nc.vector.tensor_copy(mod[:], modT[:, :, b]).then_inc(mod_ready, 1)
                dve.wait_ge(x_in, b * 16 + 16)
                norm_stats(xin, 1, True)
                dve.wait_ge(rstd_ready, b * 3 + 1)
                for t in range(NT):
                    ins = nc.vector.tensor_scalar(xn[:, t], xin[:, t], meanvar[:, t, 0:1], rstd[:, t:t + 1], ALU.subtract, ALU.mult)
                link(ins)
                g = turns["gates"]
                dve.wait_ge(slot_full[g.slot], g.filled(b))
                nc.vector.tensor_copy(gates[:].rearrange("p v d -> p (v d)"), ring[:, g.slot]).then_inc(slot_free[g.slot], 1)
                dve.wait_ge(slot_free[g.slot], g.freed(b))
                link(nc.vector.tensor_tensor(tmp[:], xn[:], gates[:, 1:2, :].broadcast_to([P, NT, D]), ALU.mult))
                link(nc.vector.tensor_tensor(h[:], tmp[:], gates[:, 0:1, :].broadcast_to([P, NT, D]), ALU.add))
                dve.sem_inc(h_ready, 1)
                dve.wait_ge(sumsq_ready, b + 1)
                nc.vector.tensor_scalar(msq[:], sumsq[:], 1.0 / D, RMS_EPS, ALU.mult, ALU.add).then_inc(var_ready, 1)
                dve.wait_ge(rstd_ready, b * 3 + 2)
                for t in range(NT):
                    ins = nc.vector.tensor_scalar(xn[:, t], h[:, t], rrms[:, t:t + 1], None, ALU.mult)
                ins.then_inc(hn_ready, 1)

                def turn_copy(t, k):
                    u = turns["stack", t, k]
                    dve.wait_ge(slot_full[u.slot], u.filled(b))
                    nc.vector.tensor_copy(stack[k][:, :, t * P:(t + 1) * P],
                                          ring[:, u.slot].rearrange("p (n q) -> p n q", q=P)).then_inc(slot_free[u.slot], 1)

                for t in range(NT):
                    u = turns["proj", t]
                    for k in range(4):
                        dve.wait_ge(hi_ready, b * 4 * NT + 4 * t + (k | 1) + 1)
                        lo = 2 if k % 2 else 1
                        ins = nc.vector.tensor_tensor(groups(nat[k][t % 2])[:, :, lo, :], heads(ring[:, u.slot, k * D:(k + 1) * D]),
                                                      groups(nat[k][t % 2])[:, :, 0, :].bitcast(F32), ALU.subtract)
                        if k == 3:
                            ins.then_inc(slot_free[u.slot], 1)
                        else:
                            ins.then_inc(lo_ready, 1)
                    if t:
                        turn_copy(t - 1, 0)
                        turn_copy(t - 1, 2)
                turn_copy(NT - 1, 0)
                turn_copy(NT - 1, 2)
                for key, out, view in (
                        [(("winmax", 0, g), negmax[:, 0, 8 * g:8 * g + 8], "first") for g in range(2)]
                        + [(("winmax", t, g), negmax[:, t, 4 * g:4 * g + 4], "other") for t in range(1, NT) for g in range(4)]):
                    u = turns[key]
                    dve.wait_ge(slot_full[u.slot], u.filled(b))
                    w = P if view == "first" else 192
                    src = ring[:, u.slot].rearrange("p (a r) -> p a r", a=2)[:, :, 0:512 // w * w].rearrange("p a (n q) -> p a n q", q=w)
                    dst = out.rearrange("p (n a) -> p a n", a=2)
                    ins = nc.vector.tensor_reduce(dst, src, AX.X, ALU.max, negate=True)
                    ins.then_inc(slot_free[u.slot], 1)
                u = turns["maxT"]
                dve.wait_ge(slot_full[u.slot], u.filled(b))
                dve.wait_ge(maxrow_ready, b * 32 + 1)
                link(nc.vector.tensor_copy(maxT[:], ring[0:NH, u.slot, 0:S]))
                dve.sem_inc(slot_free[u.slot], 1)
                dve.sem_inc(maxT_ready, 1)

                def sums_copy(a):
                    dve.wait_ge(pv_done, b * 2 * NP + 2 * a + 2)
                    nc.vector.tensor_copy(sums[a % 2][:], acc[:, a % 2, :]).then_inc(sums_ready, 1)

                def divide(a):
                    u = turns["heads", a]
                    src = ring[:, u.slot, 0:S].rearrange("p (t h v) -> p t h v", t=NT, v=VW)
                    dve.wait_ge(slot_full[u.slot], u.filled(b))
                    if a < NP // 2:
                        link(nc.vector.tensor_scalar(den[:, a % 2], src[:, :, :, HD], LIN_EPS, None, ALU.add))
                        link(nc.vector.reciprocal(rden[:, a % 2], den[:, a % 2]))
                    else:
                        link(nc.vector.reciprocal(rden[:, a % 2], src[:, :, :, HD]))
                    nc.vector.tensor_tensor(heads_of(onat, a), src[:, :, :, 0:HD],
                                            rden[:, a % 2].unsqueeze(3).broadcast_to([P, NT, 4, HD]), ALU.mult).then_inc(slot_free[u.slot], 1)

                for a in range(NP):
                    sums_copy(a)
                    divide(a)
                u = turns["oT", 1]
                dve.wait_ge(slot_full[u.slot], u.filled(b))
                nc.vector.tensor_copy(oT[:, 2:4, :].rearrange("p k s -> p (k s)"), ring[:, u.slot]).then_inc(slot_free[u.slot], 1)
                u = turns["out"]
                dve.wait_ge(slot_full[u.slot], u.filled(b))
                link(nc.vector.tensor_tensor(tmp[:], ring[:, u.slot].rearrange("p (t d) -> p t d", d=D),
                                             gates[:, 2:3, :].broadcast_to([P, NT, D]), ALU.mult))
                dve.sem_inc(slot_free[u.slot], 1)
                dve.wait_ge(xg_ready, b + 1)
                link(nc.vector.tensor_tensor(x1[:], tmp[:], xg[:], ALU.add))
                norm_stats(x1, 3, False)
                dve.wait_ge(rstd_ready, b * 3 + 3)
                for t in range(NT):
                    ins = nc.vector.tensor_scalar(xn[:, t], x1[:, t], meanvar[:, t, 0:1], rstd[:, t:t + 1], ALU.subtract, ALU.mult)
                ins.then_inc(xn_ready, 1)
                for i in range(2):
                    for k in range(ND):
                        if i == 0 and k == 0:
                            dve.wait_ge(xT_ready, b + 1)
                        if i == 0 and k == 1:
                            dve.wait_ge(slot_free[turns["xT"].slot], turns["xT"].freed(b))
                        link(nc.vector.tensor_scalar(mix[:, i, k], xT[:, k, 0:S], one_mu[:, i, k:k + 1], None, ALU.mult))
                        ins = nc.vector.scalar_tensor_tensor(mix[:, i, k], xT[:, k, 1:S + 1], mu[:, i, k:k + 1], mix[:, i, k], ALU.mult, ALU.add)
                        ins.then_inc(mix_ready, 1)
                for k in range(ND):
                    if k == 0:
                        dve.wait_ge(kr_ready, b + 1)
                    else:
                        dve.wait_ge(slot_free[turns["k"].slot], turns["k"].freed(b))
                    nc.vector.tensor_tensor(ka[:, k], kr[:, k], kr[:, k], ALU.mult).then_inc(ka_ready, 1)
                dve.wait_ge(slot_free[turns["r"].slot], turns["r"].freed(b))
                link(nc.vector.tensor_tensor(rg, rg, gates[:, 3:4, :].broadcast_to([P, NT, D]), ALU.mult))
                u = turns["ffn"]
                dve.wait_ge(slot_full[u.slot], u.filled(b))
                link(nc.vector.tensor_tensor(tmp[:], ring[:, u.slot].rearrange("p (t d) -> p t d", d=D), rg[:], ALU.mult))
                dve.sem_inc(slot_free[u.slot], 1)
                dve.wait_ge(x2_sent, b * 16 + 1)
                nc.vector.tensor_tensor(x2[:], tmp[:], x1[:], ALU.add).then_inc(x2_ready, 1)
                assert m[0] == STEPS, m[0]

        @block.scalar
        def _(act):
            act.wait_ge(s_small, 16 * (3 + ND + 2 * P // HD))
            nc.scalar.activation(cS[:], cT[:], ACT.Silu).then_inc(s_silu, 1)
            act.wait_ge(s_ready, 1)
            act.sem_inc(x2_sent, 1)
            with act.Fori(0, B) as b:
                act.wait_ge(h_ready, b + 1)
                for t in range(NT):
                    ins = nc.scalar.activation(sq[:], h[:, t], ACT.Square, accum_out=sumsq[:, t:t + 1])
                    if t < NT - 1:
                        ins.then_inc(act_step, 1)
                        act.wait_ge(act_step, b * (NT - 1) + t + 1)
                ins.then_inc(sumsq_ready, 1)
                u = turns["hT"]
                act.wait_ge(slot_full[u.slot], u.filled(b))
                nc.scalar.copy(tmp[:].rearrange("p t d -> p (t d)"), ring[:, u.slot]).then_inc(slot_free[u.slot], 1)

                def turn_copy(t, k):
                    u = turns["stack", t, k]
                    act.wait_ge(slot_full[u.slot], u.filled(b))
                    nc.scalar.copy(stack[k][:, :, t * P:(t + 1) * P],
                                   ring[:, u.slot].rearrange("p (n q) -> p n q", q=P)).then_inc(slot_free[u.slot], 1)

                for t in range(NT):
                    u = turns["proj", t]
                    act.wait_ge(slot_full[u.slot], u.filled(b))
                    for k in range(4):
                        g = groups(nat[k][t % 2])[:, :, 0:2, :] if k % 2 else groups(nat[k][t % 2])[:, :, 0:3:2, :]
                        if t >= 2:
                            v = turns["stack", t - 2, k]
                            act.wait_ge(slot_full[v.slot], v.filled(b))
                        nc.scalar.copy(g, twice(heads(ring[:, u.slot, k * D:(k + 1) * D]))).then_inc(hi_ready, 1)
                    if t:
                        turn_copy(t - 1, 1)
                        turn_copy(t - 1, 3)
                u = turns["v"]
                act.wait_ge(slot_full[u.slot], u.filled(b))
                nc.scalar.copy(va[:, :, :, 0:HD], ring[:, u.slot].rearrange("p (t h d) -> p t h d", t=NT, d=HD)).then_inc(slot_free[u.slot], 1)
                turn_copy(NT - 1, 1)
                turn_copy(NT - 1, 3)
                for p in range(NP):
                    for i, weights in enumerate(weight_views(probs[p % 2])):
                        u = turns["lin", p, i]
                        act.wait_ge(slot_full[u.slot], u.filled(b))
                        if i == 0 and p >= 2:
                            act.wait_ge(pv_done, b * 2 * NP + p - 1)
                        nc.scalar.activation(weights, banks(u.slot, weights.shape[2]), ACT.Square, bias=1.0, scale=0.5).then_inc(slot_free[u.slot], 1)
                for p in range(NP):
                    for i, (o, w) in enumerate(((0, 512), (1024, 192))):
                        u = turns["win", p, i]
                        act.wait_ge(slot_full[u.slot], u.filled(b))
                        if i == 0:
                            act.wait_ge(pv_done, b * 2 * NP + NP + p - 1)
                        nc.scalar.activation(probs[p % 2][:, o:o + 2 * w].rearrange("p (a q) -> p a q", a=2), banks(u.slot, w), ACT.Exp, scale=float(HD) ** -0.5).then_inc(slot_free[u.slot], 1)
                u = turns["oT", 0]
                act.wait_ge(slot_full[u.slot], u.filled(b))
                nc.scalar.copy(oT[:, 0:2, :].rearrange("p k s -> p (k s)"), ring[:, u.slot]).then_inc(slot_free[u.slot], 1)
                u = turns["xT"]
                act.wait_ge(slot_full[u.slot], u.filled(b))
                for k in range(ND):
                    nc.scalar.activation(xT[:, k, 1:S + 1], ring[:, u.slot, k * S:(k + 1) * S], ACT.Identity,
                                         bias=mod[:, 3 * ND + k:3 * ND + k + 1], scale=mod[:, 4 * ND + k:4 * ND + k + 1]).then_inc(slot_free[u.slot] if k else xT_ready, 1)
                u = turns["r"]
                act.wait_ge(slot_full[u.slot], u.filled(b))
                nc.scalar.activation(work[:, 4096:5120], ring[:, u.slot], ACT.Sigmoid).then_inc(slot_free[u.slot], 1)
                u = turns["k"]
                act.wait_ge(slot_full[u.slot], u.filled(b))
                for k in range(ND):
                    nc.scalar.activation(kr[:, k], ring[:, u.slot, k * S:(k + 1) * S], ACT.Relu).then_inc(slot_free[u.slot] if k else kr_ready, 1)
                act.wait_ge(x2_ready, b + 1)
                act.dma_start(out_v[b], x2[:]).then_inc(x2_sent, 16)
            act.wait_ge(x2_sent, B * 16 + 1)

        @block.tensor
        def _(pe):
            pe.wait_ge(s_silu, 1)
            pe.wait_ge(s_w, 16 * 8)
            for j in range(NMOD * ND):
                for k in range(ND):
                    ins = nc.tensor.matmul(ring[:, 0, j * B:(j + 1) * B], wm[:, k, j * P:(j + 1) * P], cS[:, k], start=(k == 0), stop=(k == ND - 1))
            ins.then_inc(s_modp, 1)
            pe.wait_ge(s_const, 1)
            pe.wait_ge(s_small, 16 * (3 + ND + 2 * P // HD))
            for i in range(3):
                pe.wait_ge(s_wr, i + 1)
                for k in range(ND):
                    for r in range(ND):
                        ins = nc.tensor.transpose(ring[:, 0, k * D + r * P:k * D + (r + 1) * P], raw[:, i, r, k * P:(k + 1) * P], ident[:])
                ins.then_inc(s_wt, 1)
            for i in range(2):
                pe.wait_ge(s_wr, 4 + 2 * i)
                for k in range(ND):
                    for r in range(ND):
                        ins = nc.tensor.transpose(ring[:, 0, k * D + r * P:k * D + (r + 1) * P],
                                                  wqk[:, r, i * D + k * P:i * D + (k + 1) * P], ident[:])
                ins.then_inc(s_wt, 1)
                pe.wait_ge(s_wr, 5 + 2 * i)
                for r in range(ND):
                    for k in range(ND):
                        ins = nc.tensor.matmul(ring[:, 0, r * D + k * P:r * D + (k + 1) * P], turned[:, k, r * P:(r + 1) * P], fold[:, i], start=True, stop=True)
                ins.then_inc(s_wt, 1)
            pe.wait_ge(s_ready, 1)
            for free in slot_free:
                pe.sem_inc(free, 1)

            with pe.Fori(0, B) as b:
                def take(key):
                    u = turns[key]
                    pe.wait_ge(slot_free[u.slot], u.emptied(b))
                    return u.slot

                s = take("gates")
                pe.wait_ge(mod_ready, b + 1)
                for i, v in enumerate((0, 1, 2, 5)):
                    for k in range(ND):
                        ins = nc.tensor.transpose(ring[:, s, i * D + k * P:i * D + (k + 1) * P],
                                                  mod[:, v * ND + k:v * ND + k + 1].broadcast_to([P, P]), ident[:])
                ins.then_inc(slot_full[s], 1)
                s = take("hT")
                pe.wait_ge(hn_ready, b + 1)
                for t in range(NT):
                    for k in range(ND):
                        ins = nc.tensor.transpose(ring[:, s, k * S + t * P:k * S + (t + 1) * P], xn[:, t, k * P:(k + 1) * P], ident[:])
                ins.then_inc(slot_full[s], 1)

                def stacks(t):
                    for k in range(4):
                        s = take(("stack", t, k))
                        if k < 3:
                            pe.wait_ge(lo_ready, b * 3 * NT + 3 * t + k + 1)
                        else:
                            u = turns["proj", t]
                            pe.wait_ge(slot_free[u.slot], u.freed(b))
                        for p in range(NP):
                            ins = nc.tensor.transpose(ring[:, s, p * P:(p + 1) * P],
                                                      nat[k][t % 2][:, 2 * p:2 * p + 2, :].rearrange("p h g -> p (h g)").bitcast(F32), ident[:])
                        ins.then_inc(slot_full[s], 1)

                pe.wait_ge(slot_free[turns["hT"].slot], turns["hT"].freed(b))
                for t in range(NT):
                    s = take(("proj", t))
                    for i, w in enumerate((wqk, wqkf)):
                        for k in range(ND):
                            ins = nc.tensor.matmul(ring[:, s, i * S:(i + 1) * S], hT[:, k, t * P:(t + 1) * P], w[:, k], start=(k == 0), stop=(k == ND - 1))
                    ins.then_inc(slot_full[s], 1)
                    if t:
                        stacks(t - 1)
                s = take("v")
                for t in range(NT):
                    for k in range(ND):
                        ins = nc.tensor.matmul(ring[:, s, t * D:(t + 1) * D], hT[:, k, t * P:(t + 1) * P], wv[:, k], start=(k == 0), stop=(k == ND - 1))
                ins.then_inc(slot_full[s], 1)
                stacks(NT - 1)
                for k in range(4):
                    u = turns["stack", NT - 1, k]
                    pe.wait_ge(slot_free[u.slot], u.freed(b))

                def rows_of(k, hd, lo, n):
                    return stack[k][(hd % 2) * G:(hd % 2 + 1) * G, hd // 2, lo:lo + n]

                for g in range(2):
                    s = take(("winmax", 0, g))
                    for q in range(2):
                        nc.tensor.matmul(ring[:, s, q * 512:(q + 1) * 512], identr[:], bandr[:, None, WIN:192].broadcast_to([P, 4, P]),
                                         start=True, stop=False, skip_group_check=True)
                    for j in range(4):
                        for q in range(2):
                            hd = 8 * g + 2 * j + q
                            ins = nc.tensor.matmul(ring[:, s, q * 512 + j * P:q * 512 + (j + 1) * P], rows_of(0, hd, 0, P), rows_of(1, hd, 0, P),
                                                   start=False, stop=(j == 3), skip_group_check=True)
                    ins.then_inc(slot_full[s], 1)
                for t in range(1, NT):
                    for g in range(4):
                        s = take(("winmax", t, g))
                        for q in range(2):
                            nc.tensor.matmul(ring[:, s, q * 512:q * 512 + 384], identr[:], bandr[:, None, :].broadcast_to([P, 2, 192]),
                                             start=True, stop=False, skip_group_check=True)
                        for j in range(2):
                            for q in range(2):
                                hd = 4 * g + 2 * j + q
                                ins = nc.tensor.matmul(ring[:, s, q * 512 + j * 192:q * 512 + (j + 1) * 192],
                                                       rows_of(0, hd, t * P, P), rows_of(1, hd, t * P - WIN, 192),
                                                       start=False, stop=(j == 1), skip_group_check=True)
                        ins.then_inc(slot_full[s], 1)
                s = take("maxT")
                for g in range(1, 4):
                    u = turns["winmax", NT - 1, g]
                    pe.wait_ge(slot_free[u.slot], u.freed(b))
                for t in range(NT):
                    ins = nc.tensor.transpose(ring[0:NH, s, t * P:(t + 1) * P], negmax[:, t, :], ident[:])
                ins.then_inc(slot_full[s], 1)

                def scores(seq):
                    p = seq % NP
                    for u in range(3 if seq < NP else 2):
                        if seq < NP:
                            s = take(("lin", p, u))
                            for e, kb, o, _ in lin_units[u]:
                                ins = nc.tensor.matmul(ring[:, s, o:o + S - kb * P], rows_of(3, 2 * p + e, kb * P, P),
                                                       rows_of(2, 2 * p + e, kb * P, S - kb * P), start=True, stop=True)
                        else:
                            s = take(("win", p, u))
                            for e in range(2):
                                w = 384 if u == 0 else 192
                                nc.tensor.matmul(ring[:, s, 512 * e:512 * e + w], identr[:], bandTr[:, None, :].broadcast_to([P, w // 192, 192]),
                                                 start=True, stop=False, skip_group_check=True)
                                if u == 0:
                                    nc.tensor.matmul(ring[:, s, 512 * e + w:512 * e + 512], identr[:], bandTr[:, 0:P], start=False, stop=False, skip_group_check=True)
                            for e, kb, o, _ in win_units[u]:
                                w = 192 if kb < NT - 1 else P
                                ins = nc.tensor.matmul(ring[:, s, o:o + w], rows_of(1, 2 * p + e, kb * P, P),
                                                       rows_of(0, 2 * p + e, kb * P, w), start=False, stop=(kb >= 2), skip_group_check=True)
                        ins.then_inc(slot_full[s], 1)

                def values(seq):
                    p = seq % NP
                    a = seq // 2
                    if seq < NP:
                        pe.wait_ge(lin_ready, b * 3 * NP + 3 * p + 3)
                    else:
                        v = turns["win", p, 1]
                        pe.wait_ge(slot_free[v.slot], v.freed(b))
                    if seq % 2 == 0 and a >= 2:
                        pe.wait_ge(sums_ready, b * NP + a - 1)
                    at = {}
                    for u in range(3 if seq < NP else 2):
                        for e, kb, _, o in (lin_units if seq < NP else win_units)[u]:
                            at[e, kb] = o
                    for kb in range(NT):
                        n = S - kb * P if seq < NP else min(192, S - kb * P)
                        for e in range(2):
                            j = 2 * (seq % 2) + e
                            ins = nc.tensor.matmul(acc[VW * j:VW * (j + 1), a % 2, kb * P:kb * P + n], va[:, kb, 2 * p + e, :],
                                                   probs[p % 2][:, at[e, kb]:at[e, kb] + n], start=(kb == 0),
                                                   stop=(kb == NT - 1), skip_group_check=True)
                    ins.then_inc(pv_done, 1)

                def heads_back(a):
                    s = take(("heads", a))
                    pe.wait_ge(sums_ready, b * NP + a + 1)
                    for t in range(NT):
                        ins = nc.tensor.transpose(ring[:, s, t * P:(t + 1) * P], sums[a % 2][:, t * P:(t + 1) * P], ident[:])
                    ins.then_inc(slot_full[s], 1)

                u = turns["v"]
                pe.wait_ge(slot_free[u.slot], u.freed(b))
                for seq in range(2 * NP + 2):
                    if seq == NP:
                        pe.wait_ge(maxrow_ready, b * 32 + 33)
                    if seq < 2 * NP:
                        scores(seq)
                    if 1 <= seq <= 2 * NP:
                        values(seq - 1)
                    if seq >= 3 and seq % 2:
                        heads_back((seq - 3) // 2)

                pe.wait_ge(slot_free[turns["heads", NP - 1].slot], turns["heads", NP - 1].freed(b))
                for i in range(2):
                    s = take(("oT", i))
                    for k in range(2):
                        for t in range(NT):
                            ins = nc.tensor.transpose(ring[:, s, k * S + t * P:k * S + (t + 1) * P], onat[:, t, (2 * i + k) * P:(2 * i + k + 1) * P], ident[:])
                    ins.then_inc(slot_full[s], 1)
                s = take("out")
                for i in range(2):
                    u = turns["oT", i]
                    pe.wait_ge(slot_free[u.slot], u.freed(b))
                for t in range(NT):
                    for k in range(2 * ND):
                        ins = nc.tensor.matmul(ring[:, s, t * D:(t + 1) * D], oT[:, k, t * P:(t + 1) * P], wout[:, k], start=(k == 0), stop=(k == 2 * ND - 1))
                ins.then_inc(slot_full[s], 1)
                s = take("xT")
                pe.wait_ge(xn_ready, b + 1)
                for t in range(NT):
                    for k in range(ND):
                        ins = nc.tensor.transpose(ring[:, s, k * S + t * P:k * S + (t + 1) * P], xn[:, t, k * P:(k + 1) * P], ident[:])
                ins.then_inc(slot_full[s], 1)
                s = take("r")
                pe.wait_ge(mix_ready, b * 2 * ND + ND)
                for t in range(NT):
                    for k in range(ND):
                        ins = nc.tensor.matmul(ring[:, s, t * D:(t + 1) * D], mix[:, 0, k, t * P:(t + 1) * P], wrT[:, k], start=(k == 0), stop=(k == ND - 1))
                ins.then_inc(slot_full[s], 1)
                s = take("k")
                pe.wait_ge(mix_ready, b * 2 * ND + 2 * ND)
                for d in range(ND):
                    for k in range(ND):
                        ins = nc.tensor.matmul(ring[:, s, d * S:(d + 1) * S], wkT[:, k, d * P:(d + 1) * P], mix[:, 1, k], start=(k == 0), stop=(k == ND - 1))
                ins.then_inc(slot_full[s], 1)
                s = take("ffn")
                pe.wait_ge(ka_ready, b * ND + ND)
                for t in range(NT):
                    for k in range(ND):
                        ins = nc.tensor.matmul(ring[:, s, t * D:(t + 1) * D], ka[:, k, t * P:(t + 1) * P], wvT[:, k], start=(k == 0), stop=(k == ND - 1))
                ins.then_inc(slot_full[s], 1)



def order_layer1():
    o = ["gates", "hT"]
    for t in range(NT):
        o.append(("proj", t))
        if t:
            o += [("stack", t - 1, k) for k in range(2)]
    o += [("stack", NT - 1, k) for k in range(2)]
    o += [("max", t, g) for t in range(NT) for g in range(MAX_UNITS[t])]
    o.append("maxT")
    for seq in range(NP + 2):
        if seq < NP:
            o += [("att", seq, u) for u in range(3)]
        if seq >= 3 and seq % 2:
            o.append(("heads", (seq - 3) // 2))
    o += ["oT", "out", "xT"]
    for name in ("gate_up", "h1", "h2"):
        o += [(name, m) for m in range(NHID)]
    o.append("w3")
    return o


MAX_HEADS = (4, 2, 1, 1)
MAX_UNITS = tuple(NH // (2 * n) for n in MAX_HEADS)
CHUNKS = ([("w1", g, 4) for g in range(2)] + [("w2", g, 4) for g in range(2)]
          + [("h1", m, 1) for m in range(NHID)] + [("h2", m, 1) for m in range(NHID)] + [("w3", m, 1) for m in range(ND)])
LOW_BITS = 0xFFF


def layer1(nc, x_mid, w_qkv, w_proj, b_proj, w1_w, w1_s, w2_w, w2_s, h1_w, h1_s, h2_w, h2_s, w3_w, w3_s, c, wmod, rope, out):
    turns = turns_of(order_layer1())
    with ExitStack() as ctx:
        def sb(name, shape, dt=F32):
            return ctx.enter_context(nc.sbuf_tensor("b_" + name, shape, dt))

        def sem(name):
            return ctx.enter_context(nc.semaphore("b_" + name))

        ring = ctx.enter_context(nc.psum_tensor("b_ring", [P, SLOTS, 1024], F32))
        acc = ctx.enter_context(nc.psum_tensor("b_acc", [P, 2, 512], F32))

        ident = sb("ident", [P, P])
        identr = sb("identr", [P, P], F32R)
        causal = sb("causal", [P, P])
        causalr = sb("causalr", [P, P], F32R)
        minus_half = sb("minus_half", [P, 4])
        cossin = sb("cossin", [P, 2, NT, HD])
        wqkv = sb("wqkv", [P, ND, 3 * D])
        wproj = sb("wproj", [P, ND, D])
        w1T = sb("w1T", [P, ND, HID], F32R)
        w2T = sb("w2T", [P, ND, HID], F32R)
        h1T = sb("h1T", [P, NHID, HID], F32R)
        h2T = sb("h2T", [P, NHID, HID], F32R)
        w3T = sb("w3T", [P, NHID, D], F32R)
        s12 = sb("s12", [P, 4, NHID])
        s3b = sb("s3b", [P, 2, ND])
        modT = sb("modT", [P, (NMOD + 1) * ND, B])
        low = sb("low", [P, 2])
        lowT = sb("lowT", [1, P])
        flag = sb("flag", [1, 2], mybir.dt.int32)
        mod = sb("mod", [P, (NMOD + 1) * ND])
        gates = sb("gates", [P, 3, D])
        xin = sb("xin", [P, NT, D])
        x = sb("x", [P, NT, D])
        xn = sb("xn", [P, NT, D])
        tmp = sb("tmp", [P, NT, D])
        flat_tmp = tmp[:].rearrange("p t d -> p (t d)")
        flat_xn = xn[:].rearrange("p t d -> p (t d)")
        hT = flat_tmp.rearrange("p (k s) -> p k s", k=ND)
        onat = tmp
        sums = [flat_xn[:, S * i:S * (i + 1)] for i in range(2)]
        stats = sb("stats", [P, NT, 6])
        meanvar = sb("meanvar", [P, NT, 2])
        vareps = sb("vareps", [P, NT])
        rstd = sb("rstd", [P, NT])
        va = sb("va", [P, NT, NH, HD + 1])
        negmax = sb("negmax", [P, NT, NH])
        den = sb("den", [P, 2, NT, 4])
        rden = sb("rden", [P, 2, NT, 4])
        arena = sb("arena", [P, 16 * 1024], F32R)
        stack = [arena[:, 4096 * k:4096 * (k + 1)].rearrange("p (n s) -> p n s", n=NP) for k in range(2)]
        nat = [[arena[:, 8192 + 1024 * (2 * k + i):8192 + 1024 * (2 * k + i + 1)].rearrange("p (h g) -> p h g", g=G) for i in range(2)] for k in range(2)]
        maxT = arena[0:NH, 12288:12288 + S]
        act_a = arena[:, 0:8192].rearrange("p (k i s) -> p k i s", k=NHID, i=2)
        act_b = arena[:, 8192:16384].rearrange("p (k i s) -> p k i s", k=NHID, i=2)
        h2r = arena[:, 8192:8192 + 2048].rearrange("p (k i s) -> p k i s", k=ND, i=2)
        work = sb("work", [P, 5120])
        probs = [work[:, 2560 * i:2560 * (i + 1)] for i in range(2)]
        qk = [work[:, 2048 * i:2048 * i + 512] for i in range(2)]
        qk_cos = [work[:, 2048 * i + 512:2048 * i + 1024] for i in range(2)]
        qk_sin = [work[:, 2048 * i + 1024:2048 * i + 1536] for i in range(2)]
        qk_rot = [work[:, 2048 * i + 1536:2048 * i + 2048] for i in range(2)]
        oT = work[:, 0:1024].rearrange("p (k s) -> p k s", k=ND)
        hfull = work[:, 1024:2048].rearrange("p (k s) -> p k s", k=ND)
        silu = [work[:, 2048 + 512 * i:2560 + 512 * i] for i in range(2)]
        full = [work[:, 3072 + 512 * i:3584 + 512 * i] for i in range(4)]
        wm = work[:, 0:ND * NMOD * D].rearrange("p (k n) -> p k n", k=ND)
        raw = [work[:, 1024 * i:1024 * (i + 1)] for i in range(3)]
        staged = [work[:, 3072 + 1024 * i:3072 + 1024 * (i + 1)] for i in range(2)]
        lows = flat_tmp
        sgn, mag, cT, cS = (flat_xn[:, 16 * i:16 * (i + 1)].rearrange("p (k b) -> p k b", k=ND) for i in range(4))

        s_w = sem("weights_loaded")
        s_small = sem("small_loaded")
        s_const = sem("constants_ready")
        s_pool = sem("pool_setup_step")
        s_silu = sem("silu_c_ready")
        s_modp = sem("modulation_product")
        raw_loaded = [sem(f"raw_weights{i}_loaded") for i in range(3)]
        w_turned = sem("weights_turned")
        w_staged = sem("weights_staged")
        w_checked = sem("low_bits_collected")
        w_placed = [sem(f"staged{i}_placed") for i in range(2)]
        s_low = sem("low_bits_reduced")
        s_lowT = sem("low_bits_turned")
        s_flag = sem("flag_ready")
        s_setup = sem("dve_setup_step")
        s_ready = sem("weights_ready")
        x_in = sem("x_loaded")
        xin_free = sem("x_used")
        slot_full = [sem(f"slot{i}_full") for i in range(SLOTS)]
        slot_free = [sem(f"slot{i}_free") for i in range(SLOTS)]
        dve_step = sem("dve_own_result")
        dve_waits = sem("dve_waits_met")
        pool_waits = sem("pool_waits_met")
        pool_step = sem("pool_own_result")
        mod_ready = sem("mod_ready")
        var_ready = sem("var_ready")
        rstd_ready = sem("rstd_ready")
        gates_ready = sem("gates_ready")
        xg_ready = sem("x_plus_bias_ready")
        spare_ready = sem("spare_columns_ready")
        xn_ready = sem("xn_ready")
        hT_ready = sem("hT_half_ready")
        qk_ready = sem("qk_copied")
        rot_ready = sem("qk_rotated")
        hi_ready = sem("hi_ready")
        lo_ready = sem("lo_ready")
        maxT_ready = sem("maxT_ready")
        maxrow_ready = sem("maxrow_in_stack")
        att_ready = sem("weights_masked")
        pv_done = sem("pair_products_done")
        sums_ready = sem("sums_copied")
        h2_full = sem("ffn_input_half_ready")
        h2_ready = sem("ffn_input_split")
        silu_ready = sem("silu_ready")
        a_ready = sem("gated_split")
        g1_full = sem("first_gelu_ready")
        g1_ready = sem("first_gelu_split")
        g2_full = sem("second_gelu_ready")
        g2_ready = sem("second_gelu_split")
        x_done = sem("x_result_ready")
        x_sent = sem("x_result_sent")
        block = ctx.enter_context(nc.Block())

        x_v = x_mid.rearrange("b (t p) d -> b p t d", p=P)
        out_v = out.rearrange("b (t p) d -> b p t d", p=P)
        rows = "(k p) n -> p k n"
        weight = {"w1": w1_w, "w2": w2_w, "h1": h1_w, "h2": h2_w, "w3": w3_w}
        turned = {"w1": w1T, "w2": w2T, "h1": h1T, "h2": h2T, "w3": w3T}

        def heads_of(o, a):
            return o[:, :, a * 4 * HD:(a + 1) * 4 * HD].rearrange("p t (h d) -> p t h d", d=HD)

        def banks(slot, w):
            return ring[:, slot].rearrange("p (a q) -> p a q", a=2)[:, :, 0:w]

        units = [[(e, 0, 512 * e, 512 * e) for e in range(2)],
                 [(e, kb, 512 * e + o, 1024 + 768 * e + o) for kb, o in ((1, 0), (3, 384)) for e in range(2)],
                 [(e, 2, 512 * e, 1536 + 768 * e) for e in range(2)]]

        @block.sync
        def _(sp):
            for dst, src in ((wqkv[:], w_qkv.rearrange(rows, p=P)), (wproj[:], w_proj.rearrange(rows, p=P)),
                             (wm, wmod.rearrange(rows, p=P)),
                             (cossin[:, 0], rope[0].rearrange("(t p) d -> p t d", p=P)),
                             (cossin[:, 1], rope[1].rearrange("(t p) d -> p t d", p=P))):
                sp.dma_start(dst, src).then_inc(s_w, 16)
            for dst, src in ((s12[:, 0], w1_s), (s12[:, 1], w2_s), (s12[:, 2], h1_s), (s12[:, 3], h2_s),
                             (s3b[:, 0], w3_s), (s3b[:, 1], b_proj)):
                sp.dma_start(dst, src.rearrange("(k p) -> p k", p=P), allow_slow_non_contiguous=True).then_inc(s_small, 16)
            for k in range(ND):
                sp.dma_start(cT[:, k, :], c[:, k * P:(k + 1) * P].rearrange("b p -> p b"), allow_slow_non_contiguous=True).then_inc(s_small, 16)
            sp.wait_ge(s_modp, 1)

            def load(i):
                name, m, r = CHUNKS[i]
                w = weight[name]
                if r == 1:
                    sp.dma_start(raw[i % 3], w[m * P:(m + 1) * P, :]).then_inc(raw_loaded[i % 3], 16)
                else:
                    sp.dma_start(raw[i % 3].rearrange("p (m n) -> p m n", m=r),
                                 w[m * r * P:(m + 1) * r * P, :].rearrange("(m p) n -> p m n", p=P)).then_inc(raw_loaded[i % 3], 16)

            for i in range(3):
                load(i)
            for i, (name, m, r) in enumerate(CHUNKS):
                sp.wait_ge(w_staged, i + 1)
                k = 8 // r
                sp.dma_start(turned[name][:, :, m * r * P:(m + 1) * r * P].bitcast(F32),
                             staged[i % 2].rearrange("p (k n) -> p k n", k=k)).then_inc(w_placed[i % 2], 16)
                if i + 3 < len(CHUNKS):
                    sp.wait_ge(w_turned, i + 1)
                    sp.wait_ge(w_checked, i + 1)
                    load(i + 3)
            with sp.Fori(0, B) as b:
                sp.wait_ge(xin_free, b + 1)
                sp.dma_start(xin[:], x_v[b]).then_inc(x_in, 16)
                sp.wait_ge(maxT_ready, b + 1)
                for e in range(2):
                    sp.dma_start(stack[0][e * G + 3 * HD:e * G + 3 * HD + 1, :, :].bitcast(F32),
                                 maxT[e:NH:2, :].bitcast(F32)).then_inc(maxrow_ready, 16)

        @block.gpsimd
        def _(pool):
            n = [0]

            def link(ins):
                n[0] += 1
                ins.then_inc(s_pool, 1)
                pool.wait_ge(s_pool, n[0])

            link(nc.gpsimd.memset(ident[:], 1.0))
            link(nc.gpsimd.affine_select(out=ident[:], in_=ident[:], compare_op=ALU.is_equal, fill=0.0, base=0,
                                         pattern=[[-1, P]], channel_multiplier=1))
            link(nc.gpsimd.memset(causal[:], 0.0))
            link(nc.gpsimd.affine_select(out=causal[:], in_=causal[:], compare_op=ALU.is_ge, fill=NEG, base=0,
                                         pattern=[[-1, P]], channel_multiplier=1))
            nc.gpsimd.memset(minus_half[:], -0.5)
            nc.gpsimd.memset(va[:, :, :, HD:HD + 1], 1.0).then_inc(s_const, 1)
            pool.wait_ge(s_ready, 1)
            own = 2
            with pool.Fori(0, B) as b:
                pool.wait_ge(x_done, b + 1)
                end_wait(pool, pool_waits)
                for i in range(2):
                    nc.gpsimd.memset(nat[0][i][:, :, 3 * HD:G].bitcast(F32), 0.0)
                    nc.gpsimd.memset(nat[1][i][:, :, 3 * HD + 1:G].bitcast(F32), 0.0)
                    ins = nc.gpsimd.memset(nat[1][i][:, :, 3 * HD:3 * HD + 1].bitcast(F32), 1.0)
                ins.then_inc(spare_ready, 1)
                pool.wait_ge(var_ready, b * 2 + 1)
                nc.gpsimd.tensor_tensor(rstd[:], vareps[:], minus_half[:], ALU.pow).then_inc(rstd_ready, 1)
                pool.wait_ge(gates_ready, b + 1)
                pool.wait_ge(x_in, b * 16 + 16)
                nc.gpsimd.tensor_tensor(x[:], xin[:], gates[:, 1:2, :].broadcast_to([P, NT, D]), ALU.add).then_inc(pool_step, 1)
                pool.wait_ge(pool_step, b + 1)
                pool.sem_inc(xg_ready, 1)
                pool.sem_inc(xin_free, 1)
                for p in range(NP):
                    for u, (o, step, blocks) in enumerate(DIAGONALS):
                        v = turns["att", p, u]
                        pb = probs[p % 2]
                        d = bass.AP(tensor=pb.tensor, offset=pb.offset + o, ap=[pb.ap[0], [step, blocks], [1, P]])
                        pool.wait_ge(slot_free[v.slot], v.freed(b))
                        end_wait(pool, pool_waits)
                        nc.gpsimd.affine_select(out=d, in_=d, compare_op=ALU.is_ge, fill=0.0, base=0,
                                                pattern=[[0, blocks], [1, P]],
                                                channel_multiplier=-1).then_inc(att_ready, 1)
                pool.wait_ge(var_ready, b * 2 + 2)
                nc.gpsimd.tensor_tensor(rstd[:], vareps[:], minus_half[:], ALU.pow).then_inc(rstd_ready, 1)

        @block.vector
        def _(dve):
            n = [0]

            def once(ins):
                n[0] += 1
                ins.then_inc(s_setup, 1)
                dve.wait_ge(s_setup, n[0])

            dve.wait_ge(s_const, 1)
            nc.vector.tensor_copy(identr[:], ident[:])
            nc.vector.tensor_copy(causalr[:], causal[:])
            nc.vector.memset(acc[:], 0.0)
            once(nc.vector.memset(lows, 0.0))
            dve.wait_ge(s_small, 16 * (6 + ND))
            dve.wait_ge(s_modp, 1)
            once(nc.vector.tensor_copy(modT[:, 0:NMOD * ND].rearrange("p v b -> p (v b)"), ring[:, 0, 0:NMOD * ND * B]))
            modulation_setup(nc, dve, once, modT, sgn, mag)
            for k in range(ND):
                once(nc.vector.tensor_scalar(modT[:, NMOD * ND + k], modT[:, 2 * ND + k], s3b[:, 1, k:k + 1], None, ALU.mult))
                once(nc.vector.tensor_scalar(modT[:, 5 * ND + k], modT[:, 5 * ND + k], s3b[:, 0, k:k + 1], None, ALU.mult))
            I32 = mybir.dt.int32
            for i in range(len(CHUNKS)):
                dve.wait_ge(raw_loaded[i % 3], 16 * (i // 3 + 1))
                if i:
                    dve.wait_ge(w_checked, i)
                nc.vector.scalar_tensor_tensor(lows.bitcast(I32), raw[i % 3].bitcast(I32), LOW_BITS, lows.bitcast(I32),
                                               ALU.bitwise_and, ALU.bitwise_or).then_inc(w_checked, 1)
            dve.wait_ge(w_checked, len(CHUNKS))
            nc.vector.tensor_reduce(low[:, 0:1], lows.bitcast(I32), AX.X, ALU.max).then_inc(s_low, 1)
            dve.wait_ge(s_lowT, 1)
            once(nc.vector.tensor_reduce(lowT[:, 0:1], ring[0:1, 0, 0:P], AX.X, ALU.max))
            nc.vector.tensor_scalar(flag[:, 0:1], lowT[:, 0:1], 0.0, None, ALU.is_gt).then_inc(s_flag, 1)
            for i in range(2):
                dve.wait_ge(w_placed[i], 16 * len(CHUNKS) // 2)
            dve.wait_ge(s_w, 16 * 5)
            dve.wait_ge(s_flag, 1)
            dve.sem_inc(xin_free, 1)
            dve.sem_inc(maxrow_ready, 1)
            dve.sem_inc(x_done, 1)
            dve.sem_inc(s_ready, 1)

            STEPS = STEPS1
            with dve.Fori(0, B) as b:
                m = [0]

                def link(ins, before_aggregate=False):
                    m[0] += 1
                    ins.then_inc(dve_step, 1)
                    dve.wait_ge(dve_step, b * STEPS + m[0])
                    if before_aggregate:
                        end_wait(dve, dve_waits)

                def normalise(src, k):
                    for t in range(NT):
                        ins = nc.vector.bn_stats(stats[:, t], src[:, t])
                    link(ins, before_aggregate=True)
                    for t in range(NT):
                        ins = nc.vector.bn_aggr(meanvar[:, t], stats[:, t])
                    link(ins)
                    nc.vector.tensor_scalar(vareps[:], meanvar[:, :, 1], LN_EPS, None, ALU.add).then_inc(var_ready, 1)
                    dve.wait_ge(rstd_ready, b * 2 + k)
                    for t in range(NT):
                        ins = nc.vector.tensor_scalar(xn[:, t], src[:, t], meanvar[:, t, 0:1], rstd[:, t:t + 1], ALU.subtract, ALU.mult)
                    ins.then_inc(xn_ready, 1)

                nc.vector.tensor_copy(mod[:], modT[:, :, b]).then_inc(mod_ready, 1)
                dve.wait_ge(x_in, b * 16 + 16)
                dve.wait_ge(x_sent, b * 16 + 1)
                normalise(xin, 1)
                dve.wait_ge(xn_ready, b * 2 + 1)
                g = turns["gates"]
                dve.wait_ge(slot_full[g.slot], g.filled(b))
                link(nc.vector.tensor_copy(gates[:].rearrange("p v d -> p (v d)"), ring[:, g.slot, 0:3 * D]))
                dve.sem_inc(slot_free[g.slot], 1)
                dve.sem_inc(gates_ready, 1)

                def turn_copy(t, k):
                    u = turns["stack", t, k]
                    dve.wait_ge(slot_full[u.slot], u.filled(b))
                    nc.vector.tensor_copy(stack[k][:, :, t * P:(t + 1) * P],
                                          ring[:, u.slot].rearrange("p (n q) -> p n q", q=P)).then_inc(slot_free[u.slot], 1)

                for t in range(NT):
                    i = t % 2
                    h32 = "p (h d) -> p h d"
                    src, a, s, r = (z[i].rearrange(h32, d=HD) for z in (qk, qk_cos, qk_sin, qk_rot))
                    half = HD // 2
                    dve.wait_ge(qk_ready, b * NT + t + 1)
                    nc.vector.tensor_tensor(a, src, cossin[:, 0, t:t + 1, :].broadcast_to([P, 2 * NH, HD]), ALU.mult)
                    nc.vector.tensor_tensor(s[:, :, 0:half], src[:, :, half:HD], cossin[:, 1, t:t + 1, 0:half].broadcast_to([P, 2 * NH, half]), ALU.mult)
                    link(nc.vector.tensor_tensor(s[:, :, half:HD], src[:, :, 0:half], cossin[:, 1, t:t + 1, half:HD].broadcast_to([P, 2 * NH, half]), ALU.mult))
                    nc.vector.tensor_tensor(r, a, s, ALU.add).then_inc(rot_ready, 1)
                    for k in range(2):
                        dve.wait_ge(hi_ready, b * 2 * NT + 2 * t + k + 1)
                        lo = 2 if k % 2 else 1
                        nc.vector.tensor_tensor(groups(nat[k][i])[:, :, lo, :], r[:, k * NH:(k + 1) * NH],
                                                groups(nat[k][i])[:, :, 0, :].bitcast(F32), ALU.subtract).then_inc(lo_ready, 1)
                    if t:
                        turn_copy(t - 1, 0)
                turn_copy(NT - 1, 0)
                for t in range(NT):
                    for g in range(MAX_UNITS[t]):
                        u = turns["max", t, g]
                        n_h, w = MAX_HEADS[t], (t + 1) * P
                        dve.wait_ge(slot_full[u.slot], u.filled(b))
                        src = banks(u.slot, n_h * w).rearrange("p a (n q) -> p a n q", q=w)
                        dst = negmax[:, t, 2 * n_h * g:2 * n_h * (g + 1)].rearrange("p (n a) -> p a n", a=2)
                        nc.vector.tensor_reduce(dst, src, AX.X, ALU.max, negate=True).then_inc(slot_free[u.slot], 1)
                u = turns["maxT"]
                dve.wait_ge(slot_full[u.slot], u.filled(b))
                dve.wait_ge(maxrow_ready, b * 32 + 1)
                link(nc.vector.tensor_copy(maxT, ring[0:NH, u.slot, 0:S]))
                dve.sem_inc(slot_free[u.slot], 1)
                dve.sem_inc(maxT_ready, 1)
                for a in range(NP // 2):
                    dve.wait_ge(pv_done, b * NP + 2 * a + 2)
                    nc.vector.tensor_copy(sums[a % 2], acc[:, a % 2, :]).then_inc(sums_ready, 1)
                    u = turns["heads", a]
                    src = ring[:, u.slot, 0:S].rearrange("p (t h v) -> p t h v", t=NT, v=VW)
                    dve.wait_ge(slot_full[u.slot], u.filled(b))
                    link(nc.vector.reciprocal(rden[:, a % 2], src[:, :, :, HD]))
                    nc.vector.tensor_tensor(heads_of(onat, a), src[:, :, :, 0:HD],
                                            rden[:, a % 2].unsqueeze(3).broadcast_to([P, NT, 4, HD]), ALU.mult).then_inc(slot_free[u.slot], 1)
                u = turns["out"]
                dve.wait_ge(slot_full[u.slot], u.filled(b))
                link(nc.vector.tensor_tensor(tmp[:], ring[:, u.slot].rearrange("p (t d) -> p t d", d=D),
                                             gates[:, 0:1, :].broadcast_to([P, NT, D]), ALU.mult))
                dve.sem_inc(slot_free[u.slot], 1)
                dve.wait_ge(xg_ready, b + 1)
                link(nc.vector.tensor_tensor(x[:], x[:], tmp[:], ALU.add))
                normalise(x, 2)
                for k in range(ND):
                    if k == 0:
                        dve.wait_ge(h2_full, b + 1)
                    else:
                        dve.wait_ge(slot_free[turns["xT"].slot], turns["xT"].freed(b))
                    link(nc.vector.tensor_copy(h2r[:, k, 0], hfull[:, k]))
                    nc.vector.tensor_tensor(h2r[:, k, 1], hfull[:, k], h2r[:, k, 0].bitcast(F32), ALU.subtract).then_inc(h2_ready, 1)
                for i in range(NHID):
                    u = turns["gate_up", i]
                    dve.wait_ge(silu_ready, b * NHID + i + 1)
                    if i >= 4:
                        dve.wait_ge(a_ready, b * NHID + i - 3)
                    link(nc.vector.scalar_tensor_tensor(full[i % 4], ring[:, u.slot, S:2 * S], s12[:, 1, i:i + 1], silu[i % 2], ALU.mult, ALU.mult))
                    dve.sem_inc(slot_free[u.slot], 1)
                    link(nc.vector.tensor_copy(act_a[:, i, 0], full[i % 4]))
                    nc.vector.tensor_tensor(act_a[:, i, 1], full[i % 4], act_a[:, i, 0].bitcast(F32), ALU.subtract).then_inc(a_ready, 1)
                for name, dst, ready in (("h1", act_b, g1_ready), ("h2", act_a, g2_ready)):
                    for i in range(NHID):
                        u = turns[name, i]
                        dve.wait_ge(slot_free[u.slot], u.freed(b))
                        link(nc.vector.tensor_copy(dst[:, i, 0], full[i % 4]))
                        nc.vector.tensor_tensor(dst[:, i, 1], full[i % 4], dst[:, i, 0].bitcast(F32), ALU.subtract).then_inc(ready, 1)
                u = turns["w3"]
                dve.wait_ge(slot_full[u.slot], u.filled(b))
                link(nc.vector.tensor_tensor(tmp[:], ring[:, u.slot].rearrange("p (t d) -> p t d", d=D),
                                             gates[:, 2:3, :].broadcast_to([P, NT, D]), ALU.mult))
                dve.sem_inc(slot_free[u.slot], 1)
                nc.vector.tensor_tensor(xn[:], x[:], tmp[:], ALU.add).then_inc(x_done, 1)
                assert m[0] == STEPS, m[0]

        @block.scalar
        def _(act):
            act.wait_ge(s_small, 16 * (6 + ND))
            nc.scalar.activation(cS[:], cT[:], ACT.Silu).then_inc(s_silu, 1)
            for i in range(len(CHUNKS)):
                act.wait_ge(w_turned, i + 1)
                if i >= 2:
                    act.wait_ge(w_placed[i % 2], 16 * (i // 2))
                nc.scalar.copy(staged[i % 2], ring[:, i % SLOTS]).then_inc(w_staged, 1)
            act.wait_ge(s_ready, 1)
            act.sem_inc(x_sent, 1)
            with act.Fori(0, B) as b:
                u = turns["hT"]
                act.wait_ge(slot_full[u.slot], u.filled(b))
                for k in range(ND):
                    nc.scalar.activation(hT[:, k], ring[:, u.slot, k * S:(k + 1) * S], ACT.Identity,
                                         bias=mod[:, k:k + 1], scale=mod[:, ND + k:ND + k + 1]).then_inc(slot_free[u.slot] if k else hT_ready, 1)

                def turn_copy(t, k):
                    u = turns["stack", t, k]
                    act.wait_ge(slot_full[u.slot], u.filled(b))
                    nc.scalar.copy(stack[k][:, :, t * P:(t + 1) * P],
                                   ring[:, u.slot].rearrange("p (n q) -> p n q", q=P)).then_inc(slot_free[u.slot], 1)

                act.wait_ge(spare_ready, b + 1)
                for t in range(NT):
                    u = turns["proj", t]
                    act.wait_ge(slot_full[u.slot], u.filled(b))
                    nc.scalar.copy(qk[t % 2], ring[:, u.slot, 0:S]).then_inc(qk_ready, 1)
                    nc.scalar.copy(va[:, t, :, 0:HD], heads(ring[:, u.slot, S:S + D])).then_inc(slot_free[u.slot], 1)
                    act.wait_ge(rot_ready, b * NT + t + 1)
                    for k in range(2):
                        g = groups(nat[k][t % 2])[:, :, 0:2, :] if k else groups(nat[k][t % 2])[:, :, 0:3:2, :]
                        if t >= 2:
                            v = turns["stack", t - 2, k]
                            act.wait_ge(slot_full[v.slot], v.filled(b))
                        nc.scalar.copy(g, twice(heads(qk_rot[t % 2][:, k * D:(k + 1) * D]))).then_inc(hi_ready, 1)
                    if t:
                        turn_copy(t - 1, 1)
                turn_copy(NT - 1, 1)
                for p in range(NP):
                    for i, weights in enumerate(weight_views(probs[p % 2])):
                        u = turns["att", p, i]
                        act.wait_ge(slot_full[u.slot], u.filled(b))
                        if i == 0 and p >= 2:
                            act.wait_ge(pv_done, b * NP + p - 1)
                        nc.scalar.activation(weights, banks(u.slot, weights.shape[2]),
                                             ACT.Exp, scale=float(HD) ** -0.5).then_inc(slot_free[u.slot], 1)
                u = turns["oT"]
                act.wait_ge(slot_full[u.slot], u.filled(b))
                nc.scalar.copy(work[:, 0:1024], ring[:, u.slot]).then_inc(slot_free[u.slot], 1)
                u = turns["xT"]
                act.wait_ge(slot_full[u.slot], u.filled(b))
                for k in range(ND):
                    nc.scalar.activation(hfull[:, k], ring[:, u.slot, k * S:(k + 1) * S], ACT.Identity, bias=mod[:, 3 * ND + k:3 * ND + k + 1],
                                         scale=mod[:, 4 * ND + k:4 * ND + k + 1]).then_inc(slot_free[u.slot] if k else h2_full, 1)
                for i in range(NHID):
                    u = turns["gate_up", i]
                    act.wait_ge(slot_full[u.slot], u.filled(b))
                    if i >= 2:
                        v = turns["gate_up", i - 2]
                        act.wait_ge(slot_free[v.slot], v.freed(b))
                    nc.scalar.activation(silu[i % 2], ring[:, u.slot, 0:S], ACT.Silu, scale=s12[:, 0, i:i + 1]).then_inc(silu_ready, 1)
                for j, (name, before, own) in enumerate((("h1", a_ready, g1_ready), ("h2", g1_ready, g2_ready))):
                    for i in range(NHID):
                        u = turns[name, i]
                        act.wait_ge(slot_full[u.slot], u.filled(b))
                        if i < 4:
                            act.wait_ge(before, b * NHID + NHID - 3 + i)
                        else:
                            act.wait_ge(own, b * NHID + i - 3)
                        nc.scalar.activation(full[i % 4], ring[:, u.slot, 0:S], ACT.Gelu, scale=s12[:, 2 + j, i:i + 1]).then_inc(slot_free[u.slot], 1)
                act.wait_ge(x_done, b + 2)
                act.dma_start(out_v[b], xn[:]).then_inc(x_sent, 16)
            act.wait_ge(x_sent, B * 16 + 1)

        @block.tensor
        def _(pe):
            pe.wait_ge(s_silu, 1)
            pe.wait_ge(s_w, 16 * 5)
            for j in range(NMOD * ND):
                for k in range(ND):
                    ins = nc.tensor.matmul(ring[:, 0, j * B:(j + 1) * B], wm[:, k, j * P:(j + 1) * P], cS[:, k], start=(k == 0), stop=(k == ND - 1))
            ins.then_inc(s_modp, 1)
            pe.wait_ge(s_const, 1)
            pe.wait_ge(w_checked, 1)
            for i, (name, m, r) in enumerate(CHUNKS):
                pe.wait_ge(raw_loaded[i % 3], 16 * (i // 3 + 1))
                if i >= SLOTS:
                    pe.wait_ge(w_staged, i - SLOTS + 1)
                nk = 8 // r
                for k in range(nk):
                    for q in range(r):
                        ins = nc.tensor.transpose(ring[:, i % SLOTS, (k * r + q) * P:(k * r + q + 1) * P],
                                                  raw[i % 3][:, q * nk * P + k * P:q * nk * P + (k + 1) * P], ident[:])
                ins.then_inc(w_turned, 1)
            pe.wait_ge(s_low, 1)
            pe.wait_ge(w_staged, len(CHUNKS))
            nc.tensor.transpose(ring[0:1, 0, 0:P], low[:, 0:1], ident[:]).then_inc(s_lowT, 1)
            pe.wait_ge(s_flag, 1)
            inexact = pe.value_load(flag[0:1, 0:1], min_val=0, max_val=1)
            pe.wait_ge(s_ready, 1)
            for free in slot_free:
                pe.sem_inc(free, 1)

            with pe.Fori(0, B) as b:
                def take(key):
                    u = turns[key]
                    pe.wait_ge(slot_free[u.slot], u.emptied(b))
                    return u.slot

                s = take("gates")
                pe.wait_ge(mod_ready, b + 1)
                for i, v in enumerate((2, 6, 5)):
                    for k in range(ND):
                        ins = nc.tensor.transpose(ring[:, s, i * D + k * P:i * D + (k + 1) * P],
                                                  mod[:, v * ND + k:v * ND + k + 1].broadcast_to([P, P]), ident[:])
                ins.then_inc(slot_full[s], 1)

                def turn_xn(key, n):
                    s = take(key)
                    pe.wait_ge(xn_ready, b * 2 + n)
                    for t in range(NT):
                        for k in range(ND):
                            ins = nc.tensor.transpose(ring[:, s, k * S + t * P:k * S + (t + 1) * P], xn[:, t, k * P:(k + 1) * P], ident[:])
                    ins.then_inc(slot_full[s], 1)

                turn_xn("hT", 1)

                def stacks(t):
                    for k in range(2):
                        s = take(("stack", t, k))
                        pe.wait_ge(lo_ready, b * 2 * NT + 2 * t + k + 1)
                        for p in range(NP):
                            ins = nc.tensor.transpose(ring[:, s, p * P:(p + 1) * P],
                                                      nat[k][t % 2][:, 2 * p:2 * p + 2, :].rearrange("p h g -> p (h g)").bitcast(F32), ident[:])
                        ins.then_inc(slot_full[s], 1)

                pe.wait_ge(slot_free[turns["hT"].slot], turns["hT"].freed(b))
                for t in range(NT):
                    s = take(("proj", t))
                    for o, w in ((0, 2 * D), (2 * D, D)):
                        for k in range(ND):
                            ins = nc.tensor.matmul(ring[:, s, o:o + w], hT[:, k, t * P:(t + 1) * P], wqkv[:, k, o:o + w], start=(k == 0), stop=(k == ND - 1))
                    ins.then_inc(slot_full[s], 1)
                    if t:
                        stacks(t - 1)
                stacks(NT - 1)
                for k in range(2):
                    u = turns["stack", NT - 1, k]
                    pe.wait_ge(slot_free[u.slot], u.freed(b))

                def rows_of(k, hd, lo, n):
                    return stack[k][(hd % 2) * G:(hd % 2 + 1) * G, hd // 2, lo:lo + n]

                for t in range(NT):
                    n_h, w = MAX_HEADS[t], (t + 1) * P
                    for g in range(MAX_UNITS[t]):
                        s = take(("max", t, g))
                        for q in range(2):
                            diag = ring[:, s, q * 512:q * 512 + n_h * w].rearrange("p (n q) -> p n q", q=w)[:, :, t * P:w]
                            nc.tensor.matmul(diag, identr[:], causalr[:, None, :].broadcast_to([P, n_h, P]),
                                             start=True, stop=False, skip_group_check=True)
                        for j in range(n_h):
                            for q in range(2):
                                hd = 2 * n_h * g + 2 * j + q
                                ins = nc.tensor.matmul(ring[:, s, q * 512 + j * w:q * 512 + (j + 1) * w], rows_of(0, hd, t * P, P), rows_of(1, hd, 0, w),
                                                       start=False, stop=(j == n_h - 1), skip_group_check=True)
                        ins.then_inc(slot_full[s], 1)
                s = take("maxT")
                u = turns["max", NT - 1, MAX_UNITS[NT - 1] - 1]
                pe.wait_ge(slot_free[u.slot], u.freed(b))
                for t in range(NT):
                    ins = nc.tensor.transpose(ring[0:NH, s, t * P:(t + 1) * P], negmax[:, t, :], ident[:])
                ins.then_inc(slot_full[s], 1)

                def scores(p):
                    for u in range(3):
                        s = take(("att", p, u))
                        for e, kb, o, _ in units[u]:
                            ins = nc.tensor.matmul(ring[:, s, o:o + S - kb * P], rows_of(1, 2 * p + e, kb * P, P),
                                                   rows_of(0, 2 * p + e, kb * P, S - kb * P), start=True, stop=True)
                        ins.then_inc(slot_full[s], 1)

                def values(p):
                    a = p // 2
                    pe.wait_ge(att_ready, b * 3 * NP + 3 * p + 3)
                    if p % 2 == 0 and a >= 2:
                        pe.wait_ge(sums_ready, b * (NP // 2) + a - 1)
                    at = {(e, kb): o for unit in units for e, kb, _, o in unit}
                    for kb in range(NT):
                        n = S - kb * P
                        for e in range(2):
                            j = 2 * (p % 2) + e
                            ins = nc.tensor.matmul(acc[VW * j:VW * j + HD + 1, a % 2, kb * P:S], va[:, kb, 2 * p + e, :],
                                                   probs[p % 2][:, at[e, kb]:at[e, kb] + n], start=(kb == 0),
                                                   stop=(kb == NT - 1), skip_group_check=True)
                    ins.then_inc(pv_done, 1)

                def heads_back(a):
                    s = take(("heads", a))
                    pe.wait_ge(sums_ready, b * (NP // 2) + a + 1)
                    for t in range(NT):
                        ins = nc.tensor.transpose(ring[:, s, t * P:(t + 1) * P], sums[a % 2][:, t * P:(t + 1) * P], ident[:])
                    ins.then_inc(slot_full[s], 1)

                pe.wait_ge(maxrow_ready, b * 32 + 33)
                for seq in range(NP + 2):
                    if seq < NP:
                        scores(seq)
                    if 1 <= seq <= NP:
                        values(seq - 1)
                    if seq >= 3 and seq % 2:
                        heads_back((seq - 3) // 2)

                s = take("oT")
                u = turns["heads", NP // 2 - 1]
                pe.wait_ge(slot_free[u.slot], u.freed(b))
                for k in range(ND):
                    for t in range(NT):
                        ins = nc.tensor.transpose(ring[:, s, k * S + t * P:k * S + (t + 1) * P], onat[:, t, k * P:(k + 1) * P], ident[:])
                ins.then_inc(slot_full[s], 1)
                s = take("out")
                pe.wait_ge(slot_free[turns["oT"].slot], turns["oT"].freed(b))
                for t in range(NT):
                    for k in range(ND):
                        ins = nc.tensor.matmul(ring[:, s, t * D:(t + 1) * D], oT[:, k, t * P:(t + 1) * P], wproj[:, k], start=(k == 0), stop=(k == ND - 1))
                ins.then_inc(slot_full[s], 1)
                turn_xn("xT", 2)

                def ffn(exact):
                    view = (lambda z: z) if exact else (lambda z: z.bitcast(F32))

                    def layer(dst, w, m, src, nk, ready):
                        for k in range(nk):
                            if ready is not None:
                                pe.wait_ge(ready, b * nk + k + 1)
                            for i in range(2):
                                ins = nc.tensor.matmul(dst, view(w[:, k, m * P:(m + 1) * P]), view(src[:, k, i]),
                                                       start=(k == 0 and i == 0), stop=(k == nk - 1 and i == 1))
                        return ins

                    for m in range(NHID):
                        s = take(("gate_up", m))
                        layer(ring[:, s, 0:S], w1T, m, h2r, ND, h2_ready if m == 0 else None)
                        layer(ring[:, s, S:2 * S], w2T, m, h2r, ND, None).then_inc(slot_full[s], 1)
                    for name, w, src, ready in (("h1", h1T, act_a, a_ready), ("h2", h2T, act_b, g1_ready)):
                        for m in range(NHID):
                            s = take((name, m))
                            layer(ring[:, s, 0:S], w, m, src, NHID, ready if m == 0 else None).then_inc(slot_full[s], 1)
                    s = take("w3")
                    pe.wait_ge(g2_ready, b * NHID + NHID)
                    for t in range(NT):
                        for k in range(NHID):
                            for i in range(2):
                                ins = nc.tensor.matmul(ring[:, s, t * D:(t + 1) * D], view(act_a[:, k, i, t * P:(t + 1) * P]), view(w3T[:, k]),
                                                       start=(k == 0 and i == 0), stop=(k == NHID - 1 and i == 1))
                    ins.then_inc(slot_full[s], 1)

                with pe.If(inexact == 0):
                    ffn(True)
                with pe.Else():
                    ffn(False)


STEPS1 = 51

_LAYER0 = ["L0_attn_x", "L0_attn_norm_w", "L0_attn_Wq", "L0_attn_Wk", "L0_attn_Wv", "L0_attn_Wqf", "L0_attn_Wkf", "L0_attn_Wout",
           "L0_ffn_W_r", "L0_ffn_W_k", "L0_ffn_W_v", "L0_ffn_mu_r", "L0_ffn_mu_k", "L0_c", "L0_wmod"]
_LAYER1 = ["L1_attn_w_qkv", "L1_attn_w_proj", "L1_attn_b_proj", "L1_ffn_w1_w", "L1_ffn_w1_s", "L1_ffn_w2_w", "L1_ffn_w2_s",
           "L1_ffn_h1_w", "L1_ffn_h1_s", "L1_ffn_h2_w", "L1_ffn_h2_s", "L1_ffn_w3_w", "L1_ffn_w3_s", "L1_c", "L1_wmod"]


def rope_table():
    f = np.float32
    inv = f(1.0) / f(10000.0) ** (np.arange(0, HD, 2, dtype=f) / f(HD))
    t = np.arange(S, dtype=f)[:, None] * inv[None, :]
    cos, sin = np.cos(t).astype(f), np.sin(t).astype(f)
    return np.stack([np.concatenate([cos, cos], 1), np.concatenate([-sin, sin], 1)])


def kernel(**inputs):
    import concourse.bacc as _bacc
    from concourse.bass_utils import run_bass_kernel_spmd as _run

    nc = _bacc.Bacc("TRN2", target_bir_lowering=False, num_devices=1)
    arrays = {f"in_{n}": np.ascontiguousarray(inputs[n]) for n in _LAYER0 + _LAYER1}
    arrays["in_rope"] = rope_table()
    ap = {n: nc.dram_tensor(n, a.shape, mybir.dt.from_np(a.dtype), kind="ExternalInput").ap() for n, a in arrays.items()}
    out = nc.dram_tensor("out", (B, S, D), F32, kind="ExternalOutput").ap()
    x_mid = nc.dram_tensor("x_mid", (B, S, D), F32, kind="Internal").ap()
    layer0(nc, *(ap[f"in_{n}"] for n in _LAYER0), x_mid)
    layer1(nc, x_mid, *(ap[f"in_{n}"] for n in _LAYER1), ap["in_rope"], out)
    return _run(nc, [arrays], core_ids=[0]).results[0]["out"]
```

```python
from contextlib import ExitStack

import numpy as np

import concourse.bass as bass
from concourse import mybir

F32 = mybir.dt.float32
F32R = mybir.dt.float32r
ALU = mybir.AluOpType
ACT = mybir.ActivationFunctionType
AX = mybir.AxisListType

P = 128
B = 8
S = 512
D = 256
NT = S // P
ND = D // P
NH = 16
HD = D // NH
NP = NH // 2
G = 64
WIN = 64
HID = 1024
NHID = HID // P
NMOD = 6
LN_EPS = 1e-5
RMS_EPS = 1e-6
LIN_EPS = 1e-6
NEG = -1e30
VW = 32
SLOTS = 3
BANKS = 2 * SLOTS
NARROW = ("lin", "win", "winmax", "att", "max", "maxT", "heads", "turn", "out", "last")


class Turn:

    def __init__(self, slot, nth):
        self.slot, self.nth, self.before = slot, nth, []

    def filled(self, b):
        return b * self.per_step + self.nth + 1

    def freed(self, b):
        return b * self.per_step + self.nth + 2

    def freed_in_step_before(self, b):
        return b * self.per_step + self.nth + 2 - self.per_step


CAUSAL = [[(0, 0, 0, 0)], [(1, 0, 0, 512)], [(0, 1, 0, 1024), (0, 3, 384, 1408)], [(1, 1, 0, 1792), (1, 3, 384, 2176)],
          [(0, 2, 0, 1536), (1, 2, 256, 2304)]]
CAUSAL_PARTS = (0, 0, 1, 1, 2)
DIAGONALS = ((1, 0, 512, 2), (3, 1024, 384, 4), (4, 1536, 768, 2))
WINDOW = [[(e, kb, o, 512 * e + o) for kb, o in ((0, 0), (1, 192), (3, 384))] for e in range(2)] + [
    [(e, 2, 192 * e, 1024 + 192 * e) for e in range(2)]]
WINDOW_PARTS = (0, 0, 1)


def weight_views(pair):
    last = pair[:, 1024:2560].rearrange("p (a q) -> p a q", a=2)[:, :, 512:768]
    return pair[:, 0:512], pair[:, 512:1024], pair[:, 1024:1536], pair[:, 1792:2304], last


def turns_of(order):
    assert len(set(order)) == len(order)
    turns, users, position = {}, [[] for _ in range(BANKS)], 0
    count = [0] * (SLOTS + BANKS)
    for key in order:
        narrow = key[0] in NARROW
        if not narrow:
            position = (position + 1) // 2 * 2
        first = position % BANKS
        slot = SLOTS + first if narrow else first // 2
        turns[key] = Turn(slot, count[slot])
        count[slot] += 1
        for bank in (first,) if narrow else (first, first + 1):
            users[bank].append(turns[key])
        position += 1 if narrow else 2
    for turn in turns.values():
        turn.per_step = count[turn.slot]
    for uses in users:
        for i, turn in enumerate(uses):
            last = (uses[i - 1], i > 0)
            if last not in turn.before:
                turn.before.append(last)
    return turns


def end_wait(eng, waits):
    eng.sem_inc(waits, 1)


def groups(nat):
    return nat.rearrange("p h (g d) -> p h g d", d=HD)


def heads(x):
    return x.rearrange("p (h d) -> p h d", d=HD)


def twice(x):
    return x.unsqueeze(2).broadcast_to([P, NH, 2, HD])


def modulation_setup(nc, eng, link, modT, sgn, mag):
    for v in (1, 4):
        a = modT[:, v * ND:(v + 1) * ND, :]
        link(nc.vector.tensor_scalar(a, a, 1.0, None, ALU.add))
    for v in (2, 5):
        a = modT[:, v * ND:(v + 1) * ND, :]
        link(nc.vector.tensor_scalar(sgn[:], a, 0.0, 2.0, ALU.is_ge, ALU.mult))
        link(nc.vector.tensor_scalar(mag[:], a, -1.0, None, ALU.mult))
        link(nc.vector.tensor_tensor(mag[:], a, mag[:], ALU.max))
        link(nc.vector.tensor_scalar(mag[:], mag[:], 0.25, None, ALU.max))
        link(nc.vector.scalar_tensor_tensor(a, sgn[:], -1.0, mag[:], ALU.add, ALU.mult))



def interleave(seq, units, beside, last_group):
    steps = []
    for i, unit in enumerate(units):
        steps.append(unit)
        if i == 2 and seq % 2 == 0 and seq >= 2:
            steps.append(("values", seq // 2 - 1))
        if beside:
            steps.append(beside.pop(0))
    steps += beside
    if seq >= 3 and seq % 2:
        steps.append(("heads", (seq - 3) // 2))
    if seq == 2 * last_group + 1:
        steps += [("values", last_group), ("heads", last_group)]
    return steps


def window_steps(seq):
    units = [("winmax", 0, g) for g in range(NH // 4)] + [("winmax", t, g) for t in range(1, NT) for g in range(NP)]
    return units[6 * seq:6 * seq + 6] + ([("maxT",)] if seq == NP - 3 else [])


def attention_layer0():
    steps = []
    for seq in range(2 * NP):
        units = [("lin", seq, u) for u in range(len(CAUSAL))] if seq < NP else [("win", seq - NP, u) for u in range(len(WINDOW))]
        steps += interleave(seq, units, window_steps(seq), NP - 1)
    return steps


def order_layer0():
    o = ["gates", "hT"]
    for t in range(NT):
        o.append(("proj", t))
        if t:
            o += [("stack", t - 1, k) for k in range(4)]
    o.append("v")
    o += [("stack", NT - 1, k) for k in range(4)]
    o += [step for step in attention_layer0() if step[0] != "values"]
    o += [("oT", 0), ("oT", 1), ("out", 0), ("out", 1), "xT", "r", "k", ("last", 0), ("last", 1)]
    return o


PARTS_LIN = 3 * NH // 4
PARTS = PARTS_LIN + 2 * NH // 4


def layer0(nc, x, norm_w, Wq, Wk, Wv, Wqf, Wkf, Wout, W_r, W_k, W_v, mu_r, mu_k, c, wmod, x_mid):
    turns = turns_of(order_layer0())
    with ExitStack() as ctx:
        def sb(name, shape, dt=F32):
            return ctx.enter_context(nc.sbuf_tensor("a_" + name, shape, dt))

        def sem(name):
            return ctx.enter_context(nc.semaphore("a_" + name))

        ring = ctx.enter_context(nc.psum_tensor("a_ring", [P, SLOTS, 1024], F32))
        acc = ctx.enter_context(nc.psum_tensor("a_acc", [P, 2, 512], F32))

        ident = sb("ident", [P, P])
        identr = sb("identr", [P, P], F32R)
        band = sb("band", [P, 192])
        bandT = sb("bandT", [P, 192])
        bandr = sb("bandr", [P, 192], F32R)
        bandTr = sb("bandTr", [P, 192], F32R)
        minus_half = sb("minus_half", [P, 4])
        wqk = sb("wqk", [P, ND, 2 * D])
        wqkf = sb("wqkf", [P, ND, 2 * D])
        wv = sb("wv", [P, ND, D])
        wout = sb("wout", [P, 2 * ND, D])
        wrT = sb("wrT", [P, ND, D])
        wkT = sb("wkT", [P, ND, D])
        wvT = sb("wvT", [P, ND, D])
        fold = sb("fold", [P, 2, P])
        normw = sb("normw", [P, ND])
        mu = sb("mu", [P, 2, ND])
        one_mu = sb("one_mu", [P, 2, ND])
        cT = sb("cT", [P, ND, B])
        cS = sb("cS", [P, ND, B])
        modT = sb("modT", [P, NMOD * ND, B])
        sgn = sb("sgn", [P, ND, B])
        mag = sb("mag", [P, ND, B])
        mod = sb("mod", [P, NMOD * ND])
        gates = sb("gates", [P, 4, D])
        xin = sb("xin", [P, NT, D])
        xn = sb("xn", [P, NT, D])
        h = sb("h", [P, NT, D])
        xg = sb("xg", [P, NT, D])
        tmp = sb("tmp", [P, NT, D])
        x1 = h
        sq = sb("sq", [P, D])
        stats = sb("stats", [P, NT, 6])
        meanvar = sb("meanvar", [P, NT, 2])
        vareps = sb("vareps", [P, NT])
        rstd = sb("rstd", [P, NT])
        sumsq = sb("sumsq", [P, NT])
        msq = sb("msq", [P, NT])
        rrms = sb("rrms", [P, NT])
        hT = tmp[:].rearrange("p t d -> p (t d)").rearrange("p (k s) -> p k s", k=ND)
        naturals = sb("naturals", [P, 8 * NH * G])
        nat = [[naturals[:, (2 * k + i) * NH * G:(2 * k + i + 1) * NH * G].rearrange("p (h g) -> p h g", g=G) for i in range(2)] for k in range(4)]
        stack = {k: sb(f"stack{k}", [P, NP, S], F32R) for k in (0, 2)}
        keys = {k: [sb(f"keys{k}_{e}", [P, NP, S], F32R) for e in range(2)] for k in (1, 3)}
        va = sb("va", [P, NT, NH, VW])
        negmax = sb("negmax", [P, NT, NH])
        work = sb("work", [P, 5120])
        probs = [work[:, 2560 * i:2560 * (i + 1)] for i in range(2)]
        wm = work[:, 0:ND * NMOD * D].rearrange("p (k n) -> p k n", k=ND)
        raw = work[:, 3072:3072 + 3 * ND * D].rearrange("p (i k n) -> p i k n", i=3, k=ND)
        mix = work[:, 0:2048].rearrange("p (i k s) -> p i k s", i=2, k=ND)
        kr = work[:, 2048:3072].rearrange("p (k s) -> p k s", k=ND)
        ka = work[:, 3072:4096].rearrange("p (k s) -> p k s", k=ND)
        rg = work[:, 4096:5120].rearrange("p (t d) -> p t d", t=NT)
        den = sb("den", [P, 2, NT, 4])
        rden = sb("rden", [P, 2, NT, 4])
        onat = naturals[:, 0:2048].rearrange("p (t d) -> p t d", t=NT)
        oT = naturals[:, 2048:4096].rearrange("p (k s) -> p k s", s=S)
        sums = [naturals[:, 4096 + S * i:4096 + S * (i + 1)] for i in range(2)]
        maxT = naturals[0:NH, 5632:5632 + S]
        xT = naturals[:, 6144:6144 + ND * (S + 2)].rearrange("p (k s) -> p k s", k=ND)
        turned = naturals[:, 5120:5632].rearrange("p (k n) -> p k n", k=ND)

        s_w = sem("weights_loaded")
        s_small = sem("small_loaded")
        s_const = sem("constants_ready")
        s_pool = sem("pool_setup_step")
        s_diag = sem("fold_blocks_zeroed")
        s_silu = sem("silu_c_ready")
        s_modp = sem("modulation_product")
        s_wt = sem("weights_turned")
        s_wr = sem("turned_weights_read")
        s_setup = sem("dve_setup_step")
        s_ready = sem("weights_ready")
        x_in = sem("x_loaded")
        xin_free = sem("x_used")
        slot_full = [sem(f"slot{i}_full") for i in range(SLOTS + BANKS)]
        slot_free = [sem(f"slot{i}_free") for i in range(SLOTS + BANKS)]
        dve_step = sem("dve_own_result")
        dve_waits = sem("dve_waits_met")
        pool_waits = sem("pool_waits_met")
        keys_half = sem("keys_first_half_copied")
        act_step = sem("act_own_result")
        pool_step = sem("pool_own_result")
        mod_ready = sem("mod_ready")
        var_ready = sem("var_ready")
        rstd_ready = sem("rstd_ready")
        h_ready = sem("h_ready")
        sumsq_ready = sem("sumsq_ready")
        hn_ready = sem("first_norm_ready")
        hT_ready = sem("hT_half_ready")
        xg_ready = sem("xg_ready")
        hi_ready = sem("hi_ready")
        lo_ready = sem("lo_ready")
        maxT_ready = sem("maxT_ready")
        maxrow_ready = sem("maxrow_in_stack")
        lin_ready = sem("lin_weights_masked")
        pv_done = sem("pair_products_done")
        sums_ready = sem("sums_copied")
        xn_ready = sem("xn_ready")
        xT_ready = sem("xT_ready")
        mix_ready = sem("mix_ready")
        kr_ready = sem("kr_ready")
        ka_ready = sem("ka_ready")
        spare_ready = sem("spare_columns_ready")
        zero_ready = sem("zero_token_ready")
        x2_ready = sem("x2_ready")
        x2_sent = sem("x2_sent")
        block = ctx.enter_context(nc.Block())

        x_v = x.rearrange("b (t p) d -> b p t d", p=P)
        out_v = x_mid.rearrange("b (t p) d -> b p t d", p=P)
        rows = "(k p) n -> p k n"

        def heads_of(o, a):
            return o[:, :, a * 4 * HD:(a + 1) * 4 * HD].rearrange("p t (h d) -> p t h d", d=HD)

        single = ring[:].rearrange("p s (a q) -> p (s a) q", a=2)

        def bank(slot):
            return single[:, slot - SLOTS]

        @block.sync
        def _(sp):
            for dst, src in ((wqk[:, :, 0:D], Wq.rearrange(rows, p=P)), (wqk[:, :, D:2 * D], Wk.rearrange(rows, p=P)),
                             (wv[:], Wv.rearrange(rows, p=P)), (wout[:], Wout.rearrange(rows, p=P)),
                             (raw[:, 0], W_r.rearrange(rows, p=P)), (raw[:, 1], W_k.rearrange(rows, p=P)),
                             (raw[:, 2], W_v.rearrange(rows, p=P)), (wm, wmod.rearrange(rows, p=P))):
                sp.dma_start(dst, src).then_inc(s_w, 16)
            for dst, src in ((normw[:], norm_w), (mu[:, 0], mu_r), (mu[:, 1], mu_k)):
                sp.dma_start(dst, src.rearrange("(k p) -> p k", p=P), allow_slow_non_contiguous=True).then_inc(s_small, 16)
            for k in range(ND):
                sp.dma_start(cT[:, k, :], c[:, k * P:(k + 1) * P].rearrange("b p -> p b"), allow_slow_non_contiguous=True).then_inc(s_small, 16)
            sp.wait_ge(s_diag, 1)
            for i, w in enumerate((Wqf, Wkf)):
                for e in range(P // HD):
                    sp.dma_start(fold[e * HD:(e + 1) * HD, i, e * HD:(e + 1) * HD], w).then_inc(s_small, 16)
            with sp.Fori(0, B) as b:
                sp.wait_ge(xin_free, b + 1)
                sp.dma_start(xin[:], x_v[b]).then_inc(x_in, 16)
                sp.wait_ge(maxT_ready, b + 1)
                for e in range(2):
                    sp.dma_start(stack[0][e * G + 3 * HD:e * G + 3 * HD + 1, :, :].bitcast(F32),
                                 maxT[e:NH:2, :]).then_inc(maxrow_ready, 16)

        @block.gpsimd
        def _(pool):
            n = [0]

            def link(ins):
                n[0] += 1
                ins.then_inc(s_pool, 1)
                pool.wait_ge(s_pool, n[0])

            nc.gpsimd.memset(fold[:], 0.0).then_inc(s_diag, 1)
            link(nc.gpsimd.memset(ident[:], 1.0))
            link(nc.gpsimd.affine_select(out=ident[:], in_=ident[:], compare_op=ALU.is_equal, fill=0.0, base=0,
                                         pattern=[[-1, P]], channel_multiplier=1))
            for m, base in ((band, WIN), (bandT, WIN)):
                link(nc.gpsimd.memset(m[:], 0.0))
                link(nc.gpsimd.affine_select(out=m[:], in_=m[:], compare_op=ALU.is_ge, fill=NEG, base=base,
                                             pattern=[[-1, 192]], channel_multiplier=1))
                link(nc.gpsimd.affine_select(out=m[:], in_=m[:], compare_op=ALU.is_ge, fill=NEG, base=0,
                                             pattern=[[1, 192]], channel_multiplier=-1))
            nc.gpsimd.memset(minus_half[:], -0.5)
            link(nc.gpsimd.memset(va[:], 0.0))
            nc.gpsimd.memset(va[:, :, :, HD:HD + 1], 1.0).then_inc(s_const, 1)
            pool.wait_ge(s_ready, 1)
            own = 2
            with pool.Fori(0, B) as b:
                pool.wait_ge(x2_ready, b * 2 + 1)
                end_wait(pool, pool_waits)
                for i in range(2):
                    for k in range(4):
                        nc.gpsimd.memset(nat[k][i][:, :, 3 * HD + (k == 1):G], 0.0)
                    ins = nc.gpsimd.memset(nat[1][i][:, :, 3 * HD:3 * HD + 1], 1.0)
                ins.then_inc(spare_ready, 1)
                pool.wait_ge(var_ready, b * 3 + 1)
                nc.gpsimd.tensor_tensor(rstd[:], vareps[:], minus_half[:], ALU.pow).then_inc(rstd_ready, 1)
                pool.wait_ge(var_ready, b * 3 + 2)
                nc.gpsimd.tensor_tensor(rrms[:], msq[:], minus_half[:], ALU.pow).then_inc(rstd_ready, 1)
                pool.wait_ge(h_ready, b + 1)
                nc.gpsimd.tensor_tensor(xg[:], h[:], gates[:, 2:3, :].broadcast_to([P, NT, D]), ALU.mult).then_inc(pool_step, 1)
                pool.wait_ge(pool_step, b * own + 1)
                pool.wait_ge(x_in, b * 16 + 16)
                nc.gpsimd.tensor_tensor(xg[:], xg[:], xin[:], ALU.add).then_inc(pool_step, 1)
                pool.wait_ge(pool_step, b * own + 2)
                pool.sem_inc(xg_ready, 1)
                pool.sem_inc(xin_free, 1)
                for p in range(NP):
                    for u, o, step, blocks in DIAGONALS:
                        v = turns["lin", p, u]
                        pb = probs[p % 2]
                        d = bass.AP(tensor=pb.tensor, offset=pb.offset + o, ap=[pb.ap[0], [step, blocks], [1, P]])
                        pool.wait_ge(slot_free[v.slot], v.freed(b))
                        end_wait(pool, pool_waits)
                        nc.gpsimd.affine_select(out=d, in_=d, compare_op=ALU.is_ge, fill=0.0, base=0,
                                                pattern=[[0, blocks], [1, P]],
                                                channel_multiplier=-1).then_inc(lin_ready, 1)
                nc.gpsimd.memset(xT[:, :, 0:1], 0.0).then_inc(zero_ready, 1)
                pool.wait_ge(var_ready, b * 3 + 3)
                nc.gpsimd.tensor_tensor(rstd[:], vareps[:], minus_half[:], ALU.pow).then_inc(rstd_ready, 1)

        @block.vector
        def _(dve):
            n = [0]

            def once(ins):
                n[0] += 1
                ins.then_inc(s_setup, 1)
                dve.wait_ge(s_setup, n[0])

            dve.wait_ge(s_const, 1)
            nc.vector.tensor_copy(identr[:], ident[:])
            nc.vector.tensor_copy(bandr[:], band[:])
            nc.vector.tensor_copy(bandTr[:], bandT[:])
            for k in (1, 3):
                for e in range(2):
                    once(nc.vector.memset(keys[k][e][(1 - e) * G:(2 - e) * G].bitcast(F32), 0.0))
            dve.wait_ge(s_small, 16 * (3 + ND + 2 * P // HD))
            once(nc.vector.tensor_scalar(one_mu[:], mu[:], -1.0, 1.0, ALU.mult, ALU.add))
            dve.wait_ge(s_modp, 1)
            once(nc.vector.tensor_copy(modT[:].rearrange("p v b -> p (v b)"), ring[:, 0, 0:NMOD * ND * B]))
            modulation_setup(nc, dve, once, modT, sgn, mag)
            dve.wait_ge(s_w, 16 * 8)
            for k in range(ND):
                once(nc.vector.tensor_scalar(wqk[:, k], wqk[:, k], normw[:, k:k + 1], None, ALU.mult))
                once(nc.vector.tensor_scalar(wv[:, k], wv[:, k], normw[:, k:k + 1], None, ALU.mult))
            dve.sem_inc(s_wr, 1)
            for i, w in enumerate((wrT, wkT, wvT)):
                dve.wait_ge(s_wt, i + 1)
                nc.vector.tensor_copy(w[:].rearrange("p k n -> p (k n)"), ring[:, 0, 0:512]).then_inc(s_wr, 1)
            for i in range(2):
                dve.wait_ge(s_wt, 4 + 2 * i)
                nc.vector.tensor_copy(turned.rearrange("p k n -> p (k n)"), ring[:, 0, 0:512]).then_inc(s_wr, 1)
                dve.wait_ge(s_wt, 5 + 2 * i)
                nc.vector.tensor_copy(wqkf[:, :, i * D:(i + 1) * D], ring[:, 0, 0:512].rearrange("p (k n) -> p k n", n=D)).then_inc(s_wr, 1)
            dve.wait_ge(s_wr, 8)
            dve.sem_inc(xin_free, 1)
            dve.sem_inc(maxrow_ready, 1)
            dve.sem_inc(x2_ready, 1)
            dve.sem_inc(s_ready, 1)

            n = [0]
            STEPS = 32
            with dve.Fori(0, B) as b:
                m = [0]

                def link(ins, before_aggregate=False):
                    m[0] += 1
                    ins.then_inc(dve_step, 1)
                    dve.wait_ge(dve_step, b * STEPS + m[0])
                    if before_aggregate:
                        end_wait(dve, dve_waits)

                def statistics(src, tiles):
                    for t in tiles:
                        ins = nc.vector.bn_stats(stats[:, t], src[:, t])
                    link(ins, before_aggregate=True)
                    for t in tiles:
                        ins = nc.vector.bn_aggr(meanvar[:, t], stats[:, t])
                    link(ins)

                def send_variance():
                    nc.vector.tensor_scalar(vareps[:], meanvar[:, :, 1], LN_EPS, None, ALU.add).then_inc(var_ready, 1)

                def gated(name, i, factor, base, dst):
                    u = turns[name, i]
                    half = slice(2 * i, 2 * i + 2)
                    dve.wait_ge(slot_full[u.slot], u.filled(b))
                    link(nc.vector.tensor_tensor(tmp[:, half], bank(u.slot).rearrange("p (t d) -> p t d", d=D), factor(half), ALU.mult))
                    dve.sem_inc(slot_free[u.slot], 1)
                    return nc.vector.tensor_tensor(dst[:, half], base[:, half], tmp[:, half], ALU.add)

                nc.vector.tensor_copy(mod[:], modT[:, :, b]).then_inc(mod_ready, 1)
                dve.wait_ge(x_in, b * 16 + 16)
                statistics(xin, range(NT))
                send_variance()
                dve.wait_ge(rstd_ready, b * 3 + 1)
                dve.wait_ge(x2_sent, b * 16 + 1)
                for t in range(NT):
                    nc.vector.tensor_scalar(xn[:, t], xin[:, t], meanvar[:, t, 0:1], rstd[:, t:t + 1], ALU.subtract, ALU.mult).then_inc(hn_ready, 1)
                dve.wait_ge(hn_ready, b * NT + NT)
                g = turns["gates"]
                dve.wait_ge(slot_full[g.slot], g.filled(b))
                nc.vector.tensor_copy(gates[:].rearrange("p v d -> p (v d)"), ring[:, g.slot]).then_inc(slot_free[g.slot], 1)
                dve.wait_ge(slot_free[g.slot], g.freed(b))
                link(nc.vector.tensor_tensor(h[:], xn[:], gates[:, 1:2, :].broadcast_to([P, NT, D]), ALU.mult))
                link(nc.vector.tensor_tensor(h[:], h[:], gates[:, 0:1, :].broadcast_to([P, NT, D]), ALU.add))
                dve.sem_inc(h_ready, 1)
                dve.wait_ge(sumsq_ready, b + 1)
                nc.vector.tensor_scalar(msq[:], sumsq[:], 1.0 / D, RMS_EPS, ALU.mult, ALU.add).then_inc(var_ready, 1)
                dve.wait_ge(rstd_ready, b * 3 + 2)

                def turn_copy(t, k):
                    u = turns["stack", t, k]
                    dve.wait_ge(slot_full[u.slot], u.filled(b))
                    nc.vector.tensor_copy(stack[k][:, :, t * P:(t + 1) * P],
                                          ring[:, u.slot].rearrange("p (n q) -> p n q", q=P)).then_inc(slot_free[u.slot], 1)

                for t in range(NT):
                    u = turns["proj", t]
                    for k in range(4):
                        dve.wait_ge(hi_ready, b * 4 * NT + 4 * t + (k | 1) + 1)
                        lo = 2 if k % 2 else 1
                        ins = nc.vector.scalar_tensor_tensor(groups(nat[k][t % 2])[:, :, lo, :].bitcast(F32R), heads(ring[:, u.slot, k * D:(k + 1) * D]),
                                                             rrms[:, t:t + 1], groups(nat[k][t % 2])[:, :, 0, :], ALU.mult, ALU.subtract)
                        if k == 3:
                            ins.then_inc(slot_free[u.slot], 1)
                        else:
                            ins.then_inc(lo_ready, 1)
                    if t:
                        turn_copy(t - 1, 0)
                        turn_copy(t - 1, 2)
                u = turns["v"]
                dve.wait_ge(slot_full[u.slot], u.filled(b))
                nc.vector.tensor_tensor(va[:, :, :, 0:HD], ring[:, u.slot].rearrange("p (t h d) -> p t h d", t=NT, d=HD),
                                        rrms[:].unsqueeze(2).unsqueeze(3).broadcast_to([P, NT, NH, HD]), ALU.mult).then_inc(slot_free[u.slot], 1)
                turn_copy(NT - 1, 0)
                turn_copy(NT - 1, 2)
                def maximum(key):
                    u = turns[key]
                    dve.wait_ge(slot_full[u.slot], u.filled(b))
                    if key[0] == "winmax":
                        t, g = key[1:]
                        w, n_h = (P, 4) if t == 0 else (192, 2)
                        src = bank(u.slot)[:, 0:n_h * w].rearrange("p (n q) -> p n q", q=w)
                        dst = negmax[:, t, n_h * g:n_h * (g + 1)]
                        nc.vector.tensor_reduce(dst, src, AX.X, ALU.max, negate=True).then_inc(slot_free[u.slot], 1)
                    else:
                        dve.wait_ge(maxrow_ready, b * 32 + 1)
                        link(nc.vector.tensor_copy(maxT.bitcast(F32R), bank(u.slot)[0:NH]))
                        dve.sem_inc(slot_free[u.slot], 1)
                        dve.sem_inc(maxT_ready, 1)

                def divide(a):
                    u = turns["heads", a]
                    src = bank(u.slot).rearrange("p (t h v) -> p t h v", t=NT, v=VW)
                    dve.wait_ge(slot_full[u.slot], u.filled(b))
                    if a < NP // 2:
                        link(nc.vector.tensor_scalar(den[:, a % 2], src[:, :, :, HD], LIN_EPS, None, ALU.add))
                        link(nc.vector.reciprocal(rden[:, a % 2], den[:, a % 2]))
                    else:
                        link(nc.vector.reciprocal(rden[:, a % 2], src[:, :, :, HD]))
                    nc.vector.tensor_tensor(heads_of(onat, a), src[:, :, :, 0:HD],
                                            rden[:, a % 2].unsqueeze(3).broadcast_to([P, NT, 4, HD]), ALU.mult).then_inc(slot_free[u.slot], 1)

                for step in attention_layer0():
                    if step[0] == "values":
                        a = step[1]
                        parts = 3 * (a + 1) if a < NP // 2 else PARTS_LIN + 2 * (a + 1 - NP // 2)
                        dve.wait_ge(pv_done, b * PARTS + parts)
                        nc.vector.tensor_copy(sums[a % 2], acc[:, a % 2, :]).then_inc(sums_ready, 1)
                    elif step[0] in ("winmax", "maxT"):
                        maximum(step)
                    elif step[0] == "heads":
                        divide(step[1])
                u = turns["oT", 1]
                dve.wait_ge(slot_full[u.slot], u.filled(b))
                nc.vector.tensor_copy(naturals[:, 3072:4096], ring[:, u.slot]).then_inc(slot_free[u.slot], 1)
                dve.wait_ge(xg_ready, b + 1)
                for i in range(2):
                    link(gated("out", i, lambda half: gates[:, 2:3, :].broadcast_to([P, 2, D]), xg, x1))
                    statistics(x1, (2 * i, 2 * i + 1))
                send_variance()
                dve.wait_ge(rstd_ready, b * 3 + 3)
                for t in range(NT):
                    nc.vector.tensor_scalar(xn[:, t], x1[:, t], meanvar[:, t, 0:1], rstd[:, t:t + 1], ALU.subtract, ALU.mult).then_inc(xn_ready, 1)
                for i in range(2):
                    for k in range(ND):
                        if i == 0 and k == 0:
                            dve.wait_ge(zero_ready, b + 1)
                            dve.wait_ge(xT_ready, b + 1)
                        if i == 0 and k == 1:
                            dve.wait_ge(slot_free[turns["xT"].slot], turns["xT"].freed(b))
                        link(nc.vector.tensor_scalar(mix[:, i, k], xT[:, k, 0:S], one_mu[:, i, k:k + 1], None, ALU.mult))
                        ins = nc.vector.scalar_tensor_tensor(mix[:, i, k], xT[:, k, 1:S + 1], mu[:, i, k:k + 1], mix[:, i, k], ALU.mult, ALU.add)
                        ins.then_inc(mix_ready, 1)
                for k in range(ND):
                    if k == 0:
                        dve.wait_ge(kr_ready, b + 1)
                    else:
                        dve.wait_ge(slot_free[turns["k"].slot], turns["k"].freed(b))
                    nc.vector.tensor_tensor(ka[:, k], kr[:, k], kr[:, k], ALU.mult).then_inc(ka_ready, 1)
                dve.wait_ge(slot_free[turns["r"].slot], turns["r"].freed(b))
                link(nc.vector.tensor_tensor(rg, rg, gates[:, 3:4, :].broadcast_to([P, NT, D]), ALU.mult))
                for i in range(2):
                    gated("last", i, lambda half: rg[:, half], x1, xn).then_inc(x2_ready, 1)
                assert m[0] == STEPS, m[0]

        @block.scalar
        def _(act):
            act.wait_ge(s_small, 16 * (3 + ND + 2 * P // HD))
            nc.scalar.activation(cS[:], cT[:], ACT.Silu).then_inc(s_silu, 1)
            act.wait_ge(s_ready, 1)
            act.sem_inc(x2_sent, 1)
            with act.Fori(0, B) as b:
                u = turns["hT"]
                act.wait_ge(slot_full[u.slot], u.filled(b))
                for k in range(ND):
                    nc.scalar.activation(hT[:, k], ring[:, u.slot, k * S:(k + 1) * S], ACT.Identity,
                                         bias=mod[:, k:k + 1], scale=mod[:, ND + k:ND + k + 1]).then_inc(slot_free[u.slot] if k else hT_ready, 1)
                act.wait_ge(h_ready, b + 1)
                for t in range(NT):
                    ins = nc.scalar.activation(sq[:], h[:, t], ACT.Square, accum_out=sumsq[:, t:t + 1])
                    if t < NT - 1:
                        ins.then_inc(act_step, 1)
                        act.wait_ge(act_step, b * (NT - 1) + t + 1)
                ins.then_inc(sumsq_ready, 1)

                def turn_copy(t, k):
                    u = turns["stack", t, k]
                    act.wait_ge(slot_full[u.slot], u.filled(b))
                    for e in range(2):
                        half = slice(e * G, (e + 1) * G)
                        nc.scalar.copy(keys[k][e][half, :, t * P:(t + 1) * P],
                                       ring[half, u.slot].rearrange("p (n q) -> p n q", q=P)).then_inc(slot_free[u.slot] if e else keys_half, 1)

                act.wait_ge(spare_ready, b + 1)
                for t in range(NT):
                    u = turns["proj", t]
                    act.wait_ge(slot_full[u.slot], u.filled(b))
                    if t == 0:
                        act.wait_ge(rstd_ready, b * 3 + 2)
                    for k in range(4):
                        g = groups(nat[k][t % 2])[:, :, 0:2, :] if k % 2 else groups(nat[k][t % 2])[:, :, 0:3:2, :]
                        if t >= 2:
                            v = turns["stack", t - 2, k]
                            act.wait_ge(slot_full[v.slot], v.filled(b))
                        nc.scalar.activation(g.bitcast(F32R), twice(heads(ring[:, u.slot, k * D:(k + 1) * D])), ACT.Copy, scale=rrms[:, t:t + 1]).then_inc(hi_ready, 1)
                    if t:
                        turn_copy(t - 1, 1)
                        turn_copy(t - 1, 3)
                turn_copy(NT - 1, 1)
                turn_copy(NT - 1, 3)
                for p in range(NP):
                    for i, weights in enumerate(weight_views(probs[p % 2])):
                        u = turns["lin", p, i]
                        act.wait_ge(slot_full[u.slot], u.filled(b))
                        if p >= 2:
                            act.wait_ge(pv_done, b * PARTS + 3 * (p // 2 - 1) + CAUSAL_PARTS[i] + 1)
                        nc.scalar.activation(weights, bank(u.slot) if i < 4 else bank(u.slot).rearrange("p (a q) -> p a q", a=2), ACT.Square, bias=1.0, scale=0.5).then_inc(slot_free[u.slot], 1)
                for p in range(NP):
                    for i, (o, w) in enumerate(((0, 512), (512, 512), (1024, 384))):
                        u = turns["win", p, i]
                        act.wait_ge(slot_full[u.slot], u.filled(b))
                        if p >= 2:
                            act.wait_ge(pv_done, b * PARTS + PARTS_LIN + 2 * (p // 2 - 1) + WINDOW_PARTS[i] + 1)
                        elif i == 0:
                            act.wait_ge(pv_done, b * PARTS + PARTS_LIN)
                        nc.scalar.activation(probs[p % 2][:, o:o + w], bank(u.slot)[:, 0:w], ACT.Exp, scale=float(HD) ** -0.5).then_inc(slot_free[u.slot], 1)
                u = turns["oT", 0]
                act.wait_ge(slot_full[u.slot], u.filled(b))
                nc.scalar.copy(naturals[:, 2048:3072], ring[:, u.slot]).then_inc(slot_free[u.slot], 1)
                u = turns["xT"]
                act.wait_ge(slot_full[u.slot], u.filled(b))
                for k in range(ND):
                    nc.scalar.activation(xT[:, k, 1:S + 1], ring[:, u.slot, k * S:(k + 1) * S], ACT.Identity,
                                         bias=mod[:, 3 * ND + k:3 * ND + k + 1], scale=mod[:, 4 * ND + k:4 * ND + k + 1]).then_inc(slot_free[u.slot] if k else xT_ready, 1)
                u = turns["r"]
                act.wait_ge(slot_full[u.slot], u.filled(b))
                nc.scalar.activation(work[:, 4096:5120], ring[:, u.slot], ACT.Sigmoid).then_inc(slot_free[u.slot], 1)
                u = turns["k"]
                act.wait_ge(slot_full[u.slot], u.filled(b))
                for k in range(ND):
                    nc.scalar.activation(kr[:, k], ring[:, u.slot, k * S:(k + 1) * S], ACT.Relu).then_inc(slot_free[u.slot] if k else kr_ready, 1)
                act.wait_ge(x2_ready, b * 2 + 3)
                act.dma_start(out_v[b], xn[:]).then_inc(x2_sent, 16)
            act.wait_ge(x2_sent, B * 16 + 1)

        @block.tensor
        def _(pe):
            pe.wait_ge(s_silu, 1)
            pe.wait_ge(s_w, 16 * 8)
            for j in range(NMOD * ND):
                for k in range(ND):
                    ins = nc.tensor.matmul(ring[:, 0, j * B:(j + 1) * B], wm[:, k, j * P:(j + 1) * P], cS[:, k], start=(k == 0), stop=(k == ND - 1))
            ins.then_inc(s_modp, 1)
            pe.wait_ge(s_const, 1)
            pe.wait_ge(s_small, 16 * (3 + ND + 2 * P // HD))
            for i in range(3):
                pe.wait_ge(s_wr, i + 1)
                for k in range(ND):
                    for r in range(ND):
                        ins = nc.tensor.transpose(ring[:, 0, k * D + r * P:k * D + (r + 1) * P], raw[:, i, r, k * P:(k + 1) * P], ident[:])
                ins.then_inc(s_wt, 1)
            for i in range(2):
                pe.wait_ge(s_wr, 4 + 2 * i)
                for k in range(ND):
                    for r in range(ND):
                        ins = nc.tensor.transpose(ring[:, 0, k * D + r * P:k * D + (r + 1) * P],
                                                  wqk[:, r, i * D + k * P:i * D + (k + 1) * P], ident[:])
                ins.then_inc(s_wt, 1)
                pe.wait_ge(s_wr, 5 + 2 * i)
                for r in range(ND):
                    for k in range(ND):
                        ins = nc.tensor.matmul(ring[:, 0, r * D + k * P:r * D + (k + 1) * P], turned[:, k, r * P:(r + 1) * P], fold[:, i], start=True, stop=True)
                ins.then_inc(s_wt, 1)
            pe.wait_ge(s_ready, 1)
            for free in slot_free:
                pe.sem_inc(free, 1)

            with pe.Fori(0, B) as b:
                def keep_clock(n):
                    for _ in range(n):
                        nc.tensor.matmul(acc[:, 0], identr[:], identr[:, None, :].broadcast_to([P, 4, P]), start=True, stop=True,
                                         skip_group_check=True)

                def take(key):
                    u = turns[key]
                    for last, in_this_step in u.before:
                        pe.wait_ge(slot_free[last.slot], last.freed(b) if in_this_step else last.freed_in_step_before(b))
                    return u.slot

                s = take("gates")
                pe.wait_ge(mod_ready, b + 1)
                for i, v in enumerate((0, 1, 2, 5)):
                    for k in range(ND):
                        ins = nc.tensor.transpose(ring[:, s, i * D + k * P:i * D + (k + 1) * P],
                                                  mod[:, v * ND + k:v * ND + k + 1].broadcast_to([P, P]), ident[:])
                ins.then_inc(slot_full[s], 1)
                keep_clock(10)
                s = take("hT")
                for t in range(NT):
                    pe.wait_ge(hn_ready, b * NT + t + 1)
                    for k in range(ND):
                        ins = nc.tensor.transpose(ring[:, s, k * S + t * P:k * S + (t + 1) * P], xn[:, t, k * P:(k + 1) * P], ident[:])
                ins.then_inc(slot_full[s], 1)

                def stacks(t):
                    for k in range(4):
                        s = take(("stack", t, k))
                        if k < 3:
                            pe.wait_ge(lo_ready, b * 3 * NT + 3 * t + k + 1)
                        else:
                            u = turns["proj", t]
                            pe.wait_ge(slot_free[u.slot], u.freed(b))
                        for p in range(NP):
                            ins = nc.tensor.transpose(ring[:, s, p * P:(p + 1) * P],
                                                      nat[k][t % 2][:, 2 * p:2 * p + 2, :].rearrange("p h g -> p (h g)"), ident[:])
                        ins.then_inc(slot_full[s], 1)

                keep_clock(4)
                pe.wait_ge(slot_free[turns["hT"].slot], turns["hT"].freed(b))
                for t in range(NT):
                    s = take(("proj", t))
                    for i, w in enumerate((wqk, wqkf)):
                        for k in range(ND):
                            ins = nc.tensor.matmul(ring[:, s, i * S:(i + 1) * S], hT[:, k, t * P:(t + 1) * P], w[:, k], start=(k == 0), stop=(k == ND - 1))
                    ins.then_inc(slot_full[s], 1)
                    if t:
                        stacks(t - 1)
                s = take("v")
                for t in range(NT):
                    for k in range(ND):
                        ins = nc.tensor.matmul(ring[:, s, t * D:(t + 1) * D], hT[:, k, t * P:(t + 1) * P], wv[:, k], start=(k == 0), stop=(k == ND - 1))
                ins.then_inc(slot_full[s], 1)
                stacks(NT - 1)
                for k in range(4):
                    u = turns["stack", NT - 1, k]
                    pe.wait_ge(slot_free[u.slot], u.freed(b))

                def queries(k, hd, lo, n):
                    return stack[k][:, hd // 2, lo:lo + n]

                def keys_of(k, hd, lo, n):
                    return keys[k][hd % 2][:, hd // 2, lo:lo + n]

                def winmax(key):
                    s = take(key)
                    t, g = key[1:]
                    n_h, lo, w = (4, WIN, P) if t == 0 else (2, 0, 192)
                    nc.tensor.matmul(bank(s)[:, 0:n_h * w], identr[:], bandr[:, None, lo:192].broadcast_to([P, n_h, w]),
                                     start=True, stop=False, skip_group_check=True)
                    for j in range(n_h):
                        ins = nc.tensor.matmul(bank(s)[:, j * w:(j + 1) * w], queries(0, n_h * g + j, t * P, P),
                                               keys_of(1, n_h * g + j, t * P + P - w, w), start=False, stop=(j == n_h - 1), skip_group_check=True)
                    ins.then_inc(slot_full[s], 1)

                def maxima_back():
                    s = take(("maxT",))
                    last = {turns[key].slot: turns[key] for seq in range(NP) for key in window_steps(seq) if key[0] == "winmax"}
                    for slot, u in last.items():
                        pe.wait_ge(slot_free[slot], u.freed(b))
                    for t in range(NT):
                        ins = nc.tensor.transpose(bank(s)[0:NH, t * P:(t + 1) * P], negmax[:, t, :], ident[:])
                    ins.then_inc(slot_full[s], 1)

                def scores(kind, p, u):
                    s = take((kind, p, u))
                    if kind == "lin":
                        for e, kb, o, _ in CAUSAL[u]:
                            ins = nc.tensor.matmul(bank(s)[:, o:o + S - kb * P], keys_of(3, 2 * p + e, kb * P, P),
                                                   queries(2, 2 * p + e, kb * P, S - kb * P), start=True, stop=True)
                    else:
                        if p == 0 and u == 0:
                            pe.wait_ge(maxrow_ready, b * 32 + 33)
                        nc.tensor.matmul(bank(s)[:, 0:384], identr[:], bandTr[:, None, :].broadcast_to([P, 2, 192]),
                                         start=True, stop=False, skip_group_check=True)
                        if u < 2:
                            nc.tensor.matmul(bank(s)[:, 384:512], identr[:], bandTr[:, 0:P], start=False, stop=False, skip_group_check=True)
                        for j, (e, kb, o, _) in enumerate(WINDOW[u]):
                            w = 192 if kb < NT - 1 else P
                            ins = nc.tensor.matmul(bank(s)[:, o:o + w], keys_of(1, 2 * p + e, kb * P, P), queries(0, 2 * p + e, kb * P, w),
                                                   start=False, stop=(j == len(WINDOW[u]) - 1), skip_group_check=True)
                    ins.then_inc(slot_full[s], 1)

                def values(a):
                    linear = a < NP // 2
                    first = a % (NP // 2) * 2
                    if linear:
                        pe.wait_ge(lin_ready, b * 3 * NP + 3 * (first + 2))
                    else:
                        v = turns["win", first + 1, 2]
                        pe.wait_ge(slot_free[v.slot], v.freed(b))
                    if a >= 2:
                        pe.wait_ge(sums_ready, b * NP + a - 1)
                    at = {(e, kb): o for unit in (CAUSAL if linear else WINDOW) for e, kb, _, o in unit}
                    for kb in (0, 1, 3, 2):
                        n = S - kb * P if linear else min(192, S - kb * P)
                        for j in range(4):
                            p, e = first + j // 2, j % 2
                            ins = nc.tensor.matmul(acc[VW * j:VW * (j + 1), a % 2, kb * P:kb * P + n], va[:, kb, 2 * p + e, :],
                                                   probs[p % 2][:, at[e, kb]:at[e, kb] + n], start=(kb == 0),
                                                   stop=(kb == 2), skip_group_check=True)
                        if kb > 1 or kb == 0 and linear:
                            ins.then_inc(pv_done, 1)

                def heads_back(a):
                    s = take(("heads", a))
                    pe.wait_ge(sums_ready, b * NP + a + 1)
                    for t in range(NT):
                        ins = nc.tensor.transpose(bank(s)[:, t * P:(t + 1) * P], sums[a % 2][:, t * P:(t + 1) * P], ident[:])
                    ins.then_inc(slot_full[s], 1)

                u = turns["v"]
                pe.wait_ge(slot_free[u.slot], u.freed(b))
                for step in attention_layer0():
                    if step[0] in ("lin", "win"):
                        scores(*step)
                    elif step[0] == "winmax":
                        winmax(step)
                    elif step[0] == "maxT":
                        maxima_back()
                    elif step[0] == "values":
                        values(step[1])
                    else:
                        heads_back(step[1])

                pe.wait_ge(slot_free[turns["heads", NP - 1].slot], turns["heads", NP - 1].freed(b))
                for i in range(2):
                    s = take(("oT", i))
                    for k in range(2):
                        for t in range(NT):
                            ins = nc.tensor.transpose(ring[:, s, k * S + t * P:k * S + (t + 1) * P], onat[:, t, (2 * i + k) * P:(2 * i + k + 1) * P], ident[:])
                    ins.then_inc(slot_full[s], 1)
                for i in range(2):
                    u = turns["oT", i]
                    pe.wait_ge(slot_free[u.slot], u.freed(b))
                for i in range(2):
                    s = take(("out", i))
                    for t in range(2):
                        for k in range(2 * ND):
                            ins = nc.tensor.matmul(bank(s)[:, t * D:(t + 1) * D], oT[:, k, (2 * i + t) * P:(2 * i + t + 1) * P], wout[:, k],
                                                   start=(k == 0), stop=(k == 2 * ND - 1))
                    ins.then_inc(slot_full[s], 1)
                keep_clock(14)
                s = take("xT")
                for t in range(NT):
                    pe.wait_ge(xn_ready, b * NT + t + 1)
                    for k in range(ND):
                        ins = nc.tensor.transpose(ring[:, s, k * S + t * P:k * S + (t + 1) * P], xn[:, t, k * P:(k + 1) * P], ident[:])
                ins.then_inc(slot_full[s], 1)
                keep_clock(8)
                s = take("r")
                pe.wait_ge(mix_ready, b * 2 * ND + ND)
                for t in range(NT):
                    for k in range(ND):
                        ins = nc.tensor.matmul(ring[:, s, t * D:(t + 1) * D], mix[:, 0, k, t * P:(t + 1) * P], wrT[:, k], start=(k == 0), stop=(k == ND - 1))
                ins.then_inc(slot_full[s], 1)
                s = take("k")
                pe.wait_ge(mix_ready, b * 2 * ND + 2 * ND)
                for d in range(ND):
                    for k in range(ND):
                        ins = nc.tensor.matmul(ring[:, s, d * S:(d + 1) * S], wkT[:, k, d * P:(d + 1) * P], mix[:, 1, k], start=(k == 0), stop=(k == ND - 1))
                ins.then_inc(slot_full[s], 1)
                pe.wait_ge(ka_ready, b * ND + ND)
                for i in range(2):
                    s = take(("last", i))
                    for t in range(2):
                        for k in range(ND):
                            ins = nc.tensor.matmul(bank(s)[:, t * D:(t + 1) * D], ka[:, k, (2 * i + t) * P:(2 * i + t + 1) * P], wvT[:, k],
                                                   start=(k == 0), stop=(k == ND - 1))
                    ins.then_inc(slot_full[s], 1)



def order_layer1():
    o = ["gates", "hT"]
    for t in range(NT):
        o.append(("proj", t))
        if t:
            o += [("stack", t - 1, k) for k in range(2)]
    o += [("stack", NT - 1, k) for k in range(2)]
    o += [step for step in attention_layer1() if step[0] != "values"]
    o += [("turn", 1), ("out", 1, 0), ("out", 1, 1), "xT"]
    for name in ("gate_up", "h1", "h2"):
        o += [(name, m) for m in range(NHID)]
    o += [("last", 0), ("last", 1)]
    return o


MAX_HEADS = (4, 2, 1, 1)
GROUPS = NH // 4


def attention_layer1():
    units = [("max", t, g, 4 * g + i) for g in range(GROUPS) for t in range(NT) for i in range(0, 4, MAX_HEADS[t])]
    per = len(units) // GROUPS
    lead = per + (per + 1) // 2
    steps = units[:per] + [("maxT", 0)] + units[per:lead]
    for seq in range(NP):
        beside = units[lead + seq * per // 2:lead + (seq + 1) * per // 2]
        if seq % 2 and seq < 2 * GROUPS - 2:
            beside.insert(0, ("maxT", (seq + 1) // 2))
        steps += interleave(seq, [("att", seq, u) for u in range(len(CAUSAL))], beside, NP // 2 - 1)
        if seq == NP - 3:
            steps.append(("turn", 0))
        if seq == NP - 2:
            steps += [("out", 0, 0), ("out", 0, 1)]
    return steps


CHUNKS = ([("w1", g, 4) for g in range(2)] + [("w2", g, 4) for g in range(2)]
          + [("h1", m, 1) for m in range(NHID)] + [("h2", m, 1) for m in range(NHID)] + [("w3", m, 1) for m in range(ND)])
LOW_BITS = 0xFFF


def layer1(nc, x_mid, w_qkv, w_proj, b_proj, w1_w, w1_s, w2_w, w2_s, h1_w, h1_s, h2_w, h2_s, w3_w, w3_s, c, wmod, rope, out):
    turns = turns_of(order_layer1())
    with ExitStack() as ctx:
        def sb(name, shape, dt=F32):
            return ctx.enter_context(nc.sbuf_tensor("b_" + name, shape, dt))

        def sem(name):
            return ctx.enter_context(nc.semaphore("b_" + name))

        ring = ctx.enter_context(nc.psum_tensor("b_ring", [P, SLOTS, 1024], F32))
        acc = ctx.enter_context(nc.psum_tensor("b_acc", [P, 2, 512], F32))

        ident = sb("ident", [P, P])
        identr = sb("identr", [P, P], F32R)
        causal = sb("causal", [P, P])
        causalr = sb("causalr", [P, P], F32R)
        minus_half = sb("minus_half", [P, 4])
        cossin = sb("cossin", [P, 2, NT, HD])
        wqkv = sb("wqkv", [P, ND, 3 * D])
        wproj = sb("wproj", [P, ND, D])
        w1T = sb("w1T", [P, ND, HID], F32R)
        w2T = sb("w2T", [P, ND, HID], F32R)
        h1T = sb("h1T", [P, NHID, HID], F32R)
        h2T = sb("h2T", [P, NHID, HID], F32R)
        w3T = sb("w3T", [P, NHID, D], F32R)
        s12 = sb("s12", [P, 4, NHID])
        s3b = sb("s3b", [P, 2, ND])
        modT = sb("modT", [P, (NMOD + 1) * ND, B])
        low = sb("low", [P, 2])
        lowT = sb("lowT", [1, P])
        flag = sb("flag", [1, 2], mybir.dt.int32)
        mod = sb("mod", [P, (NMOD + 1) * ND])
        gates = sb("gates", [P, 3, D])
        xin = sb("xin", [P, NT, D])
        x = sb("x", [P, NT, D])
        xn = sb("xn", [P, NT, D])
        tmp = sb("tmp", [P, NT, D])
        flat_tmp = tmp[:].rearrange("p t d -> p (t d)")
        flat_xn = xn[:].rearrange("p t d -> p (t d)")
        hT = flat_tmp.rearrange("p (k s) -> p k s", k=ND)
        onat = tmp
        sums = [flat_xn[:, S * i:S * (i + 1)] for i in range(2)]
        stats = sb("stats", [P, NT, 6])
        meanvar = sb("meanvar", [P, NT, 2])
        vareps = sb("vareps", [P, NT])
        rstd = sb("rstd", [P, NT])
        va = sb("va", [P, NT, NH, HD + 1])
        negmax = sb("negmax", [P, NT, NH])
        den = sb("den", [P, 2, NT, 4])
        rden = sb("rden", [P, 2, NT, 4])
        arena = sb("arena", [P, 16 * 1024], F32R)
        stack, *keys = (arena[:, 4096 * k:4096 * (k + 1)].rearrange("p (n s) -> p n s", n=NP) for k in range(3))
        nat = [[arena[:, 12288 + 1024 * (2 * k + i):12288 + 1024 * (2 * k + i + 1)].rearrange("p (h g) -> p h g", g=G) for i in range(2)] for k in range(2)]
        maxT = [arena[0:4, 12288 + S * i:12288 + S * (i + 1)] for i in range(2)]
        act_a = arena[:, 0:8192].rearrange("p (k i s) -> p k i s", k=NHID, i=2)
        act_b = arena[:, 8192:16384].rearrange("p (k i s) -> p k i s", k=NHID, i=2)
        h2r = arena[:, 8192:8192 + 2048].rearrange("p (k i s) -> p k i s", k=ND, i=2)
        work = sb("work", [P, 5120])
        probs = [work[:, 2560 * i:2560 * (i + 1)] for i in range(2)]
        qk = [work[:, 2048 * i:2048 * i + 512] for i in range(2)]
        qk_cos = [work[:, 2048 * i + 512:2048 * i + 1024] for i in range(2)]
        qk_sin = [work[:, 2048 * i + 1024:2048 * i + 1536] for i in range(2)]
        qk_rot = [work[:, 2048 * i + 1536:2048 * i + 2048] for i in range(2)]
        oT = (xin[:].rearrange("p t d -> p (t d)")[:, 0:S], work[:, 0:S])
        hfull = work[:, 1024:2048].rearrange("p (k s) -> p k s", k=ND)
        silu = [work[:, 2048 + 512 * i:2560 + 512 * i] for i in range(2)]
        full = [work[:, 3072 + 512 * i:3584 + 512 * i] for i in range(4)]
        wm = work[:, 0:ND * NMOD * D].rearrange("p (k n) -> p k n", k=ND)
        raw = [work[:, 1024 * i:1024 * (i + 1)] for i in range(3)]
        staged = [work[:, 3072 + 1024 * i:3072 + 1024 * (i + 1)] for i in range(2)]
        lows = flat_tmp
        sgn, mag, cT, cS = (flat_xn[:, 16 * i:16 * (i + 1)].rearrange("p (k b) -> p k b", k=ND) for i in range(4))

        s_w = sem("weights_loaded")
        s_small = sem("small_loaded")
        s_const = sem("constants_ready")
        s_pool = sem("pool_setup_step")
        s_silu = sem("silu_c_ready")
        s_modp = sem("modulation_product")
        raw_loaded = [sem(f"raw_weights{i}_loaded") for i in range(3)]
        w_turned = sem("weights_turned")
        w_staged = sem("weights_staged")
        w_checked = sem("low_bits_collected")
        w_placed = [sem(f"staged{i}_placed") for i in range(2)]
        s_low = sem("low_bits_reduced")
        s_lowT = sem("low_bits_turned")
        s_flag = sem("flag_ready")
        s_setup = sem("dve_setup_step")
        s_ready = sem("weights_ready")
        x_in = sem("x_loaded")
        xin_free = sem("x_used")
        slot_full = [sem(f"slot{i}_full") for i in range(SLOTS + BANKS)]
        slot_free = [sem(f"slot{i}_free") for i in range(SLOTS + BANKS)]
        dve_step = sem("dve_own_result")
        dve_waits = sem("dve_waits_met")
        pool_waits = sem("pool_waits_met")
        keys_half = sem("keys_first_half_copied")
        pool_step = sem("pool_own_result")
        mod_ready = sem("mod_ready")
        var_ready = sem("var_ready")
        rstd_ready = sem("rstd_ready")
        gates_ready = sem("gates_ready")
        xg_ready = sem("x_plus_bias_ready")
        spare_ready = sem("spare_columns_ready")
        keys_zeroed = sem("other_heads_keys_zeroed")
        xn_ready = sem("xn_ready")
        hT_ready = sem("hT_half_ready")
        qk_ready = sem("qk_copied")
        rot_ready = sem("qk_rotated")
        hi_ready = sem("hi_ready")
        lo_ready = sem("lo_ready")
        maxT_ready = sem("maxT_ready")
        maxrow_ready = [sem(f"maxrow{i}_in_stack") for i in range(2)]
        att_ready = sem("weights_masked")
        pv_done = sem("pair_products_done")
        sums_ready = sem("sums_copied")
        h2_full = sem("ffn_input_half_ready")
        h2_ready = sem("ffn_input_split")
        silu_ready = sem("silu_ready")
        a_ready = sem("gated_split")
        g1_ready = sem("first_gelu_split")
        g2_ready = sem("second_gelu_split")
        x_done = sem("x_result_ready")
        x_sent = sem("x_result_sent")
        block = ctx.enter_context(nc.Block())

        x_v = x_mid.rearrange("b (t p) d -> b p t d", p=P)
        out_v = out.rearrange("b (t p) d -> b p t d", p=P)
        rows = "(k p) n -> p k n"
        weight = {"w1": w1_w, "w2": w2_w, "h1": h1_w, "h2": h2_w, "w3": w3_w}
        turned = {"w1": w1T, "w2": w2T, "h1": h1T, "h2": h2T, "w3": w3T}

        def heads_of(o, a):
            return o[:, :, a * 4 * HD:(a + 1) * 4 * HD].rearrange("p t (h d) -> p t h d", d=HD)

        single = ring[:].rearrange("p s (a q) -> p (s a) q", a=2)

        def bank(slot):
            return single[:, slot - SLOTS]

        @block.sync
        def _(sp):
            for dst, src in ((wqkv[:], w_qkv.rearrange(rows, p=P)), (wproj[:], w_proj.rearrange(rows, p=P)),
                             (wm, wmod.rearrange(rows, p=P)),
                             (cossin[:, 0], rope[0].rearrange("(t p) d -> p t d", p=P)),
                             (cossin[:, 1], rope[1].rearrange("(t p) d -> p t d", p=P))):
                sp.dma_start(dst, src).then_inc(s_w, 16)
            for dst, src in ((s12[:, 0], w1_s), (s12[:, 1], w2_s), (s12[:, 2], h1_s), (s12[:, 3], h2_s),
                             (s3b[:, 0], w3_s), (s3b[:, 1], b_proj)):
                sp.dma_start(dst, src.rearrange("(k p) -> p k", p=P), allow_slow_non_contiguous=True).then_inc(s_small, 16)
            for k in range(ND):
                sp.dma_start(cT[:, k, :], c[:, k * P:(k + 1) * P].rearrange("b p -> p b"), allow_slow_non_contiguous=True).then_inc(s_small, 16)
            sp.wait_ge(s_modp, 1)

            def load(i):
                name, m, r = CHUNKS[i]
                w = weight[name]
                if r == 1:
                    sp.dma_start(raw[i % 3], w[m * P:(m + 1) * P, :]).then_inc(raw_loaded[i % 3], 16)
                else:
                    sp.dma_start(raw[i % 3].rearrange("p (m n) -> p m n", m=r),
                                 w[m * r * P:(m + 1) * r * P, :].rearrange("(m p) n -> p m n", p=P)).then_inc(raw_loaded[i % 3], 16)

            for i in range(3):
                load(i)
            for i, (name, m, r) in enumerate(CHUNKS):
                sp.wait_ge(w_staged, i + 1)
                k = 8 // r
                sp.dma_start(turned[name][:, :, m * r * P:(m + 1) * r * P].bitcast(F32),
                             staged[i % 2].rearrange("p (k n) -> p k n", k=k)).then_inc(w_placed[i % 2], 16)
                if i + 3 < len(CHUNKS):
                    sp.wait_ge(w_turned, i + 1)
                    sp.wait_ge(w_checked, i + 1)
                    load(i + 3)
            with sp.Fori(0, B) as b:
                sp.wait_ge(xin_free, b + 1)
                sp.dma_start(xin[:], x_v[b]).then_inc(x_in, 16)
                for g in range(GROUPS):
                    sp.wait_ge(maxT_ready, b * GROUPS + g + 1)
                    for e in range(2):
                        sp.dma_start(stack[e * G + 3 * HD:e * G + 3 * HD + 1, 2 * g:2 * g + 2, :].bitcast(F32),
                                     maxT[g % 2][e:4:2, :].bitcast(F32)).then_inc(maxrow_ready[g % 2], 16)

        @block.gpsimd
        def _(pool):
            n = [0]

            def link(ins):
                n[0] += 1
                ins.then_inc(s_pool, 1)
                pool.wait_ge(s_pool, n[0])

            link(nc.gpsimd.memset(ident[:], 1.0))
            link(nc.gpsimd.affine_select(out=ident[:], in_=ident[:], compare_op=ALU.is_equal, fill=0.0, base=0,
                                         pattern=[[-1, P]], channel_multiplier=1))
            link(nc.gpsimd.memset(causal[:], 0.0))
            link(nc.gpsimd.affine_select(out=causal[:], in_=causal[:], compare_op=ALU.is_ge, fill=NEG, base=0,
                                         pattern=[[-1, P]], channel_multiplier=1))
            nc.gpsimd.memset(minus_half[:], -0.5)
            nc.gpsimd.memset(va[:, :, :, HD:HD + 1], 1.0).then_inc(s_const, 1)
            pool.wait_ge(s_ready, 1)
            own = 4
            with pool.Fori(0, B) as b:
                pool.wait_ge(x_done, b * 2 + 1)
                end_wait(pool, pool_waits)
                for i in range(2):
                    nc.gpsimd.memset(nat[0][i][:, :, 3 * HD:G].bitcast(F32), 0.0)
                    nc.gpsimd.memset(nat[1][i][:, :, 3 * HD + 1:G].bitcast(F32), 0.0)
                    ins = nc.gpsimd.memset(nat[1][i][:, :, 3 * HD:3 * HD + 1].bitcast(F32), 1.0)
                ins.then_inc(pool_step, 1)
                pool.wait_ge(pool_step, b * own + 1)
                pool.sem_inc(spare_ready, 1)
                pool.wait_ge(var_ready, b * 2 + 1)
                nc.gpsimd.tensor_tensor(rstd[:], vareps[:], minus_half[:], ALU.pow).then_inc(rstd_ready, 1)
                pool.wait_ge(rstd_ready, b * 2 + 1)
                end_wait(pool, pool_waits)
                for e in range(2):
                    if e:
                        ins.then_inc(pool_step, 1)
                        pool.wait_ge(pool_step, b * own + 2)
                        end_wait(pool, pool_waits)
                    ins = nc.gpsimd.memset(keys[e][(1 - e) * G:(2 - e) * G].bitcast(F32), 0.0)
                ins.then_inc(pool_step, 1)
                pool.wait_ge(pool_step, b * own + 3)
                pool.sem_inc(keys_zeroed, 1)
                pool.wait_ge(gates_ready, b + 1)
                pool.wait_ge(x_in, b * 16 + 16)
                nc.gpsimd.tensor_tensor(x[:], xin[:], gates[:, 1:2, :].broadcast_to([P, NT, D]), ALU.add).then_inc(pool_step, 1)
                pool.wait_ge(pool_step, b * own + 4)
                pool.sem_inc(xg_ready, 1)
                for p in range(NP):
                    for u, o, step, blocks in DIAGONALS:
                        v = turns["att", p, u]
                        pb = probs[p % 2]
                        d = bass.AP(tensor=pb.tensor, offset=pb.offset + o, ap=[pb.ap[0], [step, blocks], [1, P]])
                        pool.wait_ge(slot_free[v.slot], v.freed(b))
                        end_wait(pool, pool_waits)
                        nc.gpsimd.affine_select(out=d, in_=d, compare_op=ALU.is_ge, fill=0.0, base=0,
                                                pattern=[[0, blocks], [1, P]],
                                                channel_multiplier=-1).then_inc(att_ready, 1)
                pool.wait_ge(var_ready, b * 2 + 2)
                nc.gpsimd.tensor_tensor(rstd[:], vareps[:], minus_half[:], ALU.pow).then_inc(rstd_ready, 1)

        @block.vector
        def _(dve):
            n = [0]

            def once(ins):
                n[0] += 1
                ins.then_inc(s_setup, 1)
                dve.wait_ge(s_setup, n[0])

            dve.wait_ge(s_const, 1)
            nc.vector.tensor_copy(identr[:], ident[:])
            nc.vector.tensor_copy(causalr[:], causal[:])
            nc.vector.memset(acc[:], 0.0)
            once(nc.vector.memset(lows, 0.0))
            dve.wait_ge(s_small, 16 * (6 + ND))
            dve.wait_ge(s_modp, 1)
            once(nc.vector.tensor_copy(modT[:, 0:NMOD * ND].rearrange("p v b -> p (v b)"), ring[:, 0, 0:NMOD * ND * B]))
            modulation_setup(nc, dve, once, modT, sgn, mag)
            for k in range(ND):
                once(nc.vector.tensor_scalar(modT[:, NMOD * ND + k], modT[:, 2 * ND + k], s3b[:, 1, k:k + 1], None, ALU.mult))
                once(nc.vector.tensor_scalar(modT[:, 5 * ND + k], modT[:, 5 * ND + k], s3b[:, 0, k:k + 1], None, ALU.mult))
            I32 = mybir.dt.int32
            for i in range(len(CHUNKS)):
                dve.wait_ge(raw_loaded[i % 3], 16 * (i // 3 + 1))
                if i:
                    dve.wait_ge(w_checked, i)
                nc.vector.scalar_tensor_tensor(lows.bitcast(I32), raw[i % 3].bitcast(I32), LOW_BITS, lows.bitcast(I32),
                                               ALU.bitwise_and, ALU.bitwise_or).then_inc(w_checked, 1)
            dve.wait_ge(w_checked, len(CHUNKS))
            nc.vector.tensor_reduce(low[:, 0:1], lows.bitcast(I32), AX.X, ALU.max).then_inc(s_low, 1)
            dve.wait_ge(s_lowT, 1)
            once(nc.vector.tensor_reduce(lowT[:, 0:1], ring[0:1, 0, 0:P], AX.X, ALU.max))
            nc.vector.tensor_scalar(flag[:, 0:1], lowT[:, 0:1], 0.0, None, ALU.is_gt).then_inc(s_flag, 1)
            for i in range(2):
                dve.wait_ge(w_placed[i], 16 * len(CHUNKS) // 2)
            dve.wait_ge(s_w, 16 * 5)
            dve.wait_ge(s_flag, 1)
            dve.sem_inc(xin_free, 1)
            for i in range(2):
                dve.sem_inc(maxrow_ready[i], 1)
            dve.sem_inc(x_done, 1)
            dve.sem_inc(s_ready, 1)

            STEPS = 63
            with dve.Fori(0, B) as b:
                m = [0]

                def link(ins, before_aggregate=False):
                    m[0] += 1
                    ins.then_inc(dve_step, 1)
                    dve.wait_ge(dve_step, b * STEPS + m[0])
                    if before_aggregate:
                        end_wait(dve, dve_waits)

                def statistics(src, tiles):
                    for t in tiles:
                        ins = nc.vector.bn_stats(stats[:, t], src[:, t])
                    link(ins, before_aggregate=True)
                    for t in tiles:
                        ins = nc.vector.bn_aggr(meanvar[:, t], stats[:, t])
                    link(ins)

                def normalise(src, k):
                    nc.vector.tensor_scalar(vareps[:], meanvar[:, :, 1], LN_EPS, None, ALU.add).then_inc(var_ready, 1)
                    dve.wait_ge(rstd_ready, b * 2 + k)
                    if k == 1:
                        dve.wait_ge(x_sent, b * 16 + 1)
                    for t in range(NT):
                        nc.vector.tensor_scalar(xn[:, t], src[:, t], meanvar[:, t, 0:1], rstd[:, t:t + 1], ALU.subtract, ALU.mult).then_inc(xn_ready, 1)

                def gated(key, i, factor, base, dst, product=None):
                    u = turns[key]
                    half = slice(2 * i, 2 * i + 2)
                    product = tmp[:, half] if product is None else product
                    dve.wait_ge(slot_full[u.slot], u.filled(b))
                    link(nc.vector.tensor_tensor(product, bank(u.slot).rearrange("p (t d) -> p t d", d=D), factor(half), ALU.mult))
                    dve.sem_inc(slot_free[u.slot], 1)
                    return nc.vector.tensor_tensor(dst[:, half], base[:, half], product, ALU.add)

                nc.vector.tensor_copy(mod[:], modT[:, :, b]).then_inc(mod_ready, 1)
                dve.wait_ge(x_in, b * 16 + 16)
                statistics(xin, range(NT))
                normalise(xin, 1)
                dve.wait_ge(xn_ready, b * 2 * NT + NT)
                g = turns["gates"]
                dve.wait_ge(slot_full[g.slot], g.filled(b))
                link(nc.vector.tensor_copy(gates[:].rearrange("p v d -> p (v d)"), ring[:, g.slot, 0:3 * D]))
                dve.sem_inc(slot_free[g.slot], 1)
                dve.sem_inc(gates_ready, 1)

                def turn_copy(t, k):
                    u = turns["stack", t, k]
                    dve.wait_ge(slot_full[u.slot], u.filled(b))
                    nc.vector.tensor_copy(stack[:, :, t * P:(t + 1) * P],
                                          ring[:, u.slot].rearrange("p (n q) -> p n q", q=P)).then_inc(slot_free[u.slot], 1)

                for t in range(NT):
                    i = t % 2
                    h32 = "p (h d) -> p h d"
                    src, a, s, r = (z[i].rearrange(h32, d=HD) for z in (qk, qk_cos, qk_sin, qk_rot))
                    half = HD // 2
                    dve.wait_ge(qk_ready, b * NT + t + 1)
                    nc.vector.tensor_tensor(a, src, cossin[:, 0, t:t + 1, :].broadcast_to([P, 2 * NH, HD]), ALU.mult)
                    nc.vector.tensor_tensor(s[:, :, 0:half], src[:, :, half:HD], cossin[:, 1, t:t + 1, 0:half].broadcast_to([P, 2 * NH, half]), ALU.mult)
                    link(nc.vector.tensor_tensor(s[:, :, half:HD], src[:, :, 0:half], cossin[:, 1, t:t + 1, half:HD].broadcast_to([P, 2 * NH, half]), ALU.mult))
                    nc.vector.tensor_tensor(r, a, s, ALU.add).then_inc(rot_ready, 1)
                    for k in range(2):
                        dve.wait_ge(hi_ready, b * 2 * NT + 2 * t + k + 1)
                        lo = 2 if k % 2 else 1
                        nc.vector.tensor_tensor(groups(nat[k][i])[:, :, lo, :], r[:, k * NH:(k + 1) * NH],
                                                groups(nat[k][i])[:, :, 0, :].bitcast(F32), ALU.subtract).then_inc(lo_ready, 1)
                    if t:
                        turn_copy(t - 1, 0)
                turn_copy(NT - 1, 0)
                def maximum(key):
                    u = turns[key]
                    dve.wait_ge(slot_full[u.slot], u.filled(b))
                    if key[0] == "max":
                        t, g, hd = key[1:]
                        n_h, w = MAX_HEADS[t], (t + 1) * P
                        src = bank(u.slot)[:, 0:n_h * w].rearrange("p (n q) -> p n q", q=w)
                        dst = negmax[:, t, hd:hd + n_h]
                        nc.vector.tensor_reduce(dst, src, AX.X, ALU.max, negate=True).then_inc(slot_free[u.slot], 1)
                    else:
                        g = key[1]
                        dve.wait_ge(maxrow_ready[g % 2], b * 16 * GROUPS + 32 * (g // 2) + 1)
                        link(nc.vector.tensor_copy(maxT[g % 2], bank(u.slot)[0:4]))
                        dve.sem_inc(slot_free[u.slot], 1)
                        dve.sem_inc(maxT_ready, 1)

                for step in attention_layer1():
                    if step[0] == "values":
                        a = step[1]
                        dve.wait_ge(pv_done, b * PARTS_LIN + 3 * (a + 1))
                        nc.vector.tensor_copy(sums[a % 2], acc[:, a % 2, :]).then_inc(sums_ready, 1)
                    elif step[0] in ("max", "maxT"):
                        maximum(step)
                    elif step[0] == "heads":
                        a = step[1]
                        u = turns["heads", a]
                        src = bank(u.slot).rearrange("p (t h v) -> p t h v", t=NT, v=VW)
                        dve.wait_ge(slot_full[u.slot], u.filled(b))
                        link(nc.vector.reciprocal(rden[:, a % 2], src[:, :, :, HD]))
                        nc.vector.tensor_tensor(heads_of(onat, a), src[:, :, :, 0:HD],
                                                rden[:, a % 2].unsqueeze(3).broadcast_to([P, NT, 4, HD]), ALU.mult).then_inc(slot_free[u.slot], 1)
                    elif step[0] == "turn":
                        u = turns[step]
                        if step[1] == 0:
                            dve.wait_ge(xg_ready, b + 1)
                        dve.wait_ge(slot_full[u.slot], u.filled(b))
                        nc.vector.tensor_copy(oT[0], bank(u.slot)).then_inc(slot_free[u.slot], 1)
                    elif step[0] == "out":
                        link(gated(step, step[2], lambda half: gates[:, 0:1, :].broadcast_to([P, 2, D]), x, x, xin[:, 2:4]))
                        if step[2] == 1:
                            dve.sem_inc(xin_free, 1)
                for i in range(2):
                    link(gated(("out", 1, i), i, lambda half: gates[:, 0:1, :].broadcast_to([P, 2, D]), x, x))
                    statistics(x, (2 * i, 2 * i + 1))
                normalise(x, 2)
                for k in range(ND):
                    if k == 0:
                        dve.wait_ge(h2_full, b + 1)
                    else:
                        dve.wait_ge(slot_free[turns["xT"].slot], turns["xT"].freed(b))
                    link(nc.vector.tensor_copy(h2r[:, k, 0], hfull[:, k]))
                    nc.vector.tensor_tensor(h2r[:, k, 1], hfull[:, k], h2r[:, k, 0].bitcast(F32), ALU.subtract).then_inc(h2_ready, 1)
                for i in range(NHID):
                    u = turns["gate_up", i]
                    dve.wait_ge(silu_ready, b * NHID + i + 1)
                    if i >= 4:
                        dve.wait_ge(a_ready, b * NHID + i - 3)
                    link(nc.vector.scalar_tensor_tensor(full[i % 4], ring[:, u.slot, S:2 * S], s12[:, 1, i:i + 1], silu[i % 2], ALU.mult, ALU.mult))
                    dve.sem_inc(slot_free[u.slot], 1)
                    link(nc.vector.tensor_copy(act_a[:, i, 0], full[i % 4]))
                    nc.vector.tensor_tensor(act_a[:, i, 1], full[i % 4], act_a[:, i, 0].bitcast(F32), ALU.subtract).then_inc(a_ready, 1)
                for name, dst, ready in (("h1", act_b, g1_ready), ("h2", act_a, g2_ready)):
                    for i in range(NHID):
                        u = turns[name, i]
                        dve.wait_ge(slot_free[u.slot], u.freed(b))
                        link(nc.vector.tensor_copy(dst[:, i, 0], full[i % 4]))
                        nc.vector.tensor_tensor(dst[:, i, 1], full[i % 4], dst[:, i, 0].bitcast(F32), ALU.subtract).then_inc(ready, 1)
                for i in range(2):
                    gated(("last", i), i, lambda half: gates[:, 2:3, :].broadcast_to([P, 2, D]), x, xn).then_inc(x_done, 1)
                assert m[0] == STEPS, m[0]

        @block.scalar
        def _(act):
            act.wait_ge(s_small, 16 * (6 + ND))
            nc.scalar.activation(cS[:], cT[:], ACT.Silu).then_inc(s_silu, 1)
            for i in range(len(CHUNKS)):
                act.wait_ge(w_turned, i + 1)
                if i >= 2:
                    act.wait_ge(w_placed[i % 2], 16 * (i // 2))
                nc.scalar.copy(staged[i % 2], ring[:, i % SLOTS]).then_inc(w_staged, 1)
            act.wait_ge(s_ready, 1)
            act.sem_inc(x_sent, 1)
            with act.Fori(0, B) as b:
                u = turns["hT"]
                act.wait_ge(slot_full[u.slot], u.filled(b))
                for k in range(ND):
                    nc.scalar.activation(hT[:, k], ring[:, u.slot, k * S:(k + 1) * S], ACT.Identity,
                                         bias=mod[:, k:k + 1], scale=mod[:, ND + k:ND + k + 1]).then_inc(slot_free[u.slot] if k else hT_ready, 1)

                def turn_copy(t, k):
                    u = turns["stack", t, k]
                    act.wait_ge(slot_full[u.slot], u.filled(b))
                    for e in range(2):
                        half = slice(e * G, (e + 1) * G)
                        nc.scalar.copy(keys[e][half, :, t * P:(t + 1) * P],
                                       ring[half, u.slot].rearrange("p (n q) -> p n q", q=P)).then_inc(slot_free[u.slot] if e else keys_half, 1)

                def empty(t):
                    u = turns["proj", t]
                    act.wait_ge(slot_full[u.slot], u.filled(b))
                    nc.scalar.copy(qk[t % 2], ring[:, u.slot, 0:S]).then_inc(qk_ready, 1)
                    nc.scalar.copy(va[:, t, :, 0:HD], heads(ring[:, u.slot, S:S + D])).then_inc(slot_free[u.slot], 1)

                empty(0)
                act.wait_ge(spare_ready, b + 1)
                for t in range(NT):
                    act.wait_ge(rot_ready, b * NT + t + 1)
                    for k in range(2):
                        g = groups(nat[k][t % 2])[:, :, 0:2, :] if k else groups(nat[k][t % 2])[:, :, 0:3:2, :]
                        if t >= 2:
                            v = turns["stack", t - 2, k]
                            act.wait_ge(slot_full[v.slot], v.filled(b))
                        nc.scalar.copy(g, twice(heads(qk_rot[t % 2][:, k * D:(k + 1) * D]))).then_inc(hi_ready, 1)
                    if t < NT - 1:
                        empty(t + 1)
                    if t:
                        turn_copy(t - 1, 1)
                turn_copy(NT - 1, 1)
                for p in range(NP):
                    for i, weights in enumerate(weight_views(probs[p % 2])):
                        u = turns["att", p, i]
                        act.wait_ge(slot_full[u.slot], u.filled(b))
                        if p >= 2:
                            act.wait_ge(pv_done, b * PARTS_LIN + 3 * (p // 2 - 1) + CAUSAL_PARTS[i] + 1)
                        nc.scalar.activation(weights, bank(u.slot) if i < 4 else bank(u.slot).rearrange("p (a q) -> p a q", a=2),
                                             ACT.Exp, scale=float(HD) ** -0.5).then_inc(slot_free[u.slot], 1)
                u = turns["turn", 1]
                act.wait_ge(slot_full[u.slot], u.filled(b))
                nc.scalar.copy(oT[1], bank(u.slot)).then_inc(slot_free[u.slot], 1)
                u = turns["xT"]
                act.wait_ge(slot_full[u.slot], u.filled(b))
                for k in range(ND):
                    nc.scalar.activation(hfull[:, k], ring[:, u.slot, k * S:(k + 1) * S], ACT.Identity, bias=mod[:, 3 * ND + k:3 * ND + k + 1],
                                         scale=mod[:, 4 * ND + k:4 * ND + k + 1]).then_inc(slot_free[u.slot] if k else h2_full, 1)
                for i in range(NHID):
                    u = turns["gate_up", i]
                    act.wait_ge(slot_full[u.slot], u.filled(b))
                    if i >= 2:
                        v = turns["gate_up", i - 2]
                        act.wait_ge(slot_free[v.slot], v.freed(b))
                    nc.scalar.activation(silu[i % 2], ring[:, u.slot, 0:S], ACT.Silu, scale=s12[:, 0, i:i + 1]).then_inc(silu_ready, 1)
                for j, (name, before, own) in enumerate((("h1", a_ready, g1_ready), ("h2", g1_ready, g2_ready))):
                    for i in range(NHID):
                        u = turns[name, i]
                        act.wait_ge(slot_full[u.slot], u.filled(b))
                        if i < 4:
                            act.wait_ge(before, b * NHID + NHID - 3 + i)
                        else:
                            act.wait_ge(own, b * NHID + i - 3)
                        nc.scalar.activation(full[i % 4], ring[:, u.slot, 0:S], ACT.Gelu, scale=s12[:, 2 + j, i:i + 1]).then_inc(slot_free[u.slot], 1)
                act.wait_ge(x_done, b * 2 + 3)
                act.dma_start(out_v[b], xn[:]).then_inc(x_sent, 16)
            act.wait_ge(x_sent, B * 16 + 1)

        @block.tensor
        def _(pe):
            pe.wait_ge(s_silu, 1)
            pe.wait_ge(s_w, 16 * 5)
            for j in range(NMOD * ND):
                for k in range(ND):
                    ins = nc.tensor.matmul(ring[:, 0, j * B:(j + 1) * B], wm[:, k, j * P:(j + 1) * P], cS[:, k], start=(k == 0), stop=(k == ND - 1))
            ins.then_inc(s_modp, 1)
            pe.wait_ge(s_const, 1)
            pe.wait_ge(w_checked, 1)
            for i, (name, m, r) in enumerate(CHUNKS):
                pe.wait_ge(raw_loaded[i % 3], 16 * (i // 3 + 1))
                if i >= SLOTS:
                    pe.wait_ge(w_staged, i - SLOTS + 1)
                nk = 8 // r
                for k in range(nk):
                    for q in range(r):
                        ins = nc.tensor.transpose(ring[:, i % SLOTS, (k * r + q) * P:(k * r + q + 1) * P],
                                                  raw[i % 3][:, q * nk * P + k * P:q * nk * P + (k + 1) * P], ident[:])
                ins.then_inc(w_turned, 1)
            pe.wait_ge(s_low, 1)
            pe.wait_ge(w_staged, len(CHUNKS))
            nc.tensor.transpose(ring[0:1, 0, 0:P], low[:, 0:1], ident[:]).then_inc(s_lowT, 1)
            pe.wait_ge(s_flag, 1)
            inexact = pe.value_load(flag[0:1, 0:1], min_val=0, max_val=1)
            pe.wait_ge(s_ready, 1)
            for free in slot_free:
                pe.sem_inc(free, 1)

            with pe.Fori(0, B) as b:
                def keep_clock(n):
                    for _ in range(n):
                        nc.tensor.matmul(acc[:, 0], identr[:], identr[:, None, :].broadcast_to([P, 4, P]), start=True, stop=True,
                                         skip_group_check=True)

                def take(key):
                    u = turns[key]
                    for last, in_this_step in u.before:
                        pe.wait_ge(slot_free[last.slot], last.freed(b) if in_this_step else last.freed_in_step_before(b))
                    return u.slot

                s = take("gates")
                pe.wait_ge(mod_ready, b + 1)
                for i, v in enumerate((2, 6, 5)):
                    for k in range(ND):
                        ins = nc.tensor.transpose(ring[:, s, i * D + k * P:i * D + (k + 1) * P],
                                                  mod[:, v * ND + k:v * ND + k + 1].broadcast_to([P, P]), ident[:])
                ins.then_inc(slot_full[s], 1)

                def turn_xn(key, n):
                    s = take(key)
                    for t in range(NT):
                        pe.wait_ge(xn_ready, b * 2 * NT + (n - 1) * NT + t + 1)
                        for k in range(ND):
                            ins = nc.tensor.transpose(ring[:, s, k * S + t * P:k * S + (t + 1) * P], xn[:, t, k * P:(k + 1) * P], ident[:])
                    ins.then_inc(slot_full[s], 1)

                keep_clock(10)
                turn_xn("hT", 1)
                keep_clock(6)

                def stacks(t):
                    for k in range(2):
                        s = take(("stack", t, k))
                        pe.wait_ge(lo_ready, b * 2 * NT + 2 * t + k + 1)
                        for p in range(NP):
                            ins = nc.tensor.transpose(ring[:, s, p * P:(p + 1) * P],
                                                      nat[k][t % 2][:, 2 * p:2 * p + 2, :].rearrange("p h g -> p (h g)").bitcast(F32), ident[:])
                        ins.then_inc(slot_full[s], 1)

                pe.wait_ge(slot_free[turns["hT"].slot], turns["hT"].freed(b))
                for t in range(NT):
                    s = take(("proj", t))
                    for o, w in ((0, 2 * D), (2 * D, D)):
                        for k in range(ND):
                            ins = nc.tensor.matmul(ring[:, s, o:o + w], hT[:, k, t * P:(t + 1) * P], wqkv[:, k, o:o + w], start=(k == 0), stop=(k == ND - 1))
                    ins.then_inc(slot_full[s], 1)
                    if t:
                        stacks(t - 1)
                stacks(NT - 1)
                pe.wait_ge(keys_zeroed, b + 1)
                for k in range(2):
                    u = turns["stack", NT - 1, k]
                    pe.wait_ge(slot_free[u.slot], u.freed(b))

                def queries(hd, lo, n):
                    return stack[:, hd // 2, lo:lo + n]

                def keys_of(hd, lo, n):
                    return keys[hd % 2][:, hd // 2, lo:lo + n]

                def max_step(key):
                    s = take(key)
                    if key[0] == "max":
                        t, g, first = key[1:]
                        n_h, w = MAX_HEADS[t], (t + 1) * P
                        diagonals = bank(s)[:, 0:n_h * w].rearrange("p (n q) -> p n q", q=w)[:, :, t * P:w]
                        nc.tensor.matmul(diagonals, identr[:], causalr[:, None, :].broadcast_to([P, n_h, P]),
                                         start=True, stop=False, skip_group_check=True)
                        for j in range(n_h):
                            ins = nc.tensor.matmul(bank(s)[:, j * w:(j + 1) * w], queries(first + j, t * P, P), keys_of(first + j, 0, w),
                                                   start=False, stop=(j == n_h - 1), skip_group_check=True)
                    else:
                        g = key[1]
                        u = turns["max", NT - 1, g, 4 * g + 3]
                        pe.wait_ge(slot_free[u.slot], u.freed(b))
                        for t in range(NT):
                            ins = nc.tensor.transpose(bank(s)[0:4, t * P:(t + 1) * P], negmax[:, t, 4 * g:4 * g + 4], ident[:])
                    ins.then_inc(slot_full[s], 1)

                def scores(p, u):
                    s = take(("att", p, u))
                    if p % 2 == 0 and u == 0:
                        g = p // 2
                        pe.wait_ge(maxrow_ready[g % 2], b * 16 * GROUPS + 32 * (g // 2) + 33)
                    for e, kb, o, _ in CAUSAL[u]:
                        ins = nc.tensor.matmul(bank(s)[:, o:o + S - kb * P], keys_of(2 * p + e, kb * P, P),
                                               queries(2 * p + e, kb * P, S - kb * P), start=True, stop=True)
                    ins.then_inc(slot_full[s], 1)

                def values(a):
                    pe.wait_ge(att_ready, b * 3 * NP + 6 * (a + 1))
                    if a >= 2:
                        pe.wait_ge(sums_ready, b * (NP // 2) + a - 1)
                    at = {(e, kb): o for unit in CAUSAL for e, kb, _, o in unit}
                    for kb in (0, 1, 3, 2):
                        for j in range(4):
                            p, e = 2 * a + j // 2, j % 2
                            ins = nc.tensor.matmul(acc[VW * j:VW * j + HD + 1, a % 2, kb * P:S], va[:, kb, 2 * p + e, :],
                                                   probs[p % 2][:, at[e, kb]:at[e, kb] + S - kb * P], start=(kb == 0),
                                                   stop=(kb == 2), skip_group_check=True)
                        if kb != 1:
                            ins.then_inc(pv_done, 1)

                def heads_back(a):
                    s = take(("heads", a))
                    pe.wait_ge(sums_ready, b * (NP // 2) + a + 1)
                    for t in range(NT):
                        ins = nc.tensor.transpose(bank(s)[:, t * P:(t + 1) * P], sums[a % 2][:, t * P:(t + 1) * P], ident[:])
                    ins.then_inc(slot_full[s], 1)

                def turn_results(part):
                    s = take(("turn", part))
                    u = turns["heads", NP // 4 * (part + 1) - 1]
                    pe.wait_ge(slot_free[u.slot], u.freed(b))
                    for t in range(NT):
                        ins = nc.tensor.transpose(bank(s)[:, t * P:(t + 1) * P], onat[:, t, part * P:(part + 1) * P], ident[:])
                    ins.then_inc(slot_full[s], 1)

                def project(part, half):
                    s = take(("out", part, half))
                    if half == 0:
                        u = turns["turn", part]
                        pe.wait_ge(slot_free[u.slot], u.freed(b))
                    for t in range(2):
                        ins = nc.tensor.matmul(bank(s)[:, t * D:(t + 1) * D], oT[part][:, (2 * half + t) * P:(2 * half + t + 1) * P], wproj[:, part],
                                               start=True, stop=True)
                    ins.then_inc(slot_full[s], 1)

                for step in attention_layer1():
                    if step[0] == "att":
                        scores(*step[1:])
                    elif step[0] == "values":
                        values(step[1])
                    elif step[0] == "heads":
                        heads_back(step[1])
                    elif step[0] == "turn":
                        turn_results(0)
                    elif step[0] == "out":
                        project(0, step[2])
                    else:
                        max_step(step)

                turn_results(1)
                for i in range(2):
                    project(1, i)
                keep_clock(10)
                turn_xn("xT", 2)
                keep_clock(6)

                def ffn(exact):
                    view = (lambda z: z) if exact else (lambda z: z.bitcast(F32))

                    def layer(dst, w, m, src, nk, ready):
                        for k in range(nk):
                            if ready is not None:
                                pe.wait_ge(ready, b * nk + k + 1)
                            for i in range(2):
                                ins = nc.tensor.matmul(dst, view(w[:, k, m * P:(m + 1) * P]), view(src[:, k, i]),
                                                       start=(k == 0 and i == 0), stop=(k == nk - 1 and i == 1))
                        return ins

                    for m in range(NHID):
                        s = take(("gate_up", m))
                        layer(ring[:, s, 0:S], w1T, m, h2r, ND, h2_ready if m == 0 else None)
                        layer(ring[:, s, S:2 * S], w2T, m, h2r, ND, None).then_inc(slot_full[s], 1)
                    for name, w, src, ready in (("h1", h1T, act_a, a_ready), ("h2", h2T, act_b, g1_ready)):
                        for m in range(NHID):
                            s = take((name, m))
                            layer(ring[:, s, 0:S], w, m, src, NHID, ready if m == 0 else None).then_inc(slot_full[s], 1)
                    pe.wait_ge(g2_ready, b * NHID + NHID)
                    for half in range(2):
                        s = take(("last", half))
                        for t in range(2):
                            rows_t = slice((2 * half + t) * P, (2 * half + t + 1) * P)
                            for k in range(NHID):
                                for i in range(2):
                                    ins = nc.tensor.matmul(bank(s)[:, t * D:(t + 1) * D], view(act_a[:, k, i, rows_t]), view(w3T[:, k]),
                                                           start=(k == 0 and i == 0), stop=(k == NHID - 1 and i == 1))
                        ins.then_inc(slot_full[s], 1)

                with pe.If(inexact == 0):
                    ffn(True)
                with pe.Else():
                    ffn(False)


_LAYER0 = ["L0_attn_x", "L0_attn_norm_w", "L0_attn_Wq", "L0_attn_Wk", "L0_attn_Wv", "L0_attn_Wqf", "L0_attn_Wkf", "L0_attn_Wout",
           "L0_ffn_W_r", "L0_ffn_W_k", "L0_ffn_W_v", "L0_ffn_mu_r", "L0_ffn_mu_k", "L0_c", "L0_wmod"]
_LAYER1 = ["L1_attn_w_qkv", "L1_attn_w_proj", "L1_attn_b_proj", "L1_ffn_w1_w", "L1_ffn_w1_s", "L1_ffn_w2_w", "L1_ffn_w2_s",
           "L1_ffn_h1_w", "L1_ffn_h1_s", "L1_ffn_h2_w", "L1_ffn_h2_s", "L1_ffn_w3_w", "L1_ffn_w3_s", "L1_c", "L1_wmod"]


def rope_table():
    f = np.float32
    inv = f(1.0) / f(10000.0) ** (np.arange(0, HD, 2, dtype=f) / f(HD))
    t = np.arange(S, dtype=f)[:, None] * inv[None, :]
    cos, sin = np.cos(t).astype(f), np.sin(t).astype(f)
    return np.stack([np.concatenate([cos, cos], 1), np.concatenate([-sin, sin], 1)])


def kernel(**inputs):
    import concourse.bacc as _bacc
    from concourse.bass_utils import run_bass_kernel_spmd as _run

    nc = _bacc.Bacc("TRN2", target_bir_lowering=False, num_devices=1)
    arrays = {f"in_{n}": np.ascontiguousarray(inputs[n]) for n in _LAYER0 + _LAYER1}
    arrays["in_rope"] = rope_table()
    ap = {n: nc.dram_tensor(n, a.shape, mybir.dt.from_np(a.dtype), kind="ExternalInput").ap() for n, a in arrays.items()}
    out = nc.dram_tensor("out", (B, S, D), F32, kind="ExternalOutput").ap()
    x_mid = nc.dram_tensor("x_mid", (B, S, D), F32, kind="Internal").ap()
    layer0(nc, *(ap[f"in_{n}"] for n in _LAYER0), x_mid)
    layer1(nc, x_mid, *(ap[f"in_{n}"] for n in _LAYER1), ap["in_rope"], out)
    return _run(nc, [arrays], core_ids=[0]).results[0]["out"]
```
